# Optimizing a Trainium2 kernel written in Bass

```python
import numpy as np
import jax
import jax.numpy as jnp

def _softmax(x, axis=-1):
    return jax.nn.softmax(x, axis=axis)

def _gelu(x):
    return jax.nn.gelu(x, approximate=True)

def _silu(x):
    return jax.nn.silu(x)

def _sigmoid(x):
    return jax.nn.sigmoid(x)

def _layernorm(x, axis=-1, eps=1e-05):
    m = jnp.mean(x, axis=axis, keepdims=True)
    v = jnp.var(x, axis=axis, keepdims=True)
    return (x - m) / jnp.sqrt(v + eps)

def _scatter_add(tgt, idx, src, axis=0):
    return tgt.at[idx].add(src)

def _segment_sum(src, seg, n):
    return jax.ops.segment_sum(src, seg, n)
kernel_name = 'mk_adaln_d2_jaxref_r8_d1f6f8'

def setup_inputs(seed: int=0):
    np.random.seed(seed)
    _w = jnp.asarray

    def _L0_attn_setup():
        import jax, jax.numpy as jnp
        from jax import lax
        import numpy as np
        D_MODEL = 128
        D_STATE = 16
        D_CONV = 4
        D_INNER = 256
        DT_RANK = D_INNER // 16
        BATCH = 2
        SEQ = 256
        key = jax.random.key(seed)
        ks = jax.random.split(key, 7)
        s = 0.02
        return {'x': jax.random.normal(ks[0], (BATCH, SEQ, D_MODEL), jnp.float32), 'in_proj_w': jax.random.normal(ks[1], (D_MODEL, 2 * D_INNER), jnp.float32) * s, 'conv_w': jax.random.normal(ks[2], (D_CONV, 1, D_INNER), jnp.float32) * 0.1, 'conv_b': jnp.zeros((D_INNER,), jnp.float32), 'x_proj_w': jax.random.normal(ks[3], (D_INNER, DT_RANK + 2 * D_STATE), jnp.float32) * s, 'dt_proj_w': jax.random.normal(ks[4], (DT_RANK, D_INNER), jnp.float32) * s, 'dt_proj_b': jnp.zeros((D_INNER,), jnp.float32), 'A_log': jnp.log(jnp.tile(jnp.arange(1.0, D_STATE + 1.0, dtype=jnp.float32), (D_INNER, 1))), 'D': jnp.ones((D_INNER,), jnp.float32), 'out_proj_w': jax.random.normal(ks[5], (D_INNER, D_MODEL), jnp.float32) * s}
    _L0_attn_in = _L0_attn_setup()

    def _L0_ffn_setup():
        import jax, jax.numpy as jnp
        import numpy as np
        B, S, H, E, DFF = (4, 512, 128, 8, 512)
        key = jax.random.key(seed)
        k0, k1, k2, k3 = jax.random.split(key, 4)
        hidden_states = jax.random.normal(k0, (B, S, H), dtype=jnp.float32)
        gate_w = jax.random.normal(k1, (E, H), dtype=jnp.float32) * 0.02
        w1 = jax.random.normal(k2, (E, H, DFF), dtype=jnp.float32) * 0.02
        b1 = jnp.zeros((E, DFF), dtype=jnp.float32)
        w2 = jax.random.normal(k3, (E, DFF, H), dtype=jnp.float32) * 0.02
        b2 = jnp.zeros((E, H), dtype=jnp.float32)
        return {'hidden_states': hidden_states, 'gate_w': gate_w, 'w1': w1, 'b1': b1, 'w2': w2, 'b2': b2}
    _L0_ffn_in = _L0_ffn_setup()
    _L0_c = _w((lambda *s: np.random.randn(*s).astype(np.float32) * 0.05)(16, 128))
    _L0_wmod = _w((lambda *s: np.random.randn(*s).astype(np.float32) * 0.05)(128, 6 * 128) * 128 ** (-0.5))

    def _L1_attn_setup():
        import jax, jax.numpy as jnp
        import numpy as np
        B, N, D = (4, 512, 128)
        H, DH = (16, 64)
        DFF = 512
        M = 64
        EPS_KERN = 1e-06
        EPS_LN = 1e-06

        def _softmax_kernel_feats(data, proj, is_query):
            dn = 1.0 / jnp.sqrt(jnp.sqrt(jnp.float32(data.shape[-1])))
            ratio = 1.0 / jnp.sqrt(jnp.float32(proj.shape[0]))
            data_dash = jnp.einsum('bnhd,md->bnhm', data * dn, proj)
            diag = jnp.sum(jnp.square(data), axis=-1, keepdims=True) * (dn * dn) / 2.0
            if is_query:
                mx = jnp.max(data_dash, axis=-1, keepdims=True)
            else:
                mx = jnp.max(data_dash)
            return ratio * (jnp.exp(data_dash - diag - mx) + EPS_KERN)

        def _layernorm(x, g, b):
            mu = jnp.mean(x, axis=-1, keepdims=True)
            var = jnp.mean(jnp.square(x - mu), axis=-1, keepdims=True)
            return (x - mu) * jax.lax.rsqrt(var + EPS_LN) * g + b

        def _encoder_forward(x, Wq, Wk, Wv, Wo, proj, W1, b1, W2, b2, ln1_g, ln1_b, ln2_g, ln2_b):
            q = jnp.einsum('bnd,dhk->bnhk', x, Wq)
            k = jnp.einsum('bnd,dhk->bnhk', x, Wk)
            v = jnp.einsum('bnd,dhk->bnhk', x, Wv)
            qf = _softmax_kernel_feats(q, proj, True)
            kf = _softmax_kernel_feats(k, proj, False)
            kv = jnp.einsum('bnhm,bnhd->bhmd', kf, v)
            num = jnp.einsum('bnhm,bhmd->bnhd', qf, kv)
            den = jnp.einsum('bnhm,bhm->bnh', qf, jnp.sum(kf, axis=1))
            attn = num / den[..., None]
            attn_out = jnp.einsum('bnhd,hdo->bno', attn, Wo)
            out1 = _layernorm(x + attn_out, ln1_g, ln1_b)
            h = jax.nn.elu(out1 @ W1 + b1)
            ffn_out = h @ W2 + b2
            return _layernorm(out1 + ffn_out, ln2_g, ln2_b)
        key = jax.random.key(seed)
        ks = jax.random.split(key, 12)
        s = 0.02
        inp = {'x': jax.random.normal(ks[0], (B, N, D), jnp.float32), 'Wq': jax.random.normal(ks[1], (D, H, DH), jnp.float32) * s, 'Wk': jax.random.normal(ks[2], (D, H, DH), jnp.float32) * s, 'Wv': jax.random.normal(ks[3], (D, H, DH), jnp.float32) * s, 'Wo': jax.random.normal(ks[4], (H, DH, D), jnp.float32) * s, 'proj': jax.random.normal(ks[5], (M, DH), jnp.float32), 'W1': jax.random.normal(ks[6], (D, DFF), jnp.float32) * s, 'b1': jnp.zeros((DFF,), jnp.float32), 'W2': jax.random.normal(ks[7], (DFF, D), jnp.float32) * s, 'b2': jnp.zeros((D,), jnp.float32), 'ln1_g': jnp.ones((D,), jnp.float32), 'ln1_b': jnp.zeros((D,), jnp.float32), 'ln2_g': jnp.ones((D,), jnp.float32), 'ln2_b': jnp.zeros((D,), jnp.float32)}
        return inp
    _L1_attn_in = _L1_attn_setup()

    def _L1_ffn_setup():
        import jax, jax.numpy as jnp
        import numpy as np
        TOP_K = 2
        key = jax.random.key(seed)
        ks = jax.random.split(key, 7)
        B, L, D, H, E, S = (2, 256, 128, 64, 16, 256)
        s = lambda fan_in: (1.0 / np.sqrt(fan_in)).astype(np.float32)
        return {'x': jax.random.normal(ks[0], (B, L, D), jnp.float32), 'gate_w': jax.random.normal(ks[1], (E, D), jnp.float32) * s(D), 'w1': jax.random.normal(ks[2], (E, H, D), jnp.float32) * s(D), 'w2': jax.random.normal(ks[3], (E, D, H), jnp.float32) * s(H), 'sfc1': jax.random.normal(ks[4], (S, D), jnp.float32) * s(D), 'sfc2': jax.random.normal(ks[5], (S, D), jnp.float32) * s(D), 'sfc3': jax.random.normal(ks[6], (D, S), jnp.float32) * s(S)}
    _L1_ffn_in = _L1_ffn_setup()
    _L1_c = _w((lambda *s: np.random.randn(*s).astype(np.float32) * 0.05)(16, 128))
    _L1_wmod = _w((lambda *s: np.random.randn(*s).astype(np.float32) * 0.05)(128, 6 * 128) * 128 ** (-0.5))
    _d = {'L0_attn_x': _L0_attn_in['x'], 'L0_attn_in_proj_w': _L0_attn_in['in_proj_w'], 'L0_attn_conv_w': _L0_attn_in['conv_w'], 'L0_attn_conv_b': _L0_attn_in['conv_b'], 'L0_attn_x_proj_w': _L0_attn_in['x_proj_w'], 'L0_attn_dt_proj_w': _L0_attn_in['dt_proj_w'], 'L0_attn_dt_proj_b': _L0_attn_in['dt_proj_b'], 'L0_attn_A_log': _L0_attn_in['A_log'], 'L0_attn_D': _L0_attn_in['D'], 'L0_attn_out_proj_w': _L0_attn_in['out_proj_w'], 'L0_ffn_gate_w': _L0_ffn_in['gate_w'], 'L0_ffn_w1': _L0_ffn_in['w1'], 'L0_ffn_b1': _L0_ffn_in['b1'], 'L0_ffn_w2': _L0_ffn_in['w2'], 'L0_ffn_b2': _L0_ffn_in['b2'], 'L0_c': _L0_c, 'L0_wmod': _L0_wmod, 'L1_attn_Wq': _L1_attn_in['Wq'], 'L1_attn_Wk': _L1_attn_in['Wk'], 'L1_attn_Wv': _L1_attn_in['Wv'], 'L1_attn_Wo': _L1_attn_in['Wo'], 'L1_attn_proj': _L1_attn_in['proj'], 'L1_attn_W1': _L1_attn_in['W1'], 'L1_attn_b1': _L1_attn_in['b1'], 'L1_attn_W2': _L1_attn_in['W2'], 'L1_attn_b2': _L1_attn_in['b2'], 'L1_attn_ln1_g': _L1_attn_in['ln1_g'], 'L1_attn_ln1_b': _L1_attn_in['ln1_b'], 'L1_attn_ln2_g': _L1_attn_in['ln2_g'], 'L1_attn_ln2_b': _L1_attn_in['ln2_b'], 'L1_ffn_gate_w': _L1_ffn_in['gate_w'], 'L1_ffn_w1': _L1_ffn_in['w1'], 'L1_ffn_w2': _L1_ffn_in['w2'], 'L1_ffn_sfc1': _L1_ffn_in['sfc1'], 'L1_ffn_sfc2': _L1_ffn_in['sfc2'], 'L1_ffn_sfc3': _L1_ffn_in['sfc3'], 'L1_c': _L1_c, 'L1_wmod': _L1_wmod}
    _x0 = _d['L0_attn_x']
    _d['L0_attn_x'] = jax.random.normal(jax.random.fold_in(jax.random.key(seed), 1), (16, 512, 128), dtype=_x0.dtype)
    del _x0
    return _d

def reference(L0_attn_x, L0_attn_in_proj_w, L0_attn_conv_w, L0_attn_conv_b, L0_attn_x_proj_w, L0_attn_dt_proj_w, L0_attn_dt_proj_b, L0_attn_A_log, L0_attn_D, L0_attn_out_proj_w, L0_ffn_gate_w, L0_ffn_w1, L0_ffn_b1, L0_ffn_w2, L0_ffn_b2, L0_c, L0_wmod, L1_attn_Wq, L1_attn_Wk, L1_attn_Wv, L1_attn_Wo, L1_attn_proj, L1_attn_W1, L1_attn_b1, L1_attn_W2, L1_attn_b2, L1_attn_ln1_g, L1_attn_ln1_b, L1_attn_ln2_g, L1_attn_ln2_b, L1_ffn_gate_w, L1_ffn_w1, L1_ffn_w2, L1_ffn_sfc1, L1_ffn_sfc2, L1_ffn_sfc3, L1_c, L1_wmod):

    def _L0_attn_ref(x, in_proj_w, conv_w, conv_b, x_proj_w, dt_proj_w, dt_proj_b, A_log, D, out_proj_w):
        import jax, jax.numpy as jnp
        from jax import lax
        import numpy as np
        D_MODEL = 128
        D_STATE = 16
        D_CONV = 4
        D_INNER = 256
        DT_RANK = D_INNER // 16
        BATCH = 2
        SEQ = 256
        xz = x @ in_proj_w
        xb, zb = jnp.split(xz, 2, axis=-1)
        xb = lax.conv_general_dilated(xb, conv_w, window_strides=(1,), padding=[(D_CONV - 1, 0)], dimension_numbers=('NWC', 'WIO', 'NWC'), feature_group_count=D_INNER) + conv_b
        xb = jax.nn.silu(xb)
        zb = jax.nn.silu(zb)
        A = -jnp.exp(A_log)
        x_dbl = xb @ x_proj_w
        dt = x_dbl[..., :DT_RANK]
        Bm = x_dbl[..., DT_RANK:DT_RANK + D_STATE]
        Cm = x_dbl[..., DT_RANK + D_STATE:]
        dt = jax.nn.softplus(dt @ dt_proj_w + dt_proj_b)
        decay = jnp.exp(dt[..., None] * A)
        inp = dt[..., None] * Bm[:, :, None, :] * xb[..., None]

        def step(h, t):
            dc, ic, c = t
            h = dc * h + ic
            y = jnp.einsum('bdn,bn->bd', h, c)
            return (h, y)
        h0 = jnp.zeros((x.shape[0], D_INNER, D_STATE), xb.dtype)
        _, ys = lax.scan(step, h0, (decay.swapaxes(0, 1), inp.swapaxes(0, 1), Cm.swapaxes(0, 1)))
        y = ys.swapaxes(0, 1)
        y = y + xb * D
        out = y * zb @ out_proj_w
        return out

    def _L0_ffn_ref(hidden_states, gate_w, w1, b1, w2, b2):
        import jax, jax.numpy as jnp
        import numpy as np
        B, S, H, E, DFF = (4, 512, 128, 8, 512)
        b, s, h = hidden_states.shape
        x = hidden_states.reshape(-1, h)
        gate_logits = x @ gate_w.T
        gate_probs = jax.nn.softmax(gate_logits, axis=-1)
        expert_idx = jnp.argmax(gate_probs, axis=-1)
        expert_w = jnp.take_along_axis(gate_probs, expert_idx[:, None], axis=1)[:, 0]
        out = jnp.zeros_like(x)
        n_experts = w1.shape[0]
        for e in range(n_experts):
            ye = jax.nn.relu(x @ w1[e] + b1[e]) @ w2[e] + b2[e]
            sel = (expert_idx == e)[:, None]
            out = out + jnp.where(sel, ye * expert_w[:, None], 0.0)
        return out.reshape(b, s, h)

    def _L1_attn_ref(x, Wq, Wk, Wv, Wo, proj, W1, b1, W2, b2, ln1_g, ln1_b, ln2_g, ln2_b):
        import jax, jax.numpy as jnp
        import numpy as np
        B, N, D = (4, 512, 128)
        H, DH = (16, 64)
        DFF = 512
        M = 64
        EPS_KERN = 1e-06
        EPS_LN = 1e-06

        def _softmax_kernel_feats(data, proj, is_query):
            dn = 1.0 / jnp.sqrt(jnp.sqrt(jnp.float32(data.shape[-1])))
            ratio = 1.0 / jnp.sqrt(jnp.float32(proj.shape[0]))
            data_dash = jnp.einsum('bnhd,md->bnhm', data * dn, proj)
            diag = jnp.sum(jnp.square(data), axis=-1, keepdims=True) * (dn * dn) / 2.0
            if is_query:
                mx = jnp.max(data_dash, axis=-1, keepdims=True)
            else:
                mx = jnp.max(data_dash)
            return ratio * (jnp.exp(data_dash - diag - mx) + EPS_KERN)

        def _layernorm(x, g, b):
            mu = jnp.mean(x, axis=-1, keepdims=True)
            var = jnp.mean(jnp.square(x - mu), axis=-1, keepdims=True)
            return (x - mu) * jax.lax.rsqrt(var + EPS_LN) * g + b

        def _encoder_forward(x, Wq, Wk, Wv, Wo, proj, W1, b1, W2, b2, ln1_g, ln1_b, ln2_g, ln2_b):
            q = jnp.einsum('bnd,dhk->bnhk', x, Wq)
            k = jnp.einsum('bnd,dhk->bnhk', x, Wk)
            v = jnp.einsum('bnd,dhk->bnhk', x, Wv)
            qf = _softmax_kernel_feats(q, proj, True)
            kf = _softmax_kernel_feats(k, proj, False)
            kv = jnp.einsum('bnhm,bnhd->bhmd', kf, v)
            num = jnp.einsum('bnhm,bhmd->bnhd', qf, kv)
            den = jnp.einsum('bnhm,bhm->bnh', qf, jnp.sum(kf, axis=1))
            attn = num / den[..., None]
            attn_out = jnp.einsum('bnhd,hdo->bno', attn, Wo)
            out1 = _layernorm(x + attn_out, ln1_g, ln1_b)
            h = jax.nn.elu(out1 @ W1 + b1)
            ffn_out = h @ W2 + b2
            return _layernorm(out1 + ffn_out, ln2_g, ln2_b)
        return _encoder_forward(x, Wq, Wk, Wv, Wo, proj, W1, b1, W2, b2, ln1_g, ln1_b, ln2_g, ln2_b)

    def _L1_ffn_ref(x, gate_w, w1, w2, sfc1, sfc2, sfc3):
        import jax, jax.numpy as jnp
        import numpy as np
        TOP_K = 2
        B, L, D = x.shape
        E = gate_w.shape[0]
        shared = jnp.einsum('bls,ds->bld', jax.nn.silu(jnp.einsum('bld,sd->bls', x, sfc1)) * jnp.einsum('bld,sd->bls', x, sfc2), sfc3)
        logits = jnp.einsum('bld,ed->ble', x, gate_w)
        top_w, top_idx = jax.lax.top_k(logits, TOP_K)
        top_w = jax.nn.softmax(top_w, axis=-1)
        xf = x.reshape(-1, D)
        T = xf.shape[0]
        idx = top_idx.reshape(T, TOP_K)
        wk = top_w.reshape(T, TOP_K)
        dispatch = jnp.zeros((T, E), xf.dtype).at[jnp.arange(T)[:, None], idx].add(wk)
        h = jax.nn.silu(jnp.einsum('td,ehd->teh', xf, w1))
        moe = jnp.einsum('teh,te,edh->td', h, dispatch, w2)
        return moe.reshape(B, L, D) + shared
    x = L0_attn_x
    mod = (_silu(L0_c) @ L0_wmod).reshape(L0_c.shape[0], 6, 1, -1)
    sa, ca, ga, sb, cb, gb = (mod[:, 0], mod[:, 1], mod[:, 2], mod[:, 3], mod[:, 4], mod[:, 5])
    ga = (2 * (ga >= 0) - 1) * jnp.maximum(jnp.abs(ga), 0.25)
    gb = (2 * (gb >= 0) - 1) * jnp.maximum(jnp.abs(gb), 0.25)
    h = _layernorm(x, axis=-1) * (1 + ca) + sa
    x = x + ga * _L0_attn_ref(h, L0_attn_in_proj_w, L0_attn_conv_w, L0_attn_conv_b, L0_attn_x_proj_w, L0_attn_dt_proj_w, L0_attn_dt_proj_b, L0_attn_A_log, L0_attn_D, L0_attn_out_proj_w)
    h = _layernorm(x, axis=-1) * (1 + cb) + sb
    x = x + gb * _L0_ffn_ref(h, L0_ffn_gate_w, L0_ffn_w1, L0_ffn_b1, L0_ffn_w2, L0_ffn_b2)
    mod = (_silu(L1_c) @ L1_wmod).reshape(L1_c.shape[0], 6, 1, -1)
    sa, ca, ga, sb, cb, gb = (mod[:, 0], mod[:, 1], mod[:, 2], mod[:, 3], mod[:, 4], mod[:, 5])
    ga = (2 * (ga >= 0) - 1) * jnp.maximum(jnp.abs(ga), 0.25)
    gb = (2 * (gb >= 0) - 1) * jnp.maximum(jnp.abs(gb), 0.25)
    h = _layernorm(x, axis=-1) * (1 + ca) + sa
    x = x + ga * _L1_attn_ref(h, L1_attn_Wq, L1_attn_Wk, L1_attn_Wv, L1_attn_Wo, L1_attn_proj, L1_attn_W1, L1_attn_b1, L1_attn_W2, L1_attn_b2, L1_attn_ln1_g, L1_attn_ln1_b, L1_attn_ln2_g, L1_attn_ln2_b)
    h = _layernorm(x, axis=-1) * (1 + cb) + sb
    x = x + gb * _L1_ffn_ref(h, L1_ffn_gate_w, L1_ffn_w1, L1_ffn_w2, L1_ffn_sfc1, L1_ffn_sfc2, L1_ffn_sfc3)
    return x

_drawn_inputs = setup_inputs


def setup_inputs(seed=0):
    import zlib

    import numpy as np

    out = dict(_drawn_inputs(seed))
    spreads = {'L0_attn_conv_b': (0.0, 0.8),
     'L0_attn_dt_proj_b': (0.0, 0.8),
     'L0_attn_D': (1.0, 0.6),
     'L0_ffn_b1': (0.0, 2.0),
     'L0_ffn_b2': (0.0, 2.0),
     'L1_attn_b1': (0.0, 2.0),
     'L1_attn_b2': (0.0, 2.0),
     'L1_attn_ln1_g': (1.0, 0.6),
     'L1_attn_ln1_b': (0.0, 2.0),
     'L1_attn_ln2_g': (1.0, 0.6),
     'L1_attn_ln2_b': (0.0, 2.0)}
    factors = {'L0_attn_in_proj_w': 8.0,
     'L0_attn_conv_w': 8.0,
     'L0_attn_x_proj_w': 8.0,
     'L0_attn_dt_proj_w': 8.0,
     'L0_attn_A_log': 8.0,
     'L0_attn_out_proj_w': 8.0,
     'L0_ffn_gate_w': 56.12,
     'L0_ffn_w1': 64.0,
     'L0_ffn_w2': 64.0,
     'L0_c': 6.858,
     'L0_wmod': 6.797,
     'L1_attn_Wq': 64.0,
     'L1_attn_Wk': 64.0,
     'L1_attn_Wv': 200.0,
     'L1_attn_Wo': 200.0,
     'L1_attn_proj': 64.0,
     'L1_attn_W1': 64.0,
     'L1_attn_W2': 64.0,
     'L1_ffn_gate_w': 25.064,
     'L1_ffn_w1': 29.055,
     'L1_ffn_w2': 24.471,
     'L1_ffn_sfc1': 8.0,
     'L1_ffn_sfc2': 8.0,
     'L1_ffn_sfc3': 8.0,
     'L1_c': 8.0,
     'L1_wmod': 8.0}
    for name, (base, spread) in spreads.items():
        noise = np.random.default_rng([zlib.crc32(name.encode()), seed]).standard_normal(out[name].shape)
        drawn = base * np.exp(spread * noise) if base else spread * noise
        out[name] = jnp.asarray(drawn.astype(out[name].dtype))
    for name, factor in factors.items():
        out[name] = (out[name] * factor).astype(out[name].dtype)
    return out
```

```python
from contextlib import ExitStack

import concourse.bass as bass
from concourse import mybir

F32 = mybir.dt.float32
BF16 = mybir.dt.bfloat16
U32 = mybir.dt.uint32
ALU = mybir.AluOpType
ACT = mybir.ActivationFunctionType
AX = mybir.AxisListType
RMAX = bass.bass_isa.ReduceOp.max

P = 128
NB, T, D = 16, 512, 128
J = T // P
DI = 256
G = DI // P
NS = 16
RK = DI // 16
TAPS = 4
PAD = TAPS - 1
E0, FF = 8, 512
FC = FF // P
H, DH = 16, 64
HD = H * DH
PR = HD // P
VW = P + 1
E1, HE = 16, 64
MC = E1 * HE // P
SC = 256 // P
EPS_MOD = 1e-5
EPS_ENC = 1e-6
EPS_FEAT = 1e-6
DN = float(DH) ** -0.25
DIAG = DN * DN / 2.0
BIG = 3.0e38


def columns(parts):
    at, where = 0, {}
    for name, n in parts:
        where[name] = (at, n)
        at += n
    return where, at


KEEP, KEEP_N = columns([("ident", P), ("iota", E1), ("wv", HD)])
ONCE, ONCE_N = columns([("wmod0", 6 * D), ("wmod1", 6 * D), ("c0", NB), ("c1", NB),
                        ("wkT", HD), ("wqT", HD), ("proj", P)])
ONE, ONE_N = columns([("inw", 2 * DI), ("convw", G * TAPS), ("convb", G), ("xw", G * P), ("dtw", DI),
                      ("dtb", G), ("alog", G * NS), ("dskip", G), ("outw", G * D), ("gate", E0),
                      ("w1", E0 * FF), ("b1", E0 * FC), ("w2", E0 * FF), ("b2", J * D), ("wk", HD)])
TWO, TWO_N = columns([("wq", HD), ("wo", HD), ("w1", FF), ("b1", FC), ("w2", FF), ("b2", T),
                      ("g1", 1), ("be1", 1), ("g2", D), ("be2", D), ("gate", E1), ("mw1", E1 * HE),
                      ("mw2", E1 * HE), ("s1", SC * P), ("s2", SC * P), ("s3", SC * D), ("pick", MC * P)])


class Signal:

    def __init__(self, sem, per):
        self.sem, self.per = sem, per

    def __call__(self, batch, n):
        return self.sem, batch * self.per + n


class Chain:

    def __init__(self, eng, signal):
        self.eng, self.step_of, self.n, self.batch = eng, signal, 0, None

    def begin(self, batch):
        assert self.n in (0, self.step_of.per), (self.n, self.step_of.per)
        self.n, self.batch = 0, batch

    def step(self, ins):
        self.n += 1
        ins.then_inc(self.step_of.sem, 1)
        self.eng.wait_ge(*self.step_of(self.batch, self.n))


class Norm:

    def __init__(self, sb, sig, name, eps):
        self.eps = eps
        self.st = sb(name + "_st", [P, J, 6])
        self.mv = sb(name + "_mv", [P, J, 2])
        self.ve = sb(name + "_ve", [P, J])
        self.rs = sb(name + "_rs", [P, J])
        self.xh = sb(name + "_xh", [P, J, D])
        self.sums, self.stats, self.veps, self.rstd, self.xhat, self.turned, self.out = (
            sig(name + "_" + n, 1) for n in ("sums", "stats", "veps", "rstd", "xhat", "turned", "out"))


def hold(eng, passed):
    eng.sem_inc(passed, 1)


def norm_dve(dve, ln, src, it, passed):
    dve.wait_ge(*ln.xhat(it, 0))
    for j in range(J):
        last = dve.bn_stats(ln.st[:, j, :], src[:, j, :])
    last.then_inc(ln.sums.sem, 1)
    dve.wait_ge(*ln.sums(it, 1))
    hold(dve, passed)
    for j in range(J):
        last = dve.bn_aggr(ln.mv[:, j, :], ln.st[:, j, :])
    last.then_inc(ln.stats.sem, 1)
    dve.wait_ge(*ln.rstd(it, 1))
    for j in range(J):
        last = dve.tensor_scalar(ln.xh[:, j, :], src[:, j, :], ln.mv[:, j, 0:1], ln.rs[:, j:j + 1],
                                 ALU.subtract, ALU.mult)
    last.then_inc(ln.xhat.sem, 1)


def norm_pool(pool, ln, half, it, passed):
    pool.wait_ge(*ln.stats(it, 1))
    hold(pool, passed)
    pool.tensor_scalar(ln.ve[:, :], ln.mv[:, :, 1], ln.eps, None, ALU.add).then_inc(ln.veps.sem, 1)
    pool.wait_ge(*ln.veps(it, 1))
    pool.tensor_tensor(ln.rs[:, :], ln.ve[:, :], half[:, 0:J], ALU.pow).then_inc(ln.rstd.sem, 1)


def norm_pe(pe, ln, ps, ident, it):
    pe.wait_ge(*ln.xhat(it, 1))
    for j in range(J):
        last = pe.transpose(ps[:, j * P:(j + 1) * P], ln.xh[:, j, :], ident)
    last.then_inc(ln.turned.sem, 1)


def mid(ap, n):
    return ap.unsqueeze(1).to_broadcast([ap.shape[0], n, ap.shape[1]])


def inner(ap, m):
    return ap.unsqueeze(2).to_broadcast([ap.shape[0], ap.shape[1], m])


def adaln_depth2(nc, x, keep, once, one, two, pick16, out):
    ctx = ExitStack()
    with ctx:
        held = []

        def sem(name):
            held.append(nc.alloc_semaphore(name=name))
            return held[-1]

        def end_part():
            nc.clear_and_free_semaphores(held)
            held.clear()
            nc.all_engine_barrier()

        def sig(name, per):
            return Signal(sem(name), per)

        def sbuf(stack):
            def sb(name, shape, dt=F32):
                return stack.enter_context(nc.sbuf_tensor(name, shape, dt))
            return sb

        x_v = x.rearrange("b (j p) d -> b p j d", p=P)
        out_v = out.rearrange("b (j p) d -> b p j d", p=P)
        gate_rows = nc.dram_tensor("gate_rows", (4, NB, D), F32, kind="Internal").ap()
        x2_dram = nc.dram_tensor("x2_dram", (NB, P, J * D), F32, kind="Internal").ap()
        h3_dram = nc.dram_tensor("h3_dram", (NB, P, T), F32, kind="Internal").ap()
        kv_dram = nc.dram_tensor("kv_dram", (NB, P, PR * VW + 1), F32, kind="Internal").ap()

        kept = sbuf(ctx)
        keep_sb = kept("keep_sb", [P, KEEP_N])
        ident, iota, wv = (keep_sb[:, KEEP[n][0]:KEEP[n][0] + KEEP[n][1]] for n in ("ident", "iota", "wv"))
        modc = kept("modc", [P, 2, NB, 4])
        pk = kept("pk", [P, HD])
        pq = kept("pq", [P, HD])
        ones = kept("ones", [P, P])
        half = kept("half", [P, 8])
        mxrun = kept("mxrun", [P, 1])
        nmx = kept("nmx", [P, 1])
        banks = [ctx.enter_context(nc.psum_tensor(f"bank{n}", [P, T], F32)) for n in range(8)]

        with ExitStack() as part:
            sb = sbuf(part)
            once_sb = sb("once_sb", [P, ONCE_N])

            def W(name, a=0, b=None):
                at, n = ONCE[name]
                return once_sb[:, at + a:at + (n if b is None else b)]

            sc = sb("sc", [P, 2 * NB])
            gr_s = sb("gr_s", [NB, T])
            gr_m = sb("gr_m", [NB, T])
            gr = sb("gr", [NB, T])
            w_in, c_ready, fold, mods, gates, chain_s, gr_ready, gr_out, done_s, setup_dve = (
                sem(n) for n in ("setup_in", "c_ready", "folded", "mods", "gates", "gate_chain", "gate_rows_ready",
                                 "gate_rows_out", "folds_kept", "setup_dve"))
            with nc.Block() as block:
                @block.sync
                def _(sp):
                    sp.dma_start(once_sb[:, :], once).then_inc(w_in, 16)
                    sp.dma_start(keep_sb[:, :], keep).then_inc(w_in, 16)
                    sp.wait_ge(gr_ready, 1)
                    sp.dma_start(gate_rows.rearrange("r b d -> b r d"),
                                 gr[:, :].rearrange("b (r d) -> b r d", r=4)).then_inc(gr_out, 16)
                    sp.wait_ge(gr_out, 16)

                @block.gpsimd
                def _(pool):
                    pool.memset(ones[:, :], 1.0)
                    pool.memset(half[:, :], -0.5)
                    pool.memset(mxrun[:, :], -BIG)

                @block.scalar
                def _(act):
                    act.wait_ge(w_in, 32)
                    act.activation(sc[:, :], W("c0", 0, 2 * NB), ACT.Silu).then_inc(c_ready, 1)
                    for n, dst in enumerate((pk, pk, pq, pq)):
                        act.wait_ge(fold, n + 1)
                        o = (n % 2) * T
                        act.activation(dst[:, o:o + T], banks[n][:, :], ACT.Copy, scale=DN).then_inc(done_s, 1)

                @block.tensor
                def _(pe):
                    pe.wait_ge(w_in, 32)
                    for n, src in enumerate(("wkT", "wkT", "wqT", "wqT")):
                        for k in range(PR // 2):
                            pr = (n % 2) * (PR // 2) + k
                            last = pe.matmul(banks[n][:, k * P:(k + 1) * P], W(src, pr * P, (pr + 1) * P),
                                             W("proj"), start=True, stop=True)
                        last.then_inc(fold, 1)
                    pe.wait_ge(c_ready, 1)
                    for l in range(2):
                        for k, col in enumerate((0, 1, 3, 4)):
                            at = (l * 4 + k) * NB
                            last = pe.matmul(banks[6][:, at:at + NB], W(f"wmod{l}", col * D, (col + 1) * D),
                                             sc[:, l * NB:(l + 1) * NB], start=True, stop=True)
                    last.then_inc(mods, 1)
                    for l in range(2):
                        for k, col in enumerate((2, 5)):
                            at = (l * 2 + k) * D
                            last = pe.matmul(banks[7][0:NB, at:at + D], sc[:, l * NB:(l + 1) * NB],
                                             W(f"wmod{l}", col * D, (col + 1) * D), start=True, stop=True)
                    last.then_inc(gates, 1)

                @block.vector
                def _(dve):
                    dve.wait_ge(mods, 1)
                    ps = banks[6][:, 0:2 * 4 * NB].rearrange("p (l k b) -> p l b k", l=2, k=4)
                    for l in range(2):
                        for k in range(4):
                            dve.tensor_scalar(modc[:, l, :, k], ps[:, l, :, k], float(k % 2), None, ALU.add)\
                               .then_inc(setup_dve, 1)
                    dve.wait_ge(gates, 1)
                    gp = banks[7][0:NB, :]
                    dve.tensor_scalar(gr_s[:, :], gp, 0.0, 2.0, ALU.is_ge, ALU.mult).then_inc(chain_s, 1)
                    dve.tensor_scalar(gr_m[:, :], gp, -1.0, None, ALU.mult).then_inc(chain_s, 1)
                    dve.wait_ge(chain_s, 2)
                    dve.tensor_tensor(gr_m[:, :], gr_m[:, :], gp, ALU.max).then_inc(chain_s, 1)
                    dve.wait_ge(chain_s, 3)
                    dve.tensor_scalar(gr_m[:, :], gr_m[:, :], 0.25, None, ALU.max).then_inc(chain_s, 1)
                    dve.wait_ge(chain_s, 4)
                    dve.scalar_tensor_tensor(gr[:, :], gr_s[:, :], -1.0, gr_m[:, :], ALU.add, ALU.mult)\
                       .then_inc(gr_ready, 1)

            end_part()

        with ExitStack() as part:
            sb = sbuf(part)
            one_sb = sb("one_sb", [P, ONE_N])

            def V1(name):
                at, n = ONE[name]
                return one_sb[:, at:at + n]

            inw, convb, dtb, dskip, alog, gatew, b1c = (V1(n) for n in ("inw", "convb", "dtb", "dskip", "alog",
                                                                       "gate", "b1"))
            convw = V1("convw").rearrange("p (g k) -> p g k", g=G)
            xw = V1("xw").rearrange("p (g m) -> p g m", g=G)
            dtw = V1("dtw")
            outw = V1("outw").rearrange("p (g d) -> p g d", g=G)
            w1 = V1("w1").rearrange("p (e f) -> p e f", e=E0)
            w2 = V1("w2").rearrange("p (e f d) -> p e f d", e=E0, f=FC)
            b2 = V1("b2")
            wk = V1("wk")
            pick_sb = sb("pick_sb", [3 * 2 * NS, 2 * NS, P], BF16)
            aneg = sb("aneg", [P, G, NS])
            xs = sb("xs", [P, J, D])
            ga = sb("ga", [P, D])
            hT = sb("hT", [P, T])
            xpad = sb("xpad", [P, G, PAD + T])
            cv = sb("cv", [P, G, T])
            ax = cv
            zs = sb("zs", [P, G, T])
            xc = sb("xc", [P, G, T])
            S = sb("S", [P, T], BF16)
            R = sb("R", [P, T])
            dtr = R
            Rb = sb("Rb", [P, T], BF16)
            dt = sb("dt", [P, G, T])
            dtx = sb("dtx", [P, G, T])
            acc = sb("acc", [P, G, T])
            dec = sb("dec", [P, 2, G, T])
            u = sb("u", [P, G, T])
            yz = u
            h = sb("h", [P, G, T])
            zz = sb("zz", [P, 2, G, T])
            ao = sb("ao", [P, J, D])
            x1 = sb("x1", [P, J, D])
            gb = sb("gb", [P, D])
            hT2 = sb("hT2", [P, T])
            m8 = sb("m8", [P, J, 8])
            idx = sb("idx", [P, J, 8], U32)
            oh = sb("oh", [P, J, E0])
            lm = sb("lm", [P, J, E0])
            ex = sb("ex", [P, J, E0])
            esum = sb("esum", [P, J])
            erec = sb("erec", [P, J])
            gp = sb("gp", [P, J, 32])
            gT = sb("gT", [P, P])
            hid = sb("hid", [P, 2, FC, T])
            prod = sb("prod", [P, 2, J, D])
            facc = sb("facc", [P, J, D])
            x2 = sb("x2", [P, J, D])
            hT3 = sb("hT3", [P, T])
            sq = sb("sq", [P, 2, T])
            ssq = sb("ssq", [P, 2 * J, 8])
            mxs = sb("mxs", [P, 2 * J])
            bmx = sb("bmx", [P, 1])
            cb = sb("cb", [P, 1])
            ncb = sb("ncb", [P, 1])
            Ek = sb("Ek", [P, J, HD])
            V = sb("V", [P, J, PR, VW])
            kvs = sb("kvs", [P, PR * VW + 1])

            w_in, a_exp, a_neg, init, passed = (sem(n) for n in ("w1_in", "a_exp", "a_neg", "init1", "passed1"))
            x_in, ga_in, gb_in, x2_out, h3_out, kv_out = (
                sig(n, 16) for n in ("x_in", "ga_in", "gb_in", "x2_out", "h3_out", "kv_out"))
            L1, L2, L3 = (Norm(sb, sig, n, EPS_MOD) for n in ("n1", "n2", "n3"))
            (in_done, xraw, zsilu, conv, xc_ok, xdbl, dtr_ok, s_hi, s_mid, s_rem, s_remb, s_lo, dtps, dtabs, dtexp,
             dtln, dtmax, dt_ok, dtx_ok, acc0, bb, cbc, dec_ok, u_ok, scan, z_ok, accum, yz_ok, oproj, ao_ok,
             x1_ok, chainA) = (sig(n, p) for n, p in (
                 ("in_done", 4), ("xraw", 2), ("zsilu", 2), ("conv", 2), ("xc_ok", 1), ("xdbl", 1), ("dtr_ok", 1),
                 ("s_hi", 1), ("s_mid", 1), ("s_rem", 1), ("s_remb", 1), ("s_lo", 1), ("dtps", 2), ("dtabs", 2),
                 ("dtexp", 1), ("dtln", 1), ("dtmax", 2), ("dt_ok", 1), ("dtx_ok", 1), ("acc0", 1), ("bb", NS),
                 ("cbc", NS), ("dec_ok", 2 * NS), ("u_ok", NS), ("scan", 2 * NS), ("z_ok", NS), ("accum", NS),
                 ("yz_ok", 1), ("oproj", 1), ("ao_ok", 1), ("x1_ok", 1), ("chainA", G * (TAPS - 1))))
            (logits, lshift, lexp, gw, gturn, gT_ok, b2ps, facc0, up, hid_ok, down, prod_ok, fadd, x2m, x2_ok,
             kps, dps, vps, sq_ok, ssum, ush, vc, bmx_ok, call, ncb_ok, mxr, kvc, kf, kv, kvs_ok, chainB) = (
                sig(n, p) for n, p in (
                    ("logits", 1), ("lshift", 1), ("lexp", 1), ("gw", 1), ("gturn", 1), ("gT_ok", 1), ("b2ps", 1),
                    ("facc0", 1), ("up", E0 * FC), ("hid_ok", E0 * FC), ("down", E0), ("prod_ok", E0), ("fadd", E0),
                    ("x2m", 1), ("x2_ok", 1), ("kps", 2 * J), ("dps", 2 * J), ("vps", 2 * J), ("sq_ok", 2 * J),
                    ("ssum", 2 * J), ("ush", 2 * J), ("vc", 2 * J), ("bmx_ok", 1), ("call", 1), ("ncb_ok", 1),
                    ("mxr", 1), ("kvc", 1), ("kf", J), ("kv", 1), ("kvs_ok", 3), ("chainB", 5 + 2 * J)))

            ring = [("turn2", L2.out, 1), ("logits", lshift, 1), ("up0", hid_ok, 1), ("up1", hid_ok, 2),
                    ("gates", gT_ok, 1)]
            ring += [(f"up{n}", hid_ok, n + 1) for n in range(2, E0 * FC)]
            ring += [("turn3", L3.out, 1)]
            for m in range(2 * J):
                ring += [(f"k{m}", sq_ok, m + 1), (f"d{m}", ush, m + 1), (f"v{m}", vc, m + 1)]
            RN = 3
            assert len(ring) % RN == 0
            use = {name: n for n, (name, _, _) in enumerate(ring)}

            def ring1(name):
                return banks[2 + use[name] % RN]

            def ring1_free(pe, name, b):
                n = use[name] - RN
                if n >= 0:
                    pe.wait_ge(*ring[n][1](b, ring[n][2]))
                else:
                    pe.wait_ge(*ring[n][1](b, 0))

            SLOTS = 4 + NS + 1

            HALVES = {1: (0,), 2: (1, 2), 3: (3, 4)}
            HALVES.update({s: (s + 1,) for s in range(4, 15)})
            PROD_SLOT = {}
            for s, hs in HALVES.items():
                for q in hs:
                    if q % 2:
                        PROD_SLOT[s + 1] = q // 2

            def sweep(eng, step):
                step(0, None)
                step(1, 0)
                with eng.Fori(2, NB) as i:
                    step(i, i - 1)
                step(None, NB - 1)

            with nc.Block() as block:
                @block.sync
                def _(sp):
                    sp.dma_start(one_sb[:, :], one).then_inc(w_in, 16)
                    sp.dma_start(pick_sb[:, :, :], pick16).then_inc(w_in, 16)

                    def step(a, b):
                        if a is not None:
                            sp.wait_ge(*x1_ok(a, 0))
                            sp.dma_start(xs[:, :, :], x_v[a]).then_inc(x_in.sem, 16)
                            sp.dma_start(ga[:, :], gate_rows[0, a].partition_broadcast(P)).then_inc(ga_in.sem, 16)
                        if b is not None:
                            sp.wait_ge(*x2_ok(b, 0))
                            sp.dma_start(gb[:, :], gate_rows[1, b].partition_broadcast(P)).then_inc(gb_in.sem, 16)
                            sp.wait_ge(*x2_ok(b, 1))
                            sp.dma_start(x2_dram[b], x2[:, :, :].rearrange("p j d -> p (j d)"))\
                              .then_inc(x2_out.sem, 16)
                            sp.wait_ge(*L3.out(b, 1))
                            sp.dma_start(h3_dram[b], hT3[:, :]).then_inc(h3_out.sem, 16)

                    sweep(sp, step)
                    sp.wait_ge(*x2_out(NB, 0))
                    sp.wait_ge(*h3_out(NB, 0))
                    sp.wait_ge(*kv_out(NB, 0))

                @block.scalar
                def _(act):
                    act.wait_ge(w_in, 32)
                    act.activation(aneg[:, :, :].rearrange("p g n -> p (g n)"), alog, ACT.Exp).then_inc(a_exp, 1)
                    act.wait_ge(a_neg, 1)
                    act.wait_ge(init, 4)

                    def mamba(slot, a):
                        if slot == 0:
                            act.wait_ge(*L1.turned(a, 1))
                            act.wait_ge(*in_done(a, 0))
                            act.activation(hT[:, :], banks[0][:, :], ACT.Identity, scale=modc[:, 0, a, 1:2],
                                           bias=modc[:, 0, a, 0:1]).then_inc(L1.out.sem, 1)
                        elif slot == 1:
                            for g in range(G):
                                act.wait_ge(*in_done(a, g + 1))
                                act.wait_ge(*conv(a, 0))
                                act.activation(xpad[:, g, PAD:], banks[g][:, :], ACT.Copy).then_inc(xraw.sem, 1)
                            for g in range(G):
                                act.wait_ge(*in_done(a, G + g + 1))
                                act.wait_ge(*yz_ok(a, 0))
                                act.activation(zs[:, g, :], banks[g][:, :], ACT.Silu).then_inc(zsilu.sem, 1)
                            act.wait_ge(*conv(a, G))
                            act.wait_ge(*acc0(a, 0))
                            act.wait_ge(*dtx_ok(a, 0))
                            act.activation(xc[:, :, :], cv[:, :, :], ACT.Silu).then_inc(xc_ok.sem, 1)
                        elif slot == 2:
                            act.wait_ge(*xdbl(a, 1))
                            act.wait_ge(*dtps(a, 0))
                            act.activation(dtr[96:96 + RK, :], banks[0][96:96 + RK, :], ACT.Copy)\
                               .then_inc(dtr_ok.sem, 1)
                            act.wait_ge(*cbc(a, 0))
                            act.activation(S[0:96, :], banks[0][0:96, :], ACT.Copy).then_inc(s_hi.sem, 1)
                            act.wait_ge(*s_rem(a, 1))
                            act.activation(Rb[64:96, :], R[64:96, :], ACT.Copy).then_inc(s_remb.sem, 1)
                        elif slot == 3:
                            for g in range(G):
                                act.wait_ge(*dtps(a, g + 1))
                                act.wait_ge(*xc_ok(a, 1))
                                act.activation(ax[:, g, :], banks[1 - g][:, :], ACT.Abs, bias=dtb[:, g:g + 1])\
                                   .then_inc(dtabs.sem, 1)
                            act.wait_ge(*dtabs(a, G))
                            act.activation(ax[:, :, :], ax[:, :, :], ACT.Exp, scale=-1.0).then_inc(dtexp.sem, 1)
                            act.wait_ge(*dtexp(a, 1))
                            act.activation(ax[:, :, :], ax[:, :, :], ACT.Ln, bias=1.0).then_inc(dtln.sem, 1)
                            act.wait_ge(*yz_ok(a, 0))
                            for g in range(G):
                                last = act.activation(acc[:, g, :], xc[:, g, :], ACT.Copy, scale=dskip[:, g:g + 1])
                            last.then_inc(acc0.sem, 1)
                        elif slot < 4 + NS:
                            n = slot - 4
                            if n == 0:
                                act.wait_ge(*dt_ok(a, 1))
                            act.wait_ge(*scan(a, G * (n - 1) if n >= 2 else 0))
                            for g in range(G):
                                act.activation(dec[:, n % 2, g, :], dt[:, g, :], ACT.Exp,
                                               scale=aneg[:, g, n:n + 1]).then_inc(dec_ok.sem, 1)

                    def relus(b, first, last):
                        for n in range(first, last):
                            e, f = divmod(n, FC)
                            act.wait_ge(*up(b, n + 1))
                            act.wait_ge(*down(b, e - 1 if e >= 2 else 0))
                            act.activation(hid[:, e % 2, f, :], banks[2 + use[f"up{n}"] % RN][:, :], ACT.Relu,
                                           bias=b1c[:, n:n + 1]).then_inc(hid_ok.sem, 1)

                    def key_tile(b, m):
                        j, s = divmod(m, 2)
                        act.wait_ge(*kps(b, m + 1))
                        act.wait_ge(*ssum(b, m - 1 if m >= 2 else 0))
                        act.activation(sq[:, m % 2, :], ring1(f"k{m}")[:, :], ACT.Square).then_inc(sq_ok.sem, 1)
                        act.wait_ge(*vps(b, m + 1))
                        act.wait_ge(*kv(b, 0))
                        act.activation(V[:, j, 4 * s:4 * s + 4, 0:P],
                                       ring1(f"v{m}")[:, :].rearrange("p (r d) -> p r d", r=4),
                                       ACT.Copy).then_inc(vc.sem, 1)

                    def experts(slot, b):
                        if slot == 0:
                            act.wait_ge(*L2.turned(b, 1))
                            act.wait_ge(*up(b, 0))
                            act.activation(hT2[:, :], ring1("turn2")[:, :], ACT.Identity, scale=modc[:, 0, b, 3:4],
                                           bias=modc[:, 0, b, 2:3]).then_inc(L2.out.sem, 1)
                        elif slot == 1:
                            act.wait_ge(*lshift(b, 1))
                            act.activation(ex[:, :, :], lm[:, :, :], ACT.Exp).then_inc(lexp.sem, 1)
                            relus(b, 0, 2)
                        elif slot == 2:
                            act.wait_ge(*gturn(b, 1))
                            act.wait_ge(*b2ps(b, 0))
                            act.activation(gT[:, :], ring1("gates")[:, 0:P], ACT.Copy).then_inc(gT_ok.sem, 1)
                            relus(b, 2, 6)
                        elif slot == 3:
                            relus(b, 6, 10)
                        elif slot <= 14:
                            relus(b, 2 * (slot + 1), 2 * (slot + 1) + 2)
                        elif slot == 16:
                            act.wait_ge(*L3.turned(b, 1))
                            act.wait_ge(*vps(b, 0))
                            act.wait_ge(*h3_out(b, 0))
                            act.activation(hT3[:, :], ring1("turn3")[:, :], ACT.Identity, scale=modc[:, 1, b, 1:2],
                                           bias=modc[:, 1, b, 0:1]).then_inc(L3.out.sem, 1)
                        elif slot >= 17:
                            key_tile(b, 2 * (slot - 17))
                            key_tile(b, 2 * (slot - 17) + 1)
                        if slot == SLOTS - 1:
                            act.wait_ge(*ncb_ok(b, 1))
                            act.wait_ge(*ush(b, 2 * J))
                            for j in range(J):
                                act.activation(Ek[:, j, :], Ek[:, j, :], ACT.Exp, bias=ncb[:, 0:1]).then_inc(kf.sem, 1)
                            act.wait_ge(*kv(b, 1))
                            act.wait_ge(*kv_out(b, 0))
                            for n, (first, count) in enumerate(((0, 3), (3, 3), (6, 2))):
                                act.activation(kvs[:, first * VW:(first + count) * VW],
                                               banks[5 + n][:, 0:count * VW], ACT.Copy).then_inc(kvs_ok.sem, 1)
                            act.wait_ge(*kvs_ok(b, 3))
                            act.wait_ge(*kvc(b, 1))
                            act.dma_start(kv_dram[b], kvs[:, :]).then_inc(kv_out.sem, 16)

                    def step(a, b):
                        for slot in range(SLOTS):
                            if a is not None:
                                mamba(slot, a)
                            if b is not None:
                                experts(slot, b)

                    sweep(act, step)

                @block.gpsimd
                def _(pool):
                    pool.memset(xpad[:, :, 0:PAD], 0.0).then_inc(init, 1)
                    pool.memset(V[:, :, :, P:VW], 1.0).then_inc(init, 1)
                    pool.memset(gp[:, :, :], 0.0).then_inc(init, 1)
                    pool.memset(x1[:, :, :], 0.0).then_inc(init, 1)

                    def mamba(slot, a):
                        if slot == 0:
                            norm_pool(pool, L1, half, a, passed)
                        elif 4 <= slot < 4 + NS:
                            n = slot - 4
                            if n == 0:
                                pool.wait_ge(*acc0(a, 1))
                            pool.wait_ge(*z_ok(a, n + 1))
                            pool.wait_ge(*accum(a, n))
                            pool.tensor_tensor(acc[:, :, :], acc[:, :, :], zz[:, n % 2, :, :], ALU.add)\
                                .then_inc(accum.sem, 1)

                    def add_expert(b, e):
                        pool.wait_ge(*prod_ok(b, e + 1))
                        if e == 0:
                            pool.wait_ge(*facc0(b, 1))
                        pool.wait_ge(*fadd(b, e))
                        pool.tensor_tensor(facc[:, :, :], facc[:, :, :], prod[:, e % 2, :, :], ALU.add)\
                            .then_inc(fadd.sem, 1)

                    def experts(slot, b):
                        if slot == 0:
                            norm_pool(pool, L2, half, b, passed)
                        elif 3 <= slot <= 15 and slot in PROD_SLOT:
                            add_expert(b, PROD_SLOT[slot])
                        if slot == 15:
                            pool.wait_ge(*fadd(b, E0))
                            pool.wait_ge(*gb_in(b, 16))
                            pool.tensor_tensor(facc[:, :, :], facc[:, :, :], mid(gb[:, :], J), ALU.mult)\
                                .then_inc(x2m.sem, 1)
                            pool.wait_ge(*x2m(b, 1))
                            pool.wait_ge(*x2_out(b, 0))
                            pool.wait_ge(*L3.xhat(b, 0))
                            pool.tensor_tensor(x2[:, :, :], x1[:, :, :], facc[:, :, :], ALU.add).then_inc(x2_ok.sem, 1)
                        elif slot == 16:
                            norm_pool(pool, L3, half, b, passed)
                        elif slot == SLOTS - 1:
                            pool.wait_ge(*bmx_ok(b, 1))
                            pool.wait_ge(*kf(b, 0))
                            pool.wait_ge(*kvc(b, 0))
                            hold(pool, passed)
                            pool.partition_all_reduce(cb[:, :], bmx[:, :], P, RMAX).then_inc(call.sem, 1)
                            pool.wait_ge(*call(b, 1))
                            hold(pool, passed)
                            pool.tensor_scalar(ncb[:, :], cb[:, :], -1.0, None, ALU.mult).then_inc(ncb_ok.sem, 1)
                            pool.wait_ge(*mxr(b, 0))
                            hold(pool, passed)
                            pool.tensor_scalar(mxrun[:, :], mxrun[:, :], cb[:, 0:1], None, ALU.max)\
                                .then_inc(mxr.sem, 1)
                            pool.wait_ge(*kv_out(b, 0))
                            hold(pool, passed)
                            pool.tensor_copy(kvs[:, PR * VW:], cb[:, :]).then_inc(kvc.sem, 1)

                    def step(a, b):
                        for slot in range(SLOTS):
                            if a is not None:
                                mamba(slot, a)
                            if b is not None:
                                experts(slot, b)

                    sweep(pool, step)

                @block.tensor
                def _(pe):
                    pe.wait_ge(w_in, 32)

                    def mamba(slot, a):
                        if slot == 0:
                            pe.wait_ge(*u_ok(a, 0))
                            norm_pe(pe, L1, banks[0], ident, a)
                        elif slot == 1:
                            pe.wait_ge(*L1.out(a, 1))
                            for c in range(2 * G):
                                if c == 1:
                                    pe.wait_ge(*ao_ok(a, 0))
                                elif c >= G:
                                    pe.wait_ge(*xraw(a, c - G + 1))
                                pe.matmul(banks[c % 2][:, :], inw[:, c * P:(c + 1) * P], hT[:, :],
                                          start=True, stop=True).then_inc(in_done.sem, 1)
                        elif slot == 2:
                            pe.wait_ge(*xc_ok(a, 1))
                            pe.wait_ge(*zsilu(a, 1))
                            for g in range(G):
                                last = pe.matmul(banks[0][:, :], xw[:, g, :], xc[:, g, :],
                                                 start=(g == 0), stop=(g == G - 1))
                            last.then_inc(xdbl.sem, 1)
                        elif slot == 3:
                            pe.wait_ge(*dtr_ok(a, 1))
                            for g in range(G):
                                if g == 0:
                                    pe.wait_ge(*zsilu(a, 2))
                                else:
                                    pe.wait_ge(*s_hi(a, 1))
                                    pe.wait_ge(*s_rem(a, 1))
                                pe.matmul(banks[1 - g][:, :], dtw[96:96 + RK, g * P:(g + 1) * P],
                                          dtr[96:96 + RK, :], start=True, stop=True).then_inc(dtps.sem, 1)

                    def spread(a, n, which):
                        if n == 0:
                            pe.wait_ge(*s_mid(a, 1))
                            pe.wait_ge(*s_lo(a, 1))
                            pe.wait_ge(*dtmax(a, 2 - which))
                        else:
                            pe.wait_ge(*(z_ok if which else u_ok)(a, n))
                        pe.matmul(banks[which][:, :], pick_sb[:, which * NS + n, :], S[0:96, :],
                                  start=True, stop=True).then_inc((cbc if which else bb).sem, 1)

                    def mamba_out(a):
                        pe.wait_ge(*yz_ok(a, 1))
                        pe.wait_ge(*z_ok(a, NS))
                        for j in range(J):
                            for g in range(G):
                                last = pe.matmul(banks[1][:, j * D:(j + 1) * D], yz[:, g, j * P:(j + 1) * P],
                                                 outw[:, g, :], start=(g == 0), stop=(g == G - 1))
                        last.then_inc(oproj.sem, 1)

                    def ups(b, q):
                        for n in range(2 * q, 2 * q + 2):
                            e, f = divmod(n, FC)
                            ring1_free(pe, f"up{n}", b)
                            pe.matmul(ring1(f"up{n}")[:, :], w1[:, e, f * P:(f + 1) * P], hT2[:, :],
                                      start=True, stop=True).then_inc(up.sem, 1)

                    def downs(b, e):
                        pe.wait_ge(*hid_ok(b, FC * (e + 1)))
                        if e < 2:
                            pe.wait_ge(*kvs_ok(b, 0))
                        else:
                            pe.wait_ge(*prod_ok(b, e - 1))
                        for j in range(J):
                            for f in range(FC):
                                last = pe.matmul(banks[5 + e % 2][:, j * D:(j + 1) * D],
                                                 hid[:, e % 2, f, j * P:(j + 1) * P], w2[:, e, f, :],
                                                 start=(f == 0), stop=(f == FC - 1))
                        last.then_inc(down.sem, 1)

                    def key_tile(b, m):
                        j, s = divmod(m, 2)
                        for name, w, done in (("k", wk, kps), ("d", pk[:, :], dps), ("v", wv, vps)):
                            ring1_free(pe, f"{name}{m}", b)
                            pe.matmul(ring1(f"{name}{m}")[:, :], hT3[:, j * P:(j + 1) * P],
                                      w[:, s * T:(s + 1) * T], start=True, stop=True).then_inc(done.sem, 1)

                    def experts(slot, b):
                        if slot == 0:
                            ring1_free(pe, "turn2", b)
                            norm_pe(pe, L2, ring1("turn2"), ident, b)
                            ring1_free(pe, "logits", b)
                            pe.wait_ge(*L2.out(b, 1))
                            for j in range(J):
                                last = pe.matmul(ring1("logits")[:, j * E0:(j + 1) * E0], hT2[:, j * P:(j + 1) * P],
                                                 gatew, start=True, stop=True)
                            last.then_inc(logits.sem, 1)
                        if slot == 2:
                            pe.wait_ge(*gw(b, 1))
                            ring1_free(pe, "gates", b)
                            pe.transpose(ring1("gates")[:, 0:P], gp[:, :, :].rearrange("p j e -> p (j e)"),
                                         ident).then_inc(gturn.sem, 1)
                        for q in HALVES.get(slot, ()):
                            ups(b, q)
                            if q == 1:
                                pe.wait_ge(*gT_ok(b, 1))
                                pe.wait_ge(*kvs_ok(b, 0))
                                pe.matmul(banks[7][:, :], gT[:, :], b2, start=True, stop=True).then_inc(b2ps.sem, 1)
                            if q % 2:
                                downs(b, q // 2)
                        if slot == 16:
                            ring1_free(pe, "turn3", b)
                            norm_pe(pe, L3, ring1("turn3"), ident, b)
                        elif slot >= 17:
                            if slot == 17:
                                pe.wait_ge(*L3.out(b, 1))
                            key_tile(b, 2 * (slot - 17))
                            key_tile(b, 2 * (slot - 17) + 1)
                        if slot == SLOTS - 1:
                            pe.wait_ge(*prod_ok(b, E0))
                            pe.wait_ge(*facc0(b, 1))
                            pe.wait_ge(*vc(b, 2 * J))
                            for j in range(J):
                                pe.wait_ge(*kf(b, j + 1))
                                for pr in range(PR):
                                    at = (pr % 3) * VW
                                    last = pe.matmul(banks[5 + pr // 3][:, at:at + VW],
                                                     Ek[:, j, pr * P:(pr + 1) * P], V[:, j, pr, :],
                                                     start=(j == 0 and pr % 3 == 0), stop=(j == J - 1),
                                                     skip_group_check=True)
                            last.then_inc(kv.sem, 1)

                    def step(a, b):
                        for slot in range(SLOTS):
                            n = slot - 4
                            if a is not None:
                                mamba(slot, a)
                                if 0 <= n < NS:
                                    spread(a, n, 0)
                                    spread(a, n, 1)
                                if n == NS:
                                    mamba_out(a)
                            if b is not None:
                                experts(slot, b)

                    sweep(pe, step)

                @block.vector
                def _(dve):
                    dve.wait_ge(a_exp, 1)
                    dve.tensor_scalar(aneg[:, :, :], aneg[:, :, :], -1.0, None, ALU.mult).then_inc(a_neg, 1)
                    dve.wait_ge(init, 4)
                    cA, cB = Chain(dve, chainA), Chain(dve, chainB)

                    def mamba(slot, a):
                        if slot == 0:
                            dve.wait_ge(*x_in(a, 16))
                            norm_dve(dve, L1, xs, a, passed)
                        elif slot == 1:
                            dve.wait_ge(*xc_ok(a, 0))
                            dve.wait_ge(*dt_ok(a, 0))
                            for g in range(G):
                                dve.wait_ge(*xraw(a, g + 1))
                                cA.step(dve.tensor_scalar(cv[:, g, :], xpad[:, g, PAD:], convw[:, g, PAD:],
                                                          convb[:, g:g + 1], ALU.mult, ALU.add))
                                for k in range(PAD):
                                    ins = dve.scalar_tensor_tensor(cv[:, g, :], xpad[:, g, k:k + T],
                                                                   convw[:, g, k:k + 1], cv[:, g, :],
                                                                   ALU.mult, ALU.add)
                                    if k < PAD - 1:
                                        cA.step(ins)
                                    else:
                                        ins.then_inc(conv.sem, 1)
                        elif slot == 2:
                            dve.wait_ge(*s_hi(a, 1))
                            dve.tensor_tensor(S[32:64, :], banks[0][32:64, :], S[32:64, :], ALU.subtract)\
                               .then_inc(s_mid.sem, 1)
                            dve.wait_ge(*s_lo(a, 0))
                            dve.tensor_tensor(R[64:96, :], banks[0][64:96, :], S[64:96, :], ALU.subtract)\
                               .then_inc(s_rem.sem, 1)
                            dve.wait_ge(*s_remb(a, 1))
                            dve.tensor_tensor(S[64:96, :], R[64:96, :], Rb[64:96, :], ALU.subtract)\
                               .then_inc(s_lo.sem, 1)
                        elif slot == 3:
                            dve.wait_ge(*dec_ok(a, 0))
                            for g in range(G):
                                dve.wait_ge(*dtabs(a, g + 1))
                                dve.tensor_scalar(dt[:, g, :], banks[1 - g][:, :], dtb[:, g:g + 1], 0.0,
                                                  ALU.add, ALU.max).then_inc(dtmax.sem, 1)
                            dve.wait_ge(*dtln(a, 1))
                            dve.wait_ge(*dtmax(a, G))
                            dve.tensor_tensor(dt[:, :, :], dt[:, :, :], ax[:, :, :], ALU.add).then_inc(dt_ok.sem, 1)
                            dve.wait_ge(*dt_ok(a, 1))
                            dve.tensor_tensor(dtx[:, :, :], dt[:, :, :], xc[:, :, :], ALU.mult)\
                               .then_inc(dtx_ok.sem, 1)
                            dve.wait_ge(*dtx_ok(a, 1))
                            dve.wait_ge(*oproj(a, 0))
                        elif slot < 4 + NS:
                            n = slot - 4
                            dve.wait_ge(*bb(a, n + 1))
                            dve.tensor_tensor(u[:, :, :], dtx[:, :, :], mid(banks[0][:, :], G), ALU.mult)\
                               .then_inc(u_ok.sem, 1)
                            dve.wait_ge(*u_ok(a, n + 1))
                            for g in range(G):
                                dve.wait_ge(*dec_ok(a, G * n + g + 1))
                                dve.tensor_tensor_scan(h[:, g, :], dec[:, n % 2, g, :], u[:, g, :], 0.0,
                                                       ALU.mult, ALU.add).then_inc(scan.sem, 1)
                            dve.wait_ge(*scan(a, G * (n + 1)))
                            dve.wait_ge(*cbc(a, n + 1))
                            dve.wait_ge(*accum(a, n - 1 if n >= 2 else 0))
                            dve.tensor_tensor(zz[:, n % 2, :, :], h[:, :, :], mid(banks[1][:, :], G), ALU.mult)\
                               .then_inc(z_ok.sem, 1)
                            dve.wait_ge(*z_ok(a, n + 1))
                        else:
                            dve.wait_ge(*accum(a, NS))
                            dve.wait_ge(*zsilu(a, G))
                            dve.tensor_tensor(yz[:, :, :], acc[:, :, :], zs[:, :, :], ALU.mult).then_inc(yz_ok.sem, 1)
                            dve.wait_ge(*oproj(a, 1))
                            dve.wait_ge(*ga_in(a, 16))
                            dve.tensor_tensor(ao[:, :, :], banks[1][:, :].rearrange("p (j d) -> p j d", j=J),
                                              mid(ga[:, :], J), ALU.mult).then_inc(ao_ok.sem, 1)
                            dve.wait_ge(*ao_ok(a, 1))
                            dve.wait_ge(*x2_ok(a, 0))
                            dve.tensor_tensor(x1[:, :, :], xs[:, :, :], ao[:, :, :], ALU.add).then_inc(x1_ok.sem, 1)

                    def key_tile(b, m):
                        j, s = divmod(m, 2)
                        dash = ring1(f"d{m}")[:, :].rearrange("p (h k) -> p h k", h=8)
                        dve.wait_ge(*sq_ok(b, m + 1))
                        dve.tensor_reduce(ssq[:, m, :], sq[:, m % 2, :].rearrange("p (h k) -> p h k", h=8),
                                          AX.X, ALU.add).then_inc(ssum.sem, 1)
                        dve.wait_ge(*dps(b, m + 1))
                        cB.step(dve.tensor_reduce(mxs[:, m:m + 1], dash, AX.XY, ALU.max))
                        dve.wait_ge(*ssum(b, m + 1))
                        dve.wait_ge(*kv(b, 0))
                        dve.scalar_tensor_tensor(
                            Ek[:, j, s * T:(s + 1) * T].rearrange("p (h k) -> p h k", h=8),
                            inner(ssq[:, m, :], DH), -DIAG, dash, ALU.mult, ALU.add).then_inc(ush.sem, 1)

                    def experts(slot, b):
                        if slot == 0:
                            dve.wait_ge(*x1_ok(b, 1))
                            norm_dve(dve, L2, x1, b, passed)
                        elif slot == 1:
                            dve.wait_ge(*logits(b, 1))
                            lg = ring1("logits")[:, 0:J * E0].rearrange("p (j e) -> p j e", j=J)
                            hold(dve, passed)
                            for j in range(J):
                                last = dve.max(m8[:, j, :], lg[:, j, :])
                            cB.step(last)
                            hold(dve, passed)
                            for j in range(J):
                                last = dve.max_index(idx[:, j, :], m8[:, j, :], lg[:, j, :])
                            cB.step(last)
                            dve.wait_ge(*gw(b, 0))
                            cB.step(dve.tensor_tensor(oh[:, :, :], mid(iota[:, 0:E0], J),
                                                      idx[:, :, 0:1].to_broadcast([P, J, E0]), ALU.is_equal))
                            dve.wait_ge(*lexp(b, 0))
                            dve.tensor_tensor(lm[:, :, :], lg, m8[:, :, 0:1].to_broadcast([P, J, E0]),
                                              ALU.subtract).then_inc(lshift.sem, 1)
                            dve.wait_ge(*lexp(b, 1))
                            cB.step(dve.tensor_reduce(esum[:, :], ex[:, :, :], AX.X, ALU.add))
                            cB.step(dve.reciprocal(erec[:, :], esum[:, :]))
                            dve.wait_ge(*gturn(b, 0))
                            dve.tensor_tensor(gp[:, :, 0:E0], oh[:, :, :], inner(erec[:, :], E0),
                                              ALU.mult).then_inc(gw.sem, 1)
                            dve.wait_ge(*gw(b, 1))
                        if slot == 3:
                            dve.wait_ge(*b2ps(b, 1))
                            dve.wait_ge(*x2_ok(b, 0))
                            dve.tensor_copy(facc[:, :, :].rearrange("p j d -> p (j d)"), banks[7][:, :])\
                               .then_inc(facc0.sem, 1)
                        if slot in PROD_SLOT:
                            e = PROD_SLOT[slot]
                            dve.wait_ge(*down(b, e + 1))
                            dve.wait_ge(*fadd(b, e - 1 if e >= 2 else 0))
                            dve.tensor_tensor(prod[:, e % 2, :, :],
                                              banks[5 + e % 2][:, :].rearrange("p (j d) -> p j d", j=J),
                                              gp[:, :, e:e + 1].to_broadcast([P, J, D]), ALU.mult)\
                               .then_inc(prod_ok.sem, 1)
                        if slot == 16:
                            dve.wait_ge(*x2_ok(b, 1))
                            norm_dve(dve, L3, x2, b, passed)
                        elif slot >= 17:
                            key_tile(b, 2 * (slot - 17))
                            key_tile(b, 2 * (slot - 17) + 1)
                        if slot == SLOTS - 1:
                            dve.wait_ge(*call(b, 0))
                            dve.tensor_reduce(bmx[:, :], mxs[:, :], AX.X, ALU.max).then_inc(bmx_ok.sem, 1)

                    def step(a, b):
                        cA.begin(a)
                        cB.begin(b)
                        for slot in range(SLOTS):
                            if a is not None:
                                mamba(slot, a)
                            if b is not None:
                                experts(slot, b)

                    sweep(dve, step)

            end_part()

        sweep_two(nc, ctx, sem, sig, sbuf, banks, ident, iota, wv, pq, modc, ones, half, mxrun, nmx, two,
                  gate_rows, x2_dram, h3_dram, kv_dram, out_v)


def sweep_two(nc, ctx, sem, sig, sbuf, banks, ident, iota, wv, pq, modc, ones, half, mxrun, nmx, two,
              gate_rows, x2_dram, h3_dram, kv_dram, out_v):
    with ExitStack() as part:
        sb = sbuf(part)
        two_sb = sb("two_sb", [P, TWO_N])

        def V2(name):
            at, n = TWO[name]
            return two_sb[:, at:at + n]

        wq, w1, b1c, b2r, g1, be1, g2, be2, gatew, mw1 = (
            V2(n) for n in ("wq", "w1", "b1", "b2", "g1", "be1", "g2", "be2", "gate", "mw1"))
        wo = V2("wo").rearrange("p (r d) -> p r d", r=PR)
        w2 = V2("w2").rearrange("p (f d) -> p f d", f=FC)
        mw2 = V2("mw2").rearrange("p (r d) -> p r d", r=MC)
        s1w, s2w = V2("s1"), V2("s2")
        s3w = V2("s3").rearrange("p (r d) -> p r d", r=SC)
        pick = V2("pick").rearrange("p (r m) -> p r m", r=MC)
        h3 = sb("h3", [P, T])
        kvl = sb("kvl", [P, PR * VW + 1])
        sfac = sb("sfac", [P, 1])
        hsum = sb("hsum", [P, 1])
        hsB = sb("hsB", [P, P])
        evs = sb("evs", [P, HD])
        kvb = sb("kvb", [P, PR, P])
        ksb = sb("ksb", [P, PR, 2])
        qsqb = sb("qsqb", [P, 2, T])
        qs = sb("qs", [P, 8])
        qm = sb("qm", [P, 8])
        nb = sb("nb", [P, 8])
        uq = sb("uq", [P, 2, T])
        qT = sb("qT", [P, 2, T])
        rd = sb("rd", [P, 8])
        at = sb("at", [P, 2, T])
        aT = sb("aT", [P, 2, T])
        o1T = sb("o1T", [P, T])
        x2 = sb("x2s", [P, J, D])
        gab = sb("gab", [P, 2, D])
        gg = sb("gg", [P, D])
        gbe = sb("gbe", [P, D])
        vb = sb("vb", [P, 2, T])
        ee = sb("ee", [P, 2, T])
        hE = sb("hE", [P, FC, T])
        t6 = sb("t6", [P, J, D])
        x3 = sb("x3", [P, J, D])
        hT4 = sb("hT4", [P, T])
        m8 = sb("m8b", [P, J, 8])
        idx = sb("idxb", [P, J, 8], U32)
        gd = sb("gd", [P, J])
        gex = sb("gex", [P, J])
        gsum = sb("gsum", [P, J])
        gw1 = sb("gw1", [P, J])
        gw2 = sb("gw2", [P, J])
        oh1 = sb("oh1", [P, J, E1])
        oh2 = sb("oh2", [P, J, E1])
        disp = sb("disp", [P, J, E1])
        dT = sb("dT", [E1, T])
        NX = MC + SC
        th = sb("th", [P, 2, T])
        sl = sb("sl", [P, 2, T])
        hm = sb("hm", [P, NX, T])
        fo = sb("fo", [P, J, D])
        ob = sb("ob", [P, J, D])

        w_in, init, nmx_ok, passed = (sem(n) for n in ("w2_in", "init2", "nmx_ok", "passed2"))
        h3_in, kv_in, x2_in, gab_in, res_out = (sig(n, 16) for n in ("h3_in", "kv_in", "x2_in", "gab_in", "res_out"))
        gab_in.per = 32
        L5, L6, L7 = (Norm(sb, sig, n, e) for n, e in (("n5", EPS_ENC), ("n6", EPS_ENC), ("n7", EPS_MOD)))
        M = 2 * J
        (sf, hsb, vsps, evs_ok, kvb_ok, qps, qd, qsq, qss, qu, qe, qt, qT_ok, num, rd_ok, at_ok, att, aT_ok,
         wo_ok, chainC) = (sig(n, p) for n, p in (
             ("sf", 1), ("hsb", 1), ("vsps", 2), ("evs_ok", 2), ("kvb_ok", 1), ("qps", M), ("qd", M), ("qsq", M),
             ("qss", M), ("qu", M), ("qe", M), ("qt", M), ("qT_ok", M), ("num", M), ("rd_ok", M), ("at_ok", M),
             ("att", M), ("aT_ok", M), ("wo_ok", M), ("chainC", 1 + 2 * M)))
        (w1ps, vb_ok, ee_ok, em_ok, he, w2ps, gg_ok, t6a, t6b, x3_ok, lg_ok, gidx, gd_ok, gex_ok, disp_ok, dtp, dT_ok,
         xps, yps, th_ok, sl_ok, hm_ok, mo, fin, ob_ok, chainD) = (sig(n, p) for n, p in (
             ("w1ps", FC), ("vb_ok", FC), ("ee_ok", FC), ("em_ok", FC), ("he", FC), ("w2ps", 1), ("gg_ok", 1), ("t6a", 1),
             ("t6b", 1), ("x3_ok", 1), ("lg_ok", 1), ("gidx", 1), ("gd_ok", 1), ("gex_ok", 1), ("disp_ok", 1),
             ("dtp", 1), ("dT_ok", 1), ("xps", NX), ("yps", NX), ("th_ok", NX), ("sl_ok", NX), ("hm_ok", NX),
             ("mo", 1), ("fin", 1), ("ob_ok", 1), ("chainD", 8)))

        ringC = [("vs0", evs_ok, 1), ("vs1", evs_ok, 2)]
        for t in range(M + 2):
            if t < M:
                ringC += [(f"q{t}", qsq, t + 1), (f"d{t}", qu, t + 1)]
            if 1 <= t <= M:
                ringC += [(f"t{t - 1}", qT_ok, t), (f"n{t - 1}", at_ok, t)]
            if t >= 2:
                ringC += [(f"a{t - 2}", aT_ok, t - 1)]
        ringC += [("turn5", L5.out, 1)]
        ringD = [(f"w{f}", vb_ok, f + 1) for f in range(FC)] + [("turn7", L7.out, 1), ("lg", gidx, 1), ("dT", dT_ok, 1)]
        for q in range(NX):
            ringD += [(f"x{q}", sl_ok, q + 1), (f"y{q}", hm_ok, q + 1)]

        def make_ring(uses, first, size):
            place = {name: n for n, (name, _, _) in enumerate(uses)}

            def bank(name):
                return banks[first + place[name] % size]

            def free(pe, name, b):
                n = place[name]
                if n >= size:
                    _, done, count = uses[n - size]
                    pe.wait_ge(*done(b, count))
                else:
                    back = max(k for k in range(len(uses)) if k % size == n % size)
                    _, done, _ = uses[back]
                    pe.wait_ge(*done(b, 0))
            return bank, free

        bankC, freeC = make_ring(ringC, 0, 3)
        bankD, freeD = make_ring(ringD, 5, 2)
        SLOTS = M + 3

        def sweep(eng, step):
            step(0, None)
            step(1, 0)
            with eng.Fori(2, NB) as i:
                step(i, i - 1)
            step(None, NB - 1)

        def steps(attend, feed, begin=None):
            def step(c, d):
                if begin:
                    begin(c, d)
                for slot in range(SLOTS):
                    if c is not None:
                        attend(slot, c)
                    if d is not None:
                        feed(slot, d)
            return step

        XQ = {5: (0, 1), 6: (2, 3), 7: (4, 5), 8: (6, 7), 9: (8, 9)}

        with nc.Block() as block:
            @block.sync
            def _(sp):
                sp.dma_start(two_sb[:, :], two).then_inc(w_in, 16)

                def step(c, d):
                    if c is not None:
                        sp.wait_ge(*wo_ok(c, 0))
                        sp.dma_start(h3[:, :], h3_dram[c]).then_inc(h3_in.sem, 16)
                        sp.wait_ge(*kvb_ok(c, 0))
                        sp.dma_start(kvl[:, :], kv_dram[c]).then_inc(kv_in.sem, 16)
                    if d is not None:
                        sp.wait_ge(*x3_ok(d, 0))
                        sp.dma_start(x2[:, :, :].rearrange("p j d -> p (j d)"), x2_dram[d]).then_inc(x2_in.sem, 16)
                        sp.wait_ge(*fin(d, 0))
                        for k in range(2):
                            sp.dma_start(gab[:, k, :], gate_rows[2 + k, d].partition_broadcast(P))\
                              .then_inc(gab_in.sem, 16)
                        sp.wait_ge(*ob_ok(d, 1))
                        sp.dma_start(out_v[d], ob[:, :, :]).then_inc(res_out.sem, 16)

                sweep(sp, step)
                sp.wait_ge(*res_out(NB, 0))

            @block.scalar
            def _(act):
                act.wait_ge(w_in, 16)
                act.wait_ge(nmx_ok, 1)

                def attend(slot, c):
                    if slot == 0:
                        act.wait_ge(*kv_in(c, 16))
                        act.wait_ge(*kvb_ok(c, 0))
                        act.activation(sfac[:, :], kvl[:, PR * VW:], ACT.Exp, bias=nmx[:, 0:1]).then_inc(sf.sem, 1)
                        for s in range(2):
                            act.wait_ge(*vsps(c, s + 1))
                            act.activation(evs[:, s * T:(s + 1) * T], bankC(f"vs{s}")[:, :], ACT.Copy,
                                           scale=EPS_FEAT).then_inc(evs_ok.sem, 1)
                    m = slot
                    if m < M:
                        act.wait_ge(*qps(c, m + 1))
                        act.wait_ge(*qss(c, m - 1 if m >= 2 else 0))
                        act.activation(qsqb[:, m % 2, :], bankC(f"q{m}")[:, :], ACT.Square).then_inc(qsq.sem, 1)
                        act.wait_ge(*qu(c, m + 1))
                        act.activation(uq[:, m % 2, :], uq[:, m % 2, :], ACT.Exp).then_inc(qe.sem, 1)
                    m = slot - 1
                    if 0 <= m < M:
                        act.wait_ge(*qt(c, m + 1))
                        act.wait_ge(*num(c, m - 1 if m >= 2 else 0))
                        act.activation(qT[:, m % 2, :], bankC(f"t{m}")[:, :], ACT.Copy, bias=EPS_FEAT)\
                           .then_inc(qT_ok.sem, 1)
                    m = slot - 2
                    if 0 <= m < M:
                        act.wait_ge(*att(c, m + 1))
                        act.wait_ge(*wo_ok(c, m - 1 if m >= 2 else 0))
                        act.activation(aT[:, m % 2, :], bankC(f"a{m}")[:, :], ACT.Copy).then_inc(aT_ok.sem, 1)
                    if slot == SLOTS - 1:
                        act.wait_ge(*L5.turned(c, 1))
                        act.wait_ge(*w2ps(c, 0))
                        act.activation(o1T[:, :], bankC("turn5")[:, :], ACT.Identity, scale=g1, bias=be1)\
                           .then_inc(L5.out.sem, 1)

                def feed(slot, d):
                    if slot < 2:
                        for f in (2 * slot, 2 * slot + 1):
                            act.wait_ge(*w1ps(d, f + 1))
                            act.wait_ge(*he(d, f - 1 if f >= 2 else 0))
                            act.activation(vb[:, f % 2, :], bankD(f"w{f}")[:, :], ACT.Identity,
                                           bias=b1c[:, f:f + 1]).then_inc(vb_ok.sem, 1)
                            act.wait_ge(*em_ok(d, f + 1))
                            act.activation(ee[:, f % 2, :], ee[:, f % 2, :], ACT.Exp).then_inc(ee_ok.sem, 1)
                    elif slot == 4:
                        act.wait_ge(*L7.turned(d, 1))
                        act.wait_ge(*xps(d, 0))
                        act.wait_ge(*yps(d, 0))
                        act.activation(hT4[:, :], bankD("turn7")[:, :], ACT.Identity, scale=modc[:, 1, d, 3:4],
                                       bias=modc[:, 1, d, 2:3]).then_inc(L7.out.sem, 1)
                        act.wait_ge(*gd_ok(d, 1))
                        act.activation(gex[:, :], gd[:, :], ACT.Exp).then_inc(gex_ok.sem, 1)
                        act.wait_ge(*dtp(d, 1))
                        act.activation(dT[:, :], bankD("dT")[0:E1, :], ACT.Copy).then_inc(dT_ok.sem, 1)
                    for q in XQ.get(slot, ()):
                        act.wait_ge(*xps(d, q + 1))
                        act.wait_ge(*sl_ok(d, q - 1 if q >= 2 else 0))
                        act.activation(th[:, q % 2, :], bankD(f"x{q}")[:, :], ACT.Tanh, scale=0.5)\
                           .then_inc(th_ok.sem, 1)

                sweep(act, steps(attend, feed))

            @block.gpsimd
            def _(pool):
                pool.memset(kvb[:, :, :], 0.0).then_inc(init, 1)
                pool.memset(ksb[:, :, :], 0.0).then_inc(init, 1)
                pool.tensor_scalar(nmx[:, :], mxrun[:, :], -1.0, None, ALU.mult).then_inc(nmx_ok, 1)
                pool.wait_ge(w_in, 16)

                def attend(slot, c):
                    if slot == SLOTS - 1:
                        norm_pool(pool, L5, half, c, passed)

                def feed(slot, d):
                    if slot == 3:
                        pool.wait_ge(*gab_in(d, 32))
                        pool.wait_ge(*x3_ok(d, 0))
                        pool.tensor_tensor(gg[:, :], g2, gab[:, 0, :], ALU.mult)
                        pool.tensor_tensor(gbe[:, :], be2, gab[:, 0, :], ALU.mult).then_inc(gg_ok.sem, 1)
                        norm_pool(pool, L6, half, d, passed)
                        pool.wait_ge(*gg_ok(d, 1))
                        pool.wait_ge(*L6.xhat(d, 1))
                        pool.tensor_tensor(t6[:, :, :], L6.xh[:, :, :], mid(gg[:, :], J), ALU.mult).then_inc(t6a.sem, 1)
                        pool.wait_ge(*t6a(d, 1))
                        pool.tensor_tensor(t6[:, :, :], t6[:, :, :], mid(gbe[:, :], J), ALU.add).then_inc(t6b.sem, 1)
                        pool.wait_ge(*t6b(d, 1))
                        pool.wait_ge(*x2_in(d, 16))
                        pool.wait_ge(*ob_ok(d, 0))
                        pool.wait_ge(*L7.xhat(d, 0))
                        pool.tensor_tensor(x3[:, :, :], x2[:, :, :], t6[:, :, :], ALU.add).then_inc(x3_ok.sem, 1)
                    elif slot == 4:
                        norm_pool(pool, L7, half, d, passed)
                    elif slot == SLOTS - 1:
                        pool.wait_ge(*fin(d, 1))
                        pool.wait_ge(*res_out(d, 0))
                        pool.tensor_tensor(ob[:, :, :], x3[:, :, :], fo[:, :, :], ALU.add).then_inc(ob_ok.sem, 1)

                sweep(pool, steps(attend, feed))

            @block.tensor
            def _(pe):
                pe.wait_ge(w_in, 16)

                def attend(slot, c):
                    if slot == 0:
                        pe.wait_ge(*hsb(c, 1))
                        for s in range(2):
                            freeC(pe, f"vs{s}", c)
                            pe.matmul(bankC(f"vs{s}")[:, :], hsB[:, :], wv[:, s * T:(s + 1) * T],
                                      start=True, stop=True).then_inc(vsps.sem, 1)
                    m = slot
                    if m < M:
                        j, s = divmod(m, 2)
                        for name, w, done in (("q", wq, qps), ("d", pq[:, :], qd)):
                            freeC(pe, f"{name}{m}", c)
                            pe.matmul(bankC(f"{name}{m}")[:, :], h3[:, j * P:(j + 1) * P], w[:, s * T:(s + 1) * T],
                                      start=True, stop=True).then_inc(done.sem, 1)
                    m = slot - 1
                    if 0 <= m < M:
                        s = m % 2
                        freeC(pe, f"t{m}", c)
                        pe.wait_ge(*qe(c, m + 1))
                        for k in range(4):
                            last = pe.transpose(bankC(f"t{m}")[:, k * P:(k + 1) * P],
                                                uq[:, m % 2, k * P:(k + 1) * P], ident)
                        last.then_inc(qt.sem, 1)
                        freeC(pe, f"n{m}", c)
                        pe.wait_ge(*qT_ok(c, m + 1))
                        pe.wait_ge(*kvb_ok(c, 1))
                        pe.wait_ge(*rd_ok(c, m))
                        for k in range(4):
                            lhs = qT[:, m % 2, k * P:(k + 1) * P]
                            pe.matmul(bankC(f"n{m}")[:, k * P:(k + 1) * P], lhs, kvb[:, 4 * s + k, :],
                                      start=True, stop=True)
                            last = pe.matmul(banks[4][:, 2 * k:2 * k + 2], lhs, ksb[:, 4 * s + k, :],
                                             start=True, stop=True)
                        last.then_inc(num.sem, 1)
                    m = slot - 2
                    if 0 <= m < M:
                        j, s = divmod(m, 2)
                        freeC(pe, f"a{m}", c)
                        pe.wait_ge(*at_ok(c, m + 1))
                        for k in range(4):
                            last = pe.transpose(bankC(f"a{m}")[:, k * P:(k + 1) * P],
                                                at[:, m % 2, k * P:(k + 1) * P], ident)
                        last.then_inc(att.sem, 1)
                        if m == 0:
                            pe.wait_ge(*L5.xhat(c, 0))
                        dst = banks[3][:, j * D:(j + 1) * D]
                        if s == 0:
                            pe.matmul(dst, h3[:, j * P:(j + 1) * P], ident, start=True, stop=False)
                        pe.wait_ge(*aT_ok(c, m + 1))
                        for k in range(4):
                            last = pe.matmul(dst, aT[:, m % 2, k * P:(k + 1) * P], wo[:, 4 * s + k, :],
                                             start=False, stop=(s == 1 and k == 3))
                        last.then_inc(wo_ok.sem, 1)
                    if slot == SLOTS - 1:
                        freeC(pe, "turn5", c)
                        norm_pe(pe, L5, bankC("turn5"), ident, c)

                def feed(slot, d):
                    if slot < 2:
                        if slot == 0:
                            pe.wait_ge(*L5.out(d, 1))
                        for f in (2 * slot, 2 * slot + 1):
                            freeD(pe, f"w{f}", d)
                            pe.matmul(bankD(f"w{f}")[:, :], w1[:, f * P:(f + 1) * P], o1T[:, :],
                                      start=True, stop=True).then_inc(w1ps.sem, 1)
                    elif slot == 2:
                        pe.wait_ge(*fin(d, 0))
                        pe.matmul(banks[7][:, :], ones[0:1, :], b2r[0:1, :], start=True, stop=False,
                                  skip_group_check=True)
                        for j in range(J):
                            pe.matmul(banks[7][:, j * D:(j + 1) * D], o1T[:, j * P:(j + 1) * P], ident,
                                      start=False, stop=False, skip_group_check=True)
                        pe.wait_ge(*he(d, FC))
                        for j in range(J):
                            for f in range(FC):
                                last = pe.matmul(banks[7][:, j * D:(j + 1) * D], hE[:, f, j * P:(j + 1) * P],
                                                 w2[:, f, :], start=False, stop=(f == FC - 1),
                                                 skip_group_check=True)
                        last.then_inc(w2ps.sem, 1)
                    elif slot == 4:
                        freeD(pe, "turn7", d)
                        norm_pe(pe, L7, bankD("turn7"), ident, d)
                        freeD(pe, "lg", d)
                        pe.wait_ge(*L7.out(d, 1))
                        for j in range(J):
                            last = pe.matmul(bankD("lg")[:, j * E1:(j + 1) * E1], hT4[:, j * P:(j + 1) * P], gatew,
                                             start=True, stop=True)
                        last.then_inc(lg_ok.sem, 1)
                        freeD(pe, "dT", d)
                        pe.wait_ge(*disp_ok(d, 1))
                        for j in range(J):
                            last = pe.transpose(bankD("dT")[0:E1, j * P:(j + 1) * P], disp[:, j, :], ident)
                        last.then_inc(dtp.sem, 1)
                    for q in XQ.get(slot, ()):
                        if q < SC:
                            lx, ly, rhs = s1w[:, q * P:(q + 1) * P], s2w[:, q * P:(q + 1) * P], hT4[:, :]
                        else:
                            r = q - SC
                            lx, ly, rhs = mw1[:, r * P:(r + 1) * P], pick[0:E1, r, :], dT[:, :]
                            pe.wait_ge(*dT_ok(d, 1))
                        freeD(pe, f"x{q}", d)
                        pe.matmul(bankD(f"x{q}")[:, :], lx, hT4[:, :], start=True, stop=True).then_inc(xps.sem, 1)
                        freeD(pe, f"y{q}", d)
                        pe.matmul(bankD(f"y{q}")[:, :], ly, rhs, start=True, stop=True).then_inc(yps.sem, 1)
                    if slot == SLOTS - 1:
                        pe.wait_ge(*hm_ok(d, NX))
                        pe.wait_ge(*L6.xhat(d, 1))
                        for j in range(J):
                            for q in range(NX):
                                w = s3w[:, q, :] if q < SC else mw2[:, q - SC, :]
                                last = pe.matmul(banks[7][:, j * D:(j + 1) * D], hm[:, q, j * P:(j + 1) * P], w,
                                                 start=(q == 0), stop=(q == NX - 1))
                        last.then_inc(mo.sem, 1)

                sweep(pe, steps(attend, feed))

            @block.vector
            def _(dve):
                dve.wait_ge(w_in, 16)
                dve.wait_ge(init, 2)
                cC, cD = Chain(dve, chainC), Chain(dve, chainD)

                def attend(slot, c):
                    if slot == 0:
                        dve.wait_ge(*h3_in(c, 16))
                        cC.step(dve.tensor_reduce(hsum[:, :], h3[:, :], AX.X, ALU.add))
                        dve.wait_ge(*vsps(c, 0))
                        dve.tensor_scalar(hsB[:, :], ones[:, :], hsum[:, 0:1], None, ALU.mult).then_inc(hsb.sem, 1)
                    m = slot
                    if m < M:
                        dash = bankC(f"d{m}")[:, :].rearrange("p (h k) -> p h k", h=8)
                        dve.wait_ge(*qsq(c, m + 1))
                        dve.wait_ge(*qu(c, m))
                        dve.tensor_reduce(qs[:, :], qsqb[:, m % 2, :].rearrange("p (h k) -> p h k", h=8),
                                          AX.X, ALU.add).then_inc(qss.sem, 1)
                        dve.wait_ge(*qd(c, m + 1))
                        cC.step(dve.tensor_reduce(qm[:, :], dash, AX.X, ALU.max))
                        cC.step(dve.scalar_tensor_tensor(nb[:, :], qs[:, :], -DIAG, qm[:, :], ALU.mult, ALU.subtract))
                        dve.wait_ge(*qt(c, m - 1 if m >= 2 else 0))
                        dve.tensor_tensor(uq[:, m % 2, :].rearrange("p (h k) -> p h k", h=8), dash,
                                          inner(nb[:, :], DH), ALU.add).then_inc(qu.sem, 1)
                    if slot == 0:
                        dve.wait_ge(*sf(c, 1))
                        dve.wait_ge(*evs_ok(c, 2))
                        dve.wait_ge(*num(c, 0))
                        kvw = kvl[:, 0:PR * VW].rearrange("p (r v) -> p r v", r=PR)
                        ev = evs[:, :].rearrange("p (r v) -> p r v", r=PR)
                        for k in range(2):
                            r = slice(k * DH, (k + 1) * DH)
                            dve.scalar_tensor_tensor(kvb[r, :, r], kvw[r, :, r], sfac[r, 0:1], ev[r, :, r],
                                                     ALU.mult, ALU.add)
                            last = dve.tensor_scalar(ksb[r, :, k:k + 1], kvw[r, :, P:VW], sfac[r, 0:1],
                                                     T * EPS_FEAT, ALU.mult, ALU.add)
                        last.then_inc(kvb_ok.sem, 1)
                    m = slot - 1
                    if 0 <= m < M:
                        dve.wait_ge(*num(c, m + 1))
                        dve.wait_ge(*at_ok(c, m))
                        dve.reciprocal(rd[:, :], banks[4][:, 0:8]).then_inc(rd_ok.sem, 1)
                        dve.wait_ge(*rd_ok(c, m + 1))
                        dve.wait_ge(*att(c, m - 1 if m >= 2 else 0))
                        dve.tensor_tensor(at[:, m % 2, :].rearrange("p (h k) -> p h k", h=8),
                                          bankC(f"n{m}")[:, :].rearrange("p (h k) -> p h k", h=8),
                                          inner(rd[:, :], DH), ALU.mult).then_inc(at_ok.sem, 1)
                    if slot == SLOTS - 1:
                        dve.wait_ge(*wo_ok(c, M))
                        dve.wait_ge(*L5.turned(c, 0))
                        norm_dve(dve, L5, banks[3][:, :].rearrange("p (j d) -> p j d", j=J), c, passed)

                def feed(slot, d):
                    if slot < 2:
                        if slot == 0:
                            dve.wait_ge(*w2ps(d, 0))
                        for f in (2 * slot, 2 * slot + 1):
                            dve.wait_ge(*vb_ok(d, f + 1))
                            dve.wait_ge(*he(d, f - 1 if f >= 2 else 0))
                            dve.tensor_scalar(ee[:, f % 2, :], vb[:, f % 2, :], 0.0, None, ALU.min)\
                               .then_inc(em_ok.sem, 1)
                            dve.wait_ge(*ee_ok(d, f + 1))
                            dve.scalar_tensor_tensor(hE[:, f, :], ee[:, f % 2, :], -1.0, vb[:, f % 2, :],
                                                     ALU.add, ALU.max).then_inc(he.sem, 1)
                    elif slot == 3:
                        dve.wait_ge(*w2ps(d, 1))
                        dve.wait_ge(*t6a(d, 0))
                        norm_dve(dve, L6, banks[7][:, :].rearrange("p (j d) -> p j d", j=J), d, passed)
                    elif slot == 4:
                        dve.wait_ge(*x3_ok(d, 1))
                        dve.wait_ge(*L7.turned(d, 0))
                        norm_dve(dve, L7, x3, d, passed)
                        lg = bankD("lg")[:, 0:J * E1].rearrange("p (j e) -> p j e", j=J)
                        dve.wait_ge(*lg_ok(d, 1))
                        hold(dve, passed)
                        for j in range(J):
                            last = dve.max(m8[:, j, :], lg[:, j, :])
                        cD.step(last)
                        hold(dve, passed)
                        for j in range(J):
                            last = dve.max_index(idx[:, j, :], m8[:, j, :], lg[:, j, :])
                        last.then_inc(gidx.sem, 1)
                        dve.wait_ge(*gidx(d, 1))
                        dve.wait_ge(*gex_ok(d, 0))
                        dve.tensor_tensor(gd[:, :], m8[:, :, 1], m8[:, :, 0], ALU.subtract).then_inc(gd_ok.sem, 1)
                        for k, oh in enumerate((oh1, oh2)):
                            cD.step(dve.tensor_tensor(oh[:, :, :], mid(iota[:, 0:E1], J),
                                                      idx[:, :, k:k + 1].to_broadcast([P, J, E1]), ALU.is_equal))
                        dve.wait_ge(*gex_ok(d, 1))
                        cD.step(dve.tensor_scalar(gsum[:, :], gex[:, :], 1.0, None, ALU.add))
                        cD.step(dve.reciprocal(gw1[:, :], gsum[:, :]))
                        cD.step(dve.tensor_tensor(gw2[:, :], gex[:, :], gw1[:, :], ALU.mult))
                        cD.step(dve.tensor_tensor(oh1[:, :, :], oh1[:, :, :], inner(gw1[:, :], E1), ALU.mult))
                        cD.step(dve.tensor_tensor(oh2[:, :, :], oh2[:, :, :], inner(gw2[:, :], E1), ALU.mult))
                        dve.wait_ge(*dtp(d, 0))
                        dve.tensor_tensor(disp[:, :, :], oh1[:, :, :], oh2[:, :, :], ALU.add).then_inc(disp_ok.sem, 1)
                    for q in XQ.get(slot, ()):
                        dve.wait_ge(*th_ok(d, q + 1))
                        dve.wait_ge(*hm_ok(d, q - 1 if q >= 2 else 0))
                        dve.scalar_tensor_tensor(sl[:, q % 2, :], th[:, q % 2, :], 1.0, bankD(f"x{q}")[:, :],
                                                 ALU.add, ALU.mult).then_inc(sl_ok.sem, 1)
                        dve.wait_ge(*sl_ok(d, q + 1))
                        dve.wait_ge(*yps(d, q + 1))
                        if q == 0:
                            dve.wait_ge(*mo(d, 0))
                        dve.scalar_tensor_tensor(hm[:, q, :], sl[:, q % 2, :], 0.5, bankD(f"y{q}")[:, :],
                                                 ALU.mult, ALU.mult).then_inc(hm_ok.sem, 1)
                    if slot == SLOTS - 1:
                        dve.wait_ge(*mo(d, 1))
                        dve.wait_ge(*ob_ok(d, 0))
                        dve.tensor_tensor(fo[:, :, :], banks[7][:, :].rearrange("p (j d) -> p j d", j=J),
                                          mid(gab[:, 1, :], J), ALU.mult).then_inc(fin.sem, 1)

                def begin(c, d):
                    cC.begin(c)
                    cD.begin(d)

                sweep(dve, steps(attend, feed, begin))


def kernel(**inputs):
    import ml_dtypes
    import numpy as np
    import concourse.bacc as _bacc
    from concourse.bass_utils import run_bass_kernel_spmd as _run

    A = {k: np.asarray(v) for k, v in inputs.items()}

    def pack(where, width, parts):
        w = np.zeros((P, width), np.float32)
        for name, (first, n) in where.items():
            a = parts[name]
            r, a = a if isinstance(a, tuple) else (0, a)
            a = a.reshape(a.shape[0], -1)
            w[r:r + a.shape[0], first:first + a.shape[1]] = a
        return w

    def chunks(a, n):
        return a.reshape(n, P, -1).transpose(1, 0, 2)

    def blocks(a, n):
        w = np.zeros((n * a.shape[0], n * a.shape[1]), np.float32)
        for k in range(n):
            w[k * a.shape[0]:(k + 1) * a.shape[0], k * a.shape[1]:(k + 1) * a.shape[1]] = a
        return w

    ident = np.eye(P, dtype=np.float32)
    iota = np.tile(np.arange(E1, dtype=np.float32), (P, 1))
    keep = pack(KEEP, KEEP_N, {"ident": ident, "iota": iota, "wv": A["L1_attn_Wv"]})

    once = pack(ONCE, ONCE_N, {
        "wmod0": A["L0_wmod"], "wmod1": A["L1_wmod"], "c0": A["L0_c"].T, "c1": A["L1_c"].T,
        "wkT": chunks(A["L1_attn_Wk"].reshape(D, HD).T, PR), "wqT": chunks(A["L1_attn_Wq"].reshape(D, HD).T, PR),
        "proj": blocks(A["L1_attn_proj"].T, 2)})

    xp = A["L0_attn_x_proj_w"]
    xw = np.zeros((DI, P), np.float32)
    for k in range(3):
        xw[:, 32 * k:32 * k + 32] = xp[:, RK:]
    xw[:, 96:96 + RK] = xp[:, :RK]
    b2 = np.zeros((P, J, D), np.float32)
    for j in range(J):
        b2[32 * j:32 * j + E0, j, :] = A["L0_ffn_b2"]
    one = pack(ONE, ONE_N, {
        "inw": A["L0_attn_in_proj_w"],
        "convw": chunks(A["L0_attn_conv_w"][:, 0, :].T, G), "convb": chunks(A["L0_attn_conv_b"], G),
        "xw": chunks(xw, G), "dtw": (96, A["L0_attn_dt_proj_w"]), "dtb": chunks(A["L0_attn_dt_proj_b"], G),
        "alog": chunks(A["L0_attn_A_log"], G), "dskip": chunks(A["L0_attn_D"], G),
        "outw": chunks(A["L0_attn_out_proj_w"], G), "gate": A["L0_ffn_gate_w"].T,
        "w1": A["L0_ffn_w1"].transpose(1, 0, 2), "b1": A["L0_ffn_b1"].reshape(E0 * FC, P).T,
        "w2": A["L0_ffn_w2"].reshape(E0, FC, P, D).transpose(2, 0, 1, 3), "b2": b2, "wk": A["L1_attn_Wk"]})

    pick = np.zeros((E1, MC, P), np.float32)
    for r in range(MC):
        for k in range(2):
            pick[2 * r + k, r, k * HE:(k + 1) * HE] = 1.0
    mw2 = A["L1_ffn_w2"].transpose(0, 2, 1).reshape(E1 * HE, D)
    two = pack(TWO, TWO_N, {
        "wq": A["L1_attn_Wq"], "wo": chunks(A["L1_attn_Wo"].reshape(HD, D), PR), "w1": A["L1_attn_W1"],
        "b1": A["L1_attn_b1"].reshape(FC, P).T, "w2": chunks(A["L1_attn_W2"], FC),
        "b2": np.tile(A["L1_attn_b2"], J)[None], "g1": A["L1_attn_ln1_g"][:, None],
        "be1": A["L1_attn_ln1_b"][:, None], "g2": np.tile(A["L1_attn_ln2_g"], (P, 1)),
        "be2": np.tile(A["L1_attn_ln2_b"], (P, 1)), "gate": A["L1_ffn_gate_w"].T,
        "mw1": A["L1_ffn_w1"].reshape(E1 * HE, D).T, "mw2": chunks(mw2, MC),
        "s1": A["L1_ffn_sfc1"].T, "s2": A["L1_ffn_sfc2"].T, "s3": chunks(A["L1_ffn_sfc3"].T, SC), "pick": pick})

    pick16 = np.zeros((3 * 2 * NS, 2 * NS, P), ml_dtypes.bfloat16)
    for n in range(2 * NS):
        pick16[n::2 * NS, n, :] = 1.0

    arrays = {"x": np.ascontiguousarray(A["L0_attn_x"]), "keep": keep, "once": once, "one": one, "two": two,
              "pick16": pick16}
    nc = _bacc.Bacc("TRN2", target_bir_lowering=False, num_devices=1)
    args = [nc.dram_tensor(f"in_{n}", a.shape, mybir.dt.from_np(a.dtype), kind="ExternalInput").ap()
            for n, a in arrays.items()]
    out = nc.dram_tensor("out_0", (NB, T, D), F32, kind="ExternalOutput").ap()
    adaln_depth2(nc, *args, out)
    r = _run(nc, [{f"in_{n}": a for n, a in arrays.items()}], core_ids=[0])
    return r.results[0]["out_0"]
```

```python
from contextlib import ExitStack

import concourse.bass as bass
from concourse import mybir

F32 = mybir.dt.float32
BF16 = mybir.dt.bfloat16
U32 = mybir.dt.uint32
ALU = mybir.AluOpType
ACT = mybir.ActivationFunctionType
AX = mybir.AxisListType
RMAX = bass.bass_isa.ReduceOp.max

P = 128
NB, T, D = 16, 512, 128
J = T // P
DI = 256
G = DI // P
NS = 16
RK = DI // 16
TAPS = 4
PAD = TAPS - 1
E0, FF = 8, 512
FC = FF // P
H, DH = 16, 64
HD = H * DH
PR = HD // P
VW = P + 1
E1, HE = 16, 64
MC = E1 * HE // P
SC = 256 // P
EPS_MOD = 1e-5
EPS_ENC = 1e-6
EPS_FEAT = 1e-6
DN = float(DH) ** -0.25
DIAG = DN * DN / 2.0
BIG = 3.0e38


def columns(parts):
    at, where = 0, {}
    for name, n in parts:
        where[name] = (at, n)
        at += n
    return where, at


KEEP, KEEP_N = columns([("ident", P), ("iota", E1), ("wv", HD)])
ONCE, ONCE_N = columns([("wmod0", 6 * D), ("wmod1", 6 * D), ("c0", NB), ("c1", NB),
                        ("wkT", HD), ("wqT", HD), ("proj", P)])
ONE, ONE_N = columns([("inw", 2 * DI), ("convw", G * TAPS), ("convb", G), ("xw", G * P), ("dtw", DI),
                      ("dtb", G), ("alog", G * NS), ("dskip", G), ("outw", G * D), ("gate", E0),
                      ("w1", E0 * FF), ("b1", E0 * FC), ("w2", E0 * FF), ("b2", J * D), ("wk", HD)])
TWO, TWO_N = columns([("wq", HD), ("wo", HD), ("w1", FF), ("b1", FC), ("w2", FF), ("b2", T),
                      ("g1", 1), ("be1", 1), ("g2", D), ("be2", D), ("gate", E1), ("mw1", E1 * HE),
                      ("mw2", E1 * HE), ("s1", SC * P), ("s2", SC * P), ("s3", SC * D), ("pick", MC * P)])


class Signal:

    def __init__(self, sem, per):
        self.sem, self.per = sem, per

    def __call__(self, batch, n):
        return self.sem, batch * self.per + n


class Chain:

    def __init__(self, eng, signal):
        self.eng, self.step_of, self.n, self.batch = eng, signal, 0, None

    def begin(self, batch):
        assert self.n in (0, self.step_of.per), (self.n, self.step_of.per)
        self.n, self.batch = 0, batch

    def step(self, ins):
        self.n += 1
        ins.then_inc(self.step_of.sem, 1)
        self.eng.wait_ge(*self.step_of(self.batch, self.n))


class Norm:

    def __init__(self, sb, sig, name, eps):
        self.eps = eps
        self.st = sb(name + "_st", [P, J, 6])
        self.mv = sb(name + "_mv", [P, J, 2])
        self.ve = sb(name + "_ve", [P, J])
        self.rs = sb(name + "_rs", [P, J])
        self.xh = sb(name + "_xh", [P, J, D])
        self.sums, self.stats, self.veps, self.rstd, self.xhat, self.turned, self.out = (
            sig(name + "_" + n, 1) for n in ("sums", "stats", "veps", "rstd", "xhat", "turned", "out"))


def hold(eng, passed):
    eng.sem_inc(passed, 1)


def norm_dve(dve, ln, src, it, passed):
    norm_stats(dve, ln, src, it, passed)
    norm_apply(dve, ln, src, it)


def norm_stats(dve, ln, src, it, passed):
    dve.wait_ge(*ln.xhat(it, 0))
    for j in range(J):
        last = dve.bn_stats(ln.st[:, j, :], src[:, j, :])
    last.then_inc(ln.sums.sem, 1)
    dve.wait_ge(*ln.sums(it, 1))
    hold(dve, passed)
    for j in range(J):
        last = dve.bn_aggr(ln.mv[:, j, :], ln.st[:, j, :])
    last.then_inc(ln.stats.sem, 1)


def norm_apply(dve, ln, src, it):
    dve.wait_ge(*ln.rstd(it, 1))
    for j in range(J):
        last = dve.tensor_scalar(ln.xh[:, j, :], src[:, j, :], ln.mv[:, j, 0:1], ln.rs[:, j:j + 1],
                                 ALU.subtract, ALU.mult)
    last.then_inc(ln.xhat.sem, 1)


def norm_pool(pool, ln, half, it, passed):
    pool.wait_ge(*ln.stats(it, 1))
    hold(pool, passed)
    pool.tensor_scalar(ln.ve[:, :], ln.mv[:, :, 1], ln.eps, None, ALU.add).then_inc(ln.veps.sem, 1)
    pool.wait_ge(*ln.veps(it, 1))
    pool.tensor_tensor(ln.rs[:, :], ln.ve[:, :], half[:, 0:J], ALU.pow).then_inc(ln.rstd.sem, 1)


def norm_pe(pe, ln, ps, ident, it):
    pe.wait_ge(*ln.xhat(it, 1))
    for j in range(J):
        last = pe.transpose(ps[:, j * P:(j + 1) * P], ln.xh[:, j, :], ident)
    last.then_inc(ln.turned.sem, 1)


def mid(ap, n):
    return ap.unsqueeze(1).to_broadcast([ap.shape[0], n, ap.shape[1]])


def inner(ap, m):
    return ap.unsqueeze(2).to_broadcast([ap.shape[0], ap.shape[1], m])


def adaln_depth2(nc, x, keep, once, one, two, pick16, out):
    ctx = ExitStack()
    with ctx:
        held = []

        def sem(name):
            held.append(nc.alloc_semaphore(name=name))
            return held[-1]

        def end_part():
            nc.clear_and_free_semaphores(held)
            held.clear()
            nc.all_engine_barrier()

        def sig(name, per):
            return Signal(sem(name), per)

        def sbuf(stack):
            def sb(name, shape, dt=F32):
                return stack.enter_context(nc.sbuf_tensor(name, shape, dt))
            return sb

        x_v = x.rearrange("b (j p) d -> b p j d", p=P)
        out_v = out.rearrange("b (j p) d -> b p j d", p=P)
        gate_rows = nc.dram_tensor("gate_rows", (4, NB, D), F32, kind="Internal").ap()
        x2_dram = nc.dram_tensor("x2_dram", (NB, P, J * D), F32, kind="Internal").ap()
        h3_dram = nc.dram_tensor("h3_dram", (NB, P, T), F32, kind="Internal").ap()
        kv_dram = nc.dram_tensor("kv_dram", (NB, P, PR * VW + 1), F32, kind="Internal").ap()

        kept = sbuf(ctx)
        keep_sb = kept("keep_sb", [P, KEEP_N])
        ident, iota, wv = (keep_sb[:, KEEP[n][0]:KEEP[n][0] + KEEP[n][1]] for n in ("ident", "iota", "wv"))
        modc = kept("modc", [P, 2, NB, 4])
        pk = kept("pk", [P, HD])
        pq = kept("pq", [P, HD])
        ones = kept("ones", [P, P])
        half = kept("half", [P, 8])
        mxrun = kept("mxrun", [P, 1])
        nmx = kept("nmx", [P, 1])
        banks = [ctx.enter_context(nc.psum_tensor(f"bank{n}", [P, T], F32)) for n in range(8)]

        with ExitStack() as part:
            sb = sbuf(part)
            once_sb = sb("once_sb", [P, ONCE_N])

            def W(name, a=0, b=None):
                at, n = ONCE[name]
                return once_sb[:, at + a:at + (n if b is None else b)]

            sc = sb("sc", [P, 2 * NB])
            gr_s = sb("gr_s", [NB, T])
            gr_m = sb("gr_m", [NB, T])
            gr = sb("gr", [NB, T])
            w_in, c_ready, fold, mods, gates, chain_s, gr_ready, gr_out, done_s, setup_dve = (
                sem(n) for n in ("setup_in", "c_ready", "folded", "mods", "gates", "gate_chain", "gate_rows_ready",
                                 "gate_rows_out", "folds_kept", "setup_dve"))
            with nc.Block() as block:
                @block.sync
                def _(sp):
                    sp.dma_start(once_sb[:, :], once).then_inc(w_in, 16)
                    sp.dma_start(keep_sb[:, :], keep).then_inc(w_in, 16)
                    sp.wait_ge(gr_ready, 1)
                    sp.dma_start(gate_rows.rearrange("r b d -> b r d"),
                                 gr[:, :].rearrange("b (r d) -> b r d", r=4)).then_inc(gr_out, 16)
                    sp.wait_ge(gr_out, 16)

                @block.gpsimd
                def _(pool):
                    pool.memset(ones[:, :], 1.0)
                    pool.memset(half[:, :], -0.5)
                    pool.memset(mxrun[:, :], -BIG)

                @block.scalar
                def _(act):
                    act.wait_ge(w_in, 32)
                    act.activation(sc[:, :], W("c0", 0, 2 * NB), ACT.Silu).then_inc(c_ready, 1)
                    for n, dst in enumerate((pk, pk, pq, pq)):
                        act.wait_ge(fold, n + 1)
                        o = (n % 2) * T
                        act.activation(dst[:, o:o + T], banks[n][:, :], ACT.Copy, scale=DN).then_inc(done_s, 1)

                @block.tensor
                def _(pe):
                    pe.wait_ge(w_in, 32)
                    for n, src in enumerate(("wkT", "wkT", "wqT", "wqT")):
                        for k in range(PR // 2):
                            pr = (n % 2) * (PR // 2) + k
                            last = pe.matmul(banks[n][:, k * P:(k + 1) * P], W(src, pr * P, (pr + 1) * P),
                                             W("proj"), start=True, stop=True)
                        last.then_inc(fold, 1)
                    pe.wait_ge(c_ready, 1)
                    for l in range(2):
                        for k, col in enumerate((0, 1, 3, 4)):
                            at = (l * 4 + k) * NB
                            last = pe.matmul(banks[6][:, at:at + NB], W(f"wmod{l}", col * D, (col + 1) * D),
                                             sc[:, l * NB:(l + 1) * NB], start=True, stop=True)
                    last.then_inc(mods, 1)
                    for l in range(2):
                        for k, col in enumerate((2, 5)):
                            at = (l * 2 + k) * D
                            last = pe.matmul(banks[7][0:NB, at:at + D], sc[:, l * NB:(l + 1) * NB],
                                             W(f"wmod{l}", col * D, (col + 1) * D), start=True, stop=True)
                    last.then_inc(gates, 1)

                @block.vector
                def _(dve):
                    dve.wait_ge(mods, 1)
                    ps = banks[6][:, 0:2 * 4 * NB].rearrange("p (l k b) -> p l b k", l=2, k=4)
                    for l in range(2):
                        for k in range(4):
                            dve.tensor_scalar(modc[:, l, :, k], ps[:, l, :, k], float(k % 2), None, ALU.add)\
                               .then_inc(setup_dve, 1)
                    dve.wait_ge(gates, 1)
                    gp = banks[7][0:NB, :]
                    dve.tensor_scalar(gr_s[:, :], gp, 0.0, 2.0, ALU.is_ge, ALU.mult).then_inc(chain_s, 1)
                    dve.tensor_scalar(gr_m[:, :], gp, -1.0, None, ALU.mult).then_inc(chain_s, 1)
                    dve.wait_ge(chain_s, 2)
                    dve.tensor_tensor(gr_m[:, :], gr_m[:, :], gp, ALU.max).then_inc(chain_s, 1)
                    dve.wait_ge(chain_s, 3)
                    dve.tensor_scalar(gr_m[:, :], gr_m[:, :], 0.25, None, ALU.max).then_inc(chain_s, 1)
                    dve.wait_ge(chain_s, 4)
                    dve.scalar_tensor_tensor(gr[:, :], gr_s[:, :], -1.0, gr_m[:, :], ALU.add, ALU.mult)\
                       .then_inc(gr_ready, 1)

            end_part()

        with ExitStack() as part:
            sb = sbuf(part)
            one_sb = sb("one_sb", [P, ONE_N])

            def V1(name):
                at, n = ONE[name]
                return one_sb[:, at:at + n]

            inw, convb, dtb, dskip, alog, gatew, b1c = (V1(n) for n in ("inw", "convb", "dtb", "dskip", "alog",
                                                                       "gate", "b1"))
            convw = V1("convw").rearrange("p (g k) -> p g k", g=G)
            xw = V1("xw").rearrange("p (g m) -> p g m", g=G)
            dtw = V1("dtw")
            outw = V1("outw").rearrange("p (g d) -> p g d", g=G)
            w1 = V1("w1").rearrange("p (e f) -> p e f", e=E0)
            w2 = V1("w2").rearrange("p (e f d) -> p e f d", e=E0, f=FC)
            b2 = V1("b2")
            wk = V1("wk")
            pick_sb = sb("pick_sb", [3 * 2 * NS, 2 * NS, P], BF16)
            aneg = sb("aneg", [P, G, NS])
            xs = sb("xs", [P, J, D])
            ga = sb("ga", [P, D])
            hT = sb("hT", [P, T])
            xpad = sb("xpad", [P, G, PAD + T])
            cv = sb("cv", [P, G, T])
            ax = cv
            zs = sb("zs", [P, G, T])
            xc = sb("xc", [P, G, T])
            S = sb("S", [P, T], BF16)
            R = sb("R", [P, T])
            dtr = R
            Rb = sb("Rb", [P, T], BF16)
            dt = sb("dt", [P, G, T])
            dtx = sb("dtx", [P, G, T])
            acc = sb("acc", [P, G, T])
            dec = sb("dec", [P, 2, G, T])
            u = sb("u", [P, G, T])
            yz = u
            h = sb("h", [P, G, T])
            zz = sb("zz", [P, 2, G, T])
            ao = sb("ao", [P, J, D])
            x1 = sb("x1", [P, J, D])
            gb = sb("gb", [P, D])
            hT2 = sb("hT2", [P, T])
            m8 = sb("m8", [P, J, 8])
            idx = sb("idx", [P, J, 8], U32)
            oh = sb("oh", [P, J, E0])
            lm = sb("lm", [P, J, E0])
            ex = sb("ex", [P, J, E0])
            esum = sb("esum", [P, J])
            erec = sb("erec", [P, J])
            gp = sb("gp", [P, J, 32])
            gT = sb("gT", [P, P])
            hid = sb("hid", [P, 2, FC, T])
            prod = sb("prod", [P, 2, J, D])
            facc = sb("facc", [P, J, D])
            x2 = sb("x2", [P, J, D])
            hT3 = sb("hT3", [P, T])
            sq = sb("sq", [P, 2, T])
            ssq = sb("ssq", [P, 2 * J, 8])
            mxs = sb("mxs", [P, 2 * J])
            bmx = sb("bmx", [P, 1])
            cb = sb("cb", [P, 1])
            ncb = sb("ncb", [P, 1])
            Ek = sb("Ek", [P, J, HD])
            V = sb("V", [P, J, PR, VW])
            kvs = sb("kvs", [P, PR * VW + 1])

            w_in, a_exp, a_neg, init, passed = (sem(n) for n in ("w1_in", "a_exp", "a_neg", "init1", "passed1"))
            x_in, ga_in, gb_in, x2_out, h3_out, kv_out = (
                sig(n, 16) for n in ("x_in", "ga_in", "gb_in", "x2_out", "h3_out", "kv_out"))
            L1, L2, L3 = (Norm(sb, sig, n, EPS_MOD) for n in ("n1", "n2", "n3"))
            (in_done, xraw, zsilu, conv, xc_ok, xdbl, dtr_ok, s_hi, s_mid, s_rem, s_remb, s_lo, dtps, dtabs, dtexp,
             dtln, dtmax, dt_ok, dtx_ok, acc0, bb, cbc, dec_ok, u_ok, scan, z_ok, accum, yz_ok, oproj, ao_ok,
             x1_ok, chainA) = (sig(n, p) for n, p in (
                 ("in_done", 4), ("xraw", 2), ("zsilu", 2), ("conv", 2), ("xc_ok", 1), ("xdbl", 1), ("dtr_ok", 1),
                 ("s_hi", 1), ("s_mid", 1), ("s_rem", 1), ("s_remb", 1), ("s_lo", 1), ("dtps", 2), ("dtabs", 2),
                 ("dtexp", 1), ("dtln", 1), ("dtmax", 2), ("dt_ok", 1), ("dtx_ok", 1), ("acc0", 1), ("bb", NS),
                 ("cbc", NS), ("dec_ok", 2 * NS), ("u_ok", NS), ("scan", 2 * NS), ("z_ok", NS), ("accum", NS),
                 ("yz_ok", 1), ("oproj", 1), ("ao_ok", 1), ("x1_ok", 1), ("chainA", G * (TAPS - 1))))
            (logits, lshift, lexp, gw, gturn, gT_ok, b2ps, facc0, up, hid_ok, down, prod_ok, fadd, x2m, x2_ok,
             kps, dps, vps, sq_ok, ssum, ush, vc, bmx_ok, call, ncb_ok, mxr, kvc, kf, kv, kvs_ok, chainB) = (
                sig(n, p) for n, p in (
                    ("logits", 1), ("lshift", 1), ("lexp", 1), ("gw", 1), ("gturn", 1), ("gT_ok", 1), ("b2ps", 1),
                    ("facc0", 1), ("up", E0 * FC), ("hid_ok", E0 * FC), ("down", E0), ("prod_ok", E0), ("fadd", E0),
                    ("x2m", 1), ("x2_ok", 1), ("kps", 2 * J), ("dps", 2 * J), ("vps", 2 * J), ("sq_ok", 2 * J),
                    ("ssum", 2 * J), ("ush", 2 * J), ("vc", 2 * J), ("bmx_ok", 1), ("call", 1), ("ncb_ok", 1),
                    ("mxr", 1), ("kvc", 1), ("kf", J), ("kv", 1), ("kvs_ok", 3), ("chainB", 5 + 2 * J)))

            ring = [("turn2", L2.out, 1), ("logits", lshift, 1), ("up0", hid_ok, 1), ("up1", hid_ok, 2),
                    ("gates", gT_ok, 1)]
            ring += [(f"up{n}", hid_ok, n + 1) for n in range(2, E0 * FC)]
            ring += [("turn3", L3.out, 1)]
            for m in range(2 * J):
                ring += [(f"k{m}", sq_ok, m + 1), (f"d{m}", ush, m + 1), (f"v{m}", vc, m + 1)]
            RN = 3
            assert len(ring) % RN == 0
            use = {name: n for n, (name, _, _) in enumerate(ring)}

            def ring1(name):
                return banks[2 + use[name] % RN]

            def ring1_free(pe, name, b):
                n = use[name] - RN
                if n >= 0:
                    pe.wait_ge(*ring[n][1](b, ring[n][2]))
                else:
                    pe.wait_ge(*ring[n][1](b, 0))

            SLOTS = 4 + NS + 1

            HALVES = {1: (0,), 2: (1, 2), 3: (3, 4)}
            HALVES.update({s: (s + 1,) for s in range(4, 15)})
            PROD_SLOT = {}
            for s, hs in HALVES.items():
                for q in hs:
                    if q % 2:
                        PROD_SLOT[s + 1] = q // 2

            def sweep(eng, step):
                step(0, None)
                step(1, 0)
                with eng.Fori(2, NB) as i:
                    step(i, i - 1)
                step(None, NB - 1)

            with nc.Block() as block:
                @block.sync
                def _(sp):
                    sp.dma_start(one_sb[:, :], one).then_inc(w_in, 16)
                    sp.dma_start(pick_sb[:, :, :], pick16).then_inc(w_in, 16)

                    def step(a, b):
                        if a is not None:
                            sp.wait_ge(*x1_ok(a, 0))
                            sp.dma_start(xs[:, :, :], x_v[a]).then_inc(x_in.sem, 16)
                            sp.dma_start(ga[:, :], gate_rows[0, a].partition_broadcast(P)).then_inc(ga_in.sem, 16)
                        if b is not None:
                            sp.wait_ge(*x2_ok(b, 0))
                            sp.dma_start(gb[:, :], gate_rows[1, b].partition_broadcast(P)).then_inc(gb_in.sem, 16)
                            sp.wait_ge(*x2_ok(b, 1))
                            sp.dma_start(x2_dram[b], x2[:, :, :].rearrange("p j d -> p (j d)"))\
                              .then_inc(x2_out.sem, 16)
                            sp.wait_ge(*L3.out(b, 1))
                            sp.dma_start(h3_dram[b], hT3[:, :]).then_inc(h3_out.sem, 16)

                    sweep(sp, step)
                    sp.wait_ge(*x2_out(NB, 0))
                    sp.wait_ge(*h3_out(NB, 0))
                    sp.wait_ge(*kv_out(NB, 0))

                @block.scalar
                def _(act):
                    act.wait_ge(w_in, 32)
                    act.activation(aneg[:, :, :].rearrange("p g n -> p (g n)"), alog, ACT.Exp).then_inc(a_exp, 1)
                    act.wait_ge(a_neg, 1)
                    act.wait_ge(init, 4)

                    def mamba(slot, a):
                        if slot == 0:
                            act.wait_ge(*L1.turned(a, 1))
                            act.wait_ge(*in_done(a, 0))
                            act.activation(hT[:, :], banks[0][:, :], ACT.Identity, scale=modc[:, 0, a, 1:2],
                                           bias=modc[:, 0, a, 0:1]).then_inc(L1.out.sem, 1)
                        elif slot == 1:
                            for g in range(G):
                                act.wait_ge(*in_done(a, g + 1))
                                act.wait_ge(*conv(a, 0))
                                act.activation(xpad[:, g, PAD:], banks[g][:, :], ACT.Copy).then_inc(xraw.sem, 1)
                            for g in range(G):
                                act.wait_ge(*in_done(a, G + g + 1))
                                act.wait_ge(*yz_ok(a, 0))
                                act.activation(zs[:, g, :], banks[g][:, :], ACT.Silu).then_inc(zsilu.sem, 1)
                            act.wait_ge(*conv(a, G))
                            act.wait_ge(*acc0(a, 0))
                            act.wait_ge(*dtx_ok(a, 0))
                            act.activation(xc[:, :, :], cv[:, :, :], ACT.Silu).then_inc(xc_ok.sem, 1)
                        elif slot == 2:
                            act.wait_ge(*xdbl(a, 1))
                            act.wait_ge(*dtps(a, 0))
                            act.activation(dtr[96:96 + RK, :], banks[0][96:96 + RK, :], ACT.Copy)\
                               .then_inc(dtr_ok.sem, 1)
                            act.wait_ge(*cbc(a, 0))
                            act.activation(S[0:96, :], banks[0][0:96, :], ACT.Copy).then_inc(s_hi.sem, 1)
                            act.wait_ge(*s_rem(a, 1))
                            act.activation(Rb[64:96, :], R[64:96, :], ACT.Copy).then_inc(s_remb.sem, 1)
                        elif slot == 3:
                            for g in range(G):
                                act.wait_ge(*dtps(a, g + 1))
                                act.wait_ge(*xc_ok(a, 1))
                                act.activation(ax[:, g, :], banks[1 - g][:, :], ACT.Abs, bias=dtb[:, g:g + 1])\
                                   .then_inc(dtabs.sem, 1)
                            act.wait_ge(*dtabs(a, G))
                            act.activation(ax[:, :, :], ax[:, :, :], ACT.Exp, scale=-1.0).then_inc(dtexp.sem, 1)
                            act.wait_ge(*dtexp(a, 1))
                            act.activation(ax[:, :, :], ax[:, :, :], ACT.Ln, bias=1.0).then_inc(dtln.sem, 1)
                            act.wait_ge(*yz_ok(a, 0))
                            for g in range(G):
                                last = act.activation(acc[:, g, :], xc[:, g, :], ACT.Copy, scale=dskip[:, g:g + 1])
                            last.then_inc(acc0.sem, 1)
                        elif slot < 4 + NS:
                            n = slot - 4
                            if n == 0:
                                act.wait_ge(*dt_ok(a, 1))
                            act.wait_ge(*scan(a, G * (n - 1) if n >= 2 else 0))
                            for g in range(G):
                                act.activation(dec[:, n % 2, g, :], dt[:, g, :], ACT.Exp,
                                               scale=aneg[:, g, n:n + 1]).then_inc(dec_ok.sem, 1)

                    def relus(b, first, last):
                        for n in range(first, last):
                            e, f = divmod(n, FC)
                            act.wait_ge(*up(b, n + 1))
                            act.wait_ge(*down(b, e - 1 if e >= 2 else 0))
                            act.activation(hid[:, e % 2, f, :], banks[2 + use[f"up{n}"] % RN][:, :], ACT.Relu,
                                           bias=b1c[:, n:n + 1]).then_inc(hid_ok.sem, 1)

                    def key_tile(b, m):
                        j, s = divmod(m, 2)
                        act.wait_ge(*kps(b, m + 1))
                        act.wait_ge(*ssum(b, m - 1 if m >= 2 else 0))
                        act.activation(sq[:, m % 2, :], ring1(f"k{m}")[:, :], ACT.Square).then_inc(sq_ok.sem, 1)
                        act.wait_ge(*vps(b, m + 1))
                        act.wait_ge(*kv(b, 0))
                        act.activation(V[:, j, 4 * s:4 * s + 4, 0:P],
                                       ring1(f"v{m}")[:, :].rearrange("p (r d) -> p r d", r=4),
                                       ACT.Copy).then_inc(vc.sem, 1)

                    def experts(slot, b):
                        if slot == 0:
                            act.wait_ge(*L2.turned(b, 1))
                            act.wait_ge(*up(b, 0))
                            act.activation(hT2[:, :], ring1("turn2")[:, :], ACT.Identity, scale=modc[:, 0, b, 3:4],
                                           bias=modc[:, 0, b, 2:3]).then_inc(L2.out.sem, 1)
                        elif slot == 1:
                            act.wait_ge(*lshift(b, 1))
                            act.activation(ex[:, :, :], lm[:, :, :], ACT.Exp).then_inc(lexp.sem, 1)
                            relus(b, 0, 2)
                        elif slot == 2:
                            act.wait_ge(*gturn(b, 1))
                            act.wait_ge(*b2ps(b, 0))
                            act.activation(gT[:, :], ring1("gates")[:, 0:P], ACT.Copy).then_inc(gT_ok.sem, 1)
                            relus(b, 2, 6)
                        elif slot == 3:
                            relus(b, 6, 10)
                        elif slot <= 14:
                            relus(b, 2 * (slot + 1), 2 * (slot + 1) + 2)
                        elif slot == 16:
                            act.wait_ge(*L3.turned(b, 1))
                            act.wait_ge(*vps(b, 0))
                            act.wait_ge(*h3_out(b, 0))
                            act.activation(hT3[:, :], ring1("turn3")[:, :], ACT.Identity, scale=modc[:, 1, b, 1:2],
                                           bias=modc[:, 1, b, 0:1]).then_inc(L3.out.sem, 1)
                        elif slot >= 17:
                            key_tile(b, 2 * (slot - 17))
                            key_tile(b, 2 * (slot - 17) + 1)
                        if slot == SLOTS - 1:
                            act.wait_ge(*ncb_ok(b, 1))
                            act.wait_ge(*ush(b, 2 * J))
                            for j in range(J):
                                act.activation(Ek[:, j, :], Ek[:, j, :], ACT.Exp, bias=ncb[:, 0:1]).then_inc(kf.sem, 1)
                            act.wait_ge(*kv(b, 1))
                            act.wait_ge(*kv_out(b, 0))
                            for n, (first, count) in enumerate(((0, 3), (3, 3), (6, 2))):
                                act.activation(kvs[:, first * VW:(first + count) * VW],
                                               banks[5 + n][:, 0:count * VW], ACT.Copy).then_inc(kvs_ok.sem, 1)
                            act.wait_ge(*kvs_ok(b, 3))
                            act.wait_ge(*kvc(b, 1))
                            act.dma_start(kv_dram[b], kvs[:, :]).then_inc(kv_out.sem, 16)

                    def step(a, b):
                        for slot in range(SLOTS):
                            if a is not None:
                                mamba(slot, a)
                            if b is not None:
                                experts(slot, b)

                    sweep(act, step)

                @block.gpsimd
                def _(pool):
                    pool.memset(xpad[:, :, 0:PAD], 0.0).then_inc(init, 1)
                    pool.memset(V[:, :, :, P:VW], 1.0).then_inc(init, 1)
                    pool.memset(gp[:, :, :], 0.0).then_inc(init, 1)
                    pool.memset(x1[:, :, :], 0.0).then_inc(init, 1)

                    def mamba(slot, a):
                        if slot == 0:
                            norm_pool(pool, L1, half, a, passed)
                        elif 4 <= slot < 4 + NS:
                            n = slot - 4
                            if n == 0:
                                pool.wait_ge(*acc0(a, 1))
                            pool.wait_ge(*z_ok(a, n + 1))
                            pool.wait_ge(*accum(a, n))
                            pool.tensor_tensor(acc[:, :, :], acc[:, :, :], zz[:, n % 2, :, :], ALU.add)\
                                .then_inc(accum.sem, 1)

                    def add_expert(b, e):
                        pool.wait_ge(*prod_ok(b, e + 1))
                        if e == 0:
                            pool.wait_ge(*facc0(b, 1))
                        pool.wait_ge(*fadd(b, e))
                        pool.tensor_tensor(facc[:, :, :], facc[:, :, :], prod[:, e % 2, :, :], ALU.add)\
                            .then_inc(fadd.sem, 1)

                    def experts(slot, b):
                        if slot == 0:
                            norm_pool(pool, L2, half, b, passed)
                        elif 3 <= slot <= 15 and slot in PROD_SLOT:
                            add_expert(b, PROD_SLOT[slot])
                        if slot == 15:
                            pool.wait_ge(*fadd(b, E0))
                            pool.wait_ge(*gb_in(b, 16))
                            pool.tensor_tensor(facc[:, :, :], facc[:, :, :], mid(gb[:, :], J), ALU.mult)\
                                .then_inc(x2m.sem, 1)
                            pool.wait_ge(*x2m(b, 1))
                            pool.wait_ge(*x2_out(b, 0))
                            pool.wait_ge(*L3.xhat(b, 0))
                            pool.tensor_tensor(x2[:, :, :], x1[:, :, :], facc[:, :, :], ALU.add).then_inc(x2_ok.sem, 1)
                        elif slot == 16:
                            norm_pool(pool, L3, half, b, passed)
                        elif slot == SLOTS - 1:
                            pool.wait_ge(*bmx_ok(b, 1))
                            pool.wait_ge(*kf(b, 0))
                            pool.wait_ge(*kvc(b, 0))
                            hold(pool, passed)
                            pool.partition_all_reduce(cb[:, :], bmx[:, :], P, RMAX).then_inc(call.sem, 1)
                            pool.wait_ge(*call(b, 1))
                            hold(pool, passed)
                            pool.tensor_scalar(ncb[:, :], cb[:, :], -1.0, None, ALU.mult).then_inc(ncb_ok.sem, 1)
                            pool.wait_ge(*mxr(b, 0))
                            hold(pool, passed)
                            pool.tensor_scalar(mxrun[:, :], mxrun[:, :], cb[:, 0:1], None, ALU.max)\
                                .then_inc(mxr.sem, 1)
                            pool.wait_ge(*kv_out(b, 0))
                            hold(pool, passed)
                            pool.tensor_copy(kvs[:, PR * VW:], cb[:, :]).then_inc(kvc.sem, 1)

                    def step(a, b):
                        for slot in range(SLOTS):
                            if a is not None:
                                mamba(slot, a)
                            if b is not None:
                                experts(slot, b)

                    sweep(pool, step)

                @block.tensor
                def _(pe):
                    pe.wait_ge(w_in, 32)

                    def mamba(slot, a):
                        if slot == 0:
                            pe.wait_ge(*u_ok(a, 0))
                            norm_pe(pe, L1, banks[0], ident, a)
                        elif slot == 1:
                            pe.wait_ge(*L1.out(a, 1))
                            for c in range(2 * G):
                                if c == 1:
                                    pe.wait_ge(*ao_ok(a, 0))
                                elif c >= G:
                                    pe.wait_ge(*xraw(a, c - G + 1))
                                pe.matmul(banks[c % 2][:, :], inw[:, c * P:(c + 1) * P], hT[:, :],
                                          start=True, stop=True).then_inc(in_done.sem, 1)
                        elif slot == 2:
                            pe.wait_ge(*xc_ok(a, 1))
                            pe.wait_ge(*zsilu(a, 1))
                            for g in range(G):
                                last = pe.matmul(banks[0][:, :], xw[:, g, :], xc[:, g, :],
                                                 start=(g == 0), stop=(g == G - 1))
                            last.then_inc(xdbl.sem, 1)
                        elif slot == 3:
                            pe.wait_ge(*dtr_ok(a, 1))
                            for g in range(G):
                                if g == 0:
                                    pe.wait_ge(*zsilu(a, 2))
                                else:
                                    pe.wait_ge(*s_hi(a, 1))
                                    pe.wait_ge(*s_rem(a, 1))
                                pe.matmul(banks[1 - g][:, :], dtw[96:96 + RK, g * P:(g + 1) * P],
                                          dtr[96:96 + RK, :], start=True, stop=True).then_inc(dtps.sem, 1)

                    def spread(a, n, which):
                        if n == 0:
                            pe.wait_ge(*s_mid(a, 1))
                            pe.wait_ge(*s_lo(a, 1))
                            pe.wait_ge(*dtmax(a, 2 - which))
                        else:
                            pe.wait_ge(*(z_ok if which else u_ok)(a, n))
                        pe.matmul(banks[which][:, :], pick_sb[:, which * NS + n, :], S[0:96, :],
                                  start=True, stop=True).then_inc((cbc if which else bb).sem, 1)

                    def mamba_out(a):
                        pe.wait_ge(*yz_ok(a, 1))
                        pe.wait_ge(*z_ok(a, NS))
                        for j in range(J):
                            for g in range(G):
                                last = pe.matmul(banks[1][:, j * D:(j + 1) * D], yz[:, g, j * P:(j + 1) * P],
                                                 outw[:, g, :], start=(g == 0), stop=(g == G - 1))
                        last.then_inc(oproj.sem, 1)

                    def ups(b, q):
                        for n in range(2 * q, 2 * q + 2):
                            e, f = divmod(n, FC)
                            ring1_free(pe, f"up{n}", b)
                            pe.matmul(ring1(f"up{n}")[:, :], w1[:, e, f * P:(f + 1) * P], hT2[:, :],
                                      start=True, stop=True).then_inc(up.sem, 1)

                    def downs(b, e):
                        pe.wait_ge(*hid_ok(b, FC * (e + 1)))
                        if e < 2:
                            pe.wait_ge(*kvs_ok(b, 0))
                        else:
                            pe.wait_ge(*prod_ok(b, e - 1))
                        for j in range(J):
                            for f in range(FC):
                                last = pe.matmul(banks[5 + e % 2][:, j * D:(j + 1) * D],
                                                 hid[:, e % 2, f, j * P:(j + 1) * P], w2[:, e, f, :],
                                                 start=(f == 0), stop=(f == FC - 1))
                        last.then_inc(down.sem, 1)

                    def key_tile(b, m):
                        j, s = divmod(m, 2)
                        for name, w, done in (("k", wk, kps), ("d", pk[:, :], dps), ("v", wv, vps)):
                            ring1_free(pe, f"{name}{m}", b)
                            pe.matmul(ring1(f"{name}{m}")[:, :], hT3[:, j * P:(j + 1) * P],
                                      w[:, s * T:(s + 1) * T], start=True, stop=True).then_inc(done.sem, 1)

                    def experts(slot, b):
                        if slot == 0:
                            ring1_free(pe, "turn2", b)
                            norm_pe(pe, L2, ring1("turn2"), ident, b)
                            ring1_free(pe, "logits", b)
                            pe.wait_ge(*L2.out(b, 1))
                            for j in range(J):
                                last = pe.matmul(ring1("logits")[:, j * E0:(j + 1) * E0], hT2[:, j * P:(j + 1) * P],
                                                 gatew, start=True, stop=True)
                            last.then_inc(logits.sem, 1)
                        if slot == 2:
                            pe.wait_ge(*gw(b, 1))
                            ring1_free(pe, "gates", b)
                            pe.transpose(ring1("gates")[:, 0:P], gp[:, :, :].rearrange("p j e -> p (j e)"),
                                         ident).then_inc(gturn.sem, 1)
                        for q in HALVES.get(slot, ()):
                            ups(b, q)
                            if q == 1:
                                pe.wait_ge(*gT_ok(b, 1))
                                pe.wait_ge(*kvs_ok(b, 0))
                                pe.matmul(banks[7][:, :], gT[:, :], b2, start=True, stop=True).then_inc(b2ps.sem, 1)
                            if q % 2:
                                downs(b, q // 2)
                        if slot == 16:
                            ring1_free(pe, "turn3", b)
                            norm_pe(pe, L3, ring1("turn3"), ident, b)
                        elif slot >= 17:
                            if slot == 17:
                                pe.wait_ge(*L3.out(b, 1))
                            key_tile(b, 2 * (slot - 17))
                            key_tile(b, 2 * (slot - 17) + 1)
                        if slot == SLOTS - 1:
                            pe.wait_ge(*prod_ok(b, E0))
                            pe.wait_ge(*facc0(b, 1))
                            pe.wait_ge(*vc(b, 2 * J))
                            for j in range(J):
                                pe.wait_ge(*kf(b, j + 1))
                                for pr in range(PR):
                                    at = (pr % 3) * VW
                                    last = pe.matmul(banks[5 + pr // 3][:, at:at + VW],
                                                     Ek[:, j, pr * P:(pr + 1) * P], V[:, j, pr, :],
                                                     start=(j == 0 and pr % 3 == 0), stop=(j == J - 1),
                                                     skip_group_check=True)
                            last.then_inc(kv.sem, 1)

                    def step(a, b):
                        for slot in range(SLOTS):
                            n = slot - 4
                            if a is not None:
                                mamba(slot, a)
                                if 0 <= n < NS:
                                    spread(a, n, 0)
                                    spread(a, n, 1)
                                if n == NS:
                                    mamba_out(a)
                            if b is not None:
                                experts(slot, b)

                    sweep(pe, step)

                @block.vector
                def _(dve):
                    dve.wait_ge(a_exp, 1)
                    dve.tensor_scalar(aneg[:, :, :], aneg[:, :, :], -1.0, None, ALU.mult).then_inc(a_neg, 1)
                    dve.wait_ge(init, 4)
                    cA, cB = Chain(dve, chainA), Chain(dve, chainB)

                    def mamba(slot, a):
                        if slot == 0:
                            dve.wait_ge(*x_in(a, 16))
                            norm_dve(dve, L1, xs, a, passed)
                        elif slot == 1:
                            dve.wait_ge(*xc_ok(a, 0))
                            dve.wait_ge(*dt_ok(a, 0))
                            for g in range(G):
                                dve.wait_ge(*xraw(a, g + 1))
                                cA.step(dve.tensor_scalar(cv[:, g, :], xpad[:, g, PAD:], convw[:, g, PAD:],
                                                          convb[:, g:g + 1], ALU.mult, ALU.add))
                                for k in range(PAD):
                                    ins = dve.scalar_tensor_tensor(cv[:, g, :], xpad[:, g, k:k + T],
                                                                   convw[:, g, k:k + 1], cv[:, g, :],
                                                                   ALU.mult, ALU.add)
                                    if k < PAD - 1:
                                        cA.step(ins)
                                    else:
                                        ins.then_inc(conv.sem, 1)
                        elif slot == 2:
                            dve.wait_ge(*s_hi(a, 1))
                            dve.tensor_tensor(S[32:64, :], banks[0][32:64, :], S[32:64, :], ALU.subtract)\
                               .then_inc(s_mid.sem, 1)
                            dve.wait_ge(*s_lo(a, 0))
                            dve.tensor_tensor(R[64:96, :], banks[0][64:96, :], S[64:96, :], ALU.subtract)\
                               .then_inc(s_rem.sem, 1)
                            dve.wait_ge(*s_remb(a, 1))
                            dve.tensor_tensor(S[64:96, :], R[64:96, :], Rb[64:96, :], ALU.subtract)\
                               .then_inc(s_lo.sem, 1)
                        elif slot == 3:
                            dve.wait_ge(*dec_ok(a, 0))
                            for g in range(G):
                                dve.wait_ge(*dtabs(a, g + 1))
                                dve.tensor_scalar(dt[:, g, :], banks[1 - g][:, :], dtb[:, g:g + 1], 0.0,
                                                  ALU.add, ALU.max).then_inc(dtmax.sem, 1)
                            dve.wait_ge(*dtln(a, 1))
                            dve.wait_ge(*dtmax(a, G))
                            dve.tensor_tensor(dt[:, :, :], dt[:, :, :], ax[:, :, :], ALU.add).then_inc(dt_ok.sem, 1)
                            dve.wait_ge(*dt_ok(a, 1))
                            dve.tensor_tensor(dtx[:, :, :], dt[:, :, :], xc[:, :, :], ALU.mult)\
                               .then_inc(dtx_ok.sem, 1)
                            dve.wait_ge(*dtx_ok(a, 1))
                            dve.wait_ge(*oproj(a, 0))
                        elif slot < 4 + NS:
                            n = slot - 4
                            dve.wait_ge(*bb(a, n + 1))
                            dve.tensor_tensor(u[:, :, :], dtx[:, :, :], mid(banks[0][:, :], G), ALU.mult)\
                               .then_inc(u_ok.sem, 1)
                            dve.wait_ge(*u_ok(a, n + 1))
                            for g in range(G):
                                dve.wait_ge(*dec_ok(a, G * n + g + 1))
                                dve.tensor_tensor_scan(h[:, g, :], dec[:, n % 2, g, :], u[:, g, :], 0.0,
                                                       ALU.mult, ALU.add).then_inc(scan.sem, 1)
                            dve.wait_ge(*scan(a, G * (n + 1)))
                            dve.wait_ge(*cbc(a, n + 1))
                            dve.wait_ge(*accum(a, n - 1 if n >= 2 else 0))
                            dve.tensor_tensor(zz[:, n % 2, :, :], h[:, :, :], mid(banks[1][:, :], G), ALU.mult)\
                               .then_inc(z_ok.sem, 1)
                            dve.wait_ge(*z_ok(a, n + 1))
                        else:
                            dve.wait_ge(*accum(a, NS))
                            dve.wait_ge(*zsilu(a, G))
                            dve.tensor_tensor(yz[:, :, :], acc[:, :, :], zs[:, :, :], ALU.mult).then_inc(yz_ok.sem, 1)
                            dve.wait_ge(*oproj(a, 1))
                            dve.wait_ge(*ga_in(a, 16))
                            dve.tensor_tensor(ao[:, :, :], banks[1][:, :].rearrange("p (j d) -> p j d", j=J),
                                              mid(ga[:, :], J), ALU.mult).then_inc(ao_ok.sem, 1)
                            dve.wait_ge(*ao_ok(a, 1))
                            dve.wait_ge(*x2_ok(a, 0))
                            dve.tensor_tensor(x1[:, :, :], xs[:, :, :], ao[:, :, :], ALU.add).then_inc(x1_ok.sem, 1)

                    def key_tile(b, m):
                        j, s = divmod(m, 2)
                        dash = ring1(f"d{m}")[:, :].rearrange("p (h k) -> p h k", h=8)
                        dve.wait_ge(*sq_ok(b, m + 1))
                        dve.tensor_reduce(ssq[:, m, :], sq[:, m % 2, :].rearrange("p (h k) -> p h k", h=8),
                                          AX.X, ALU.add).then_inc(ssum.sem, 1)
                        dve.wait_ge(*dps(b, m + 1))
                        cB.step(dve.tensor_reduce(mxs[:, m:m + 1], dash, AX.XY, ALU.max))
                        dve.wait_ge(*ssum(b, m + 1))
                        dve.wait_ge(*kv(b, 0))
                        dve.scalar_tensor_tensor(
                            Ek[:, j, s * T:(s + 1) * T].rearrange("p (h k) -> p h k", h=8),
                            inner(ssq[:, m, :], DH), -DIAG, dash, ALU.mult, ALU.add).then_inc(ush.sem, 1)

                    def experts(slot, b):
                        if slot == 0:
                            dve.wait_ge(*x1_ok(b, 1))
                            norm_dve(dve, L2, x1, b, passed)
                        elif slot == 1:
                            dve.wait_ge(*logits(b, 1))
                            lg = ring1("logits")[:, 0:J * E0].rearrange("p (j e) -> p j e", j=J)
                            hold(dve, passed)
                            for j in range(J):
                                last = dve.max(m8[:, j, :], lg[:, j, :])
                            cB.step(last)
                            hold(dve, passed)
                            for j in range(J):
                                last = dve.max_index(idx[:, j, :], m8[:, j, :], lg[:, j, :])
                            cB.step(last)
                            dve.wait_ge(*gw(b, 0))
                            cB.step(dve.tensor_tensor(oh[:, :, :], mid(iota[:, 0:E0], J),
                                                      idx[:, :, 0:1].to_broadcast([P, J, E0]), ALU.is_equal))
                            dve.wait_ge(*lexp(b, 0))
                            dve.tensor_tensor(lm[:, :, :], lg, m8[:, :, 0:1].to_broadcast([P, J, E0]),
                                              ALU.subtract).then_inc(lshift.sem, 1)
                            dve.wait_ge(*lexp(b, 1))
                            cB.step(dve.tensor_reduce(esum[:, :], ex[:, :, :], AX.X, ALU.add))
                            cB.step(dve.reciprocal(erec[:, :], esum[:, :]))
                            dve.wait_ge(*gturn(b, 0))
                            dve.tensor_tensor(gp[:, :, 0:E0], oh[:, :, :], inner(erec[:, :], E0),
                                              ALU.mult).then_inc(gw.sem, 1)
                            dve.wait_ge(*gw(b, 1))
                        if slot == 3:
                            dve.wait_ge(*b2ps(b, 1))
                            dve.wait_ge(*x2_ok(b, 0))
                            dve.tensor_copy(facc[:, :, :].rearrange("p j d -> p (j d)"), banks[7][:, :])\
                               .then_inc(facc0.sem, 1)
                        if slot in PROD_SLOT:
                            e = PROD_SLOT[slot]
                            dve.wait_ge(*down(b, e + 1))
                            dve.wait_ge(*fadd(b, e - 1 if e >= 2 else 0))
                            dve.tensor_tensor(prod[:, e % 2, :, :],
                                              banks[5 + e % 2][:, :].rearrange("p (j d) -> p j d", j=J),
                                              gp[:, :, e:e + 1].to_broadcast([P, J, D]), ALU.mult)\
                               .then_inc(prod_ok.sem, 1)
                        if slot == 16:
                            dve.wait_ge(*x2_ok(b, 1))
                            norm_dve(dve, L3, x2, b, passed)
                        elif slot >= 17:
                            key_tile(b, 2 * (slot - 17))
                            key_tile(b, 2 * (slot - 17) + 1)
                        if slot == SLOTS - 1:
                            dve.wait_ge(*call(b, 0))
                            dve.tensor_reduce(bmx[:, :], mxs[:, :], AX.X, ALU.max).then_inc(bmx_ok.sem, 1)

                    def step(a, b):
                        cA.begin(a)
                        cB.begin(b)
                        for slot in range(SLOTS):
                            if a is not None:
                                mamba(slot, a)
                            if b is not None:
                                experts(slot, b)

                    sweep(dve, step)

            end_part()

        sweep_two(nc, ctx, sem, sig, sbuf, banks, ident, iota, wv, pq, modc, ones, half, mxrun, nmx, two,
                  gate_rows, x2_dram, h3_dram, kv_dram, out_v)


def sweep_two(nc, ctx, sem, sig, sbuf, banks, ident, iota, wv, pq, modc, ones, half, mxrun, nmx, two,
              gate_rows, x2_dram, h3_dram, kv_dram, out_v):
    with ExitStack() as part:
        sb = sbuf(part)
        two_sb = sb("two_sb", [P, TWO_N])

        def V2(name):
            at, n = TWO[name]
            return two_sb[:, at:at + n]

        wq, w1, b1c, b2r, g1, be1, g2, be2, gatew, mw1 = (
            V2(n) for n in ("wq", "w1", "b1", "b2", "g1", "be1", "g2", "be2", "gate", "mw1"))
        wo = V2("wo").rearrange("p (r d) -> p r d", r=PR)
        w2 = V2("w2").rearrange("p (f d) -> p f d", f=FC)
        mw2 = V2("mw2").rearrange("p (r d) -> p r d", r=MC)
        s1w, s2w = V2("s1"), V2("s2")
        s3w = V2("s3").rearrange("p (r d) -> p r d", r=SC)
        pick = V2("pick").rearrange("p (r m) -> p r m", r=MC)
        h3 = sb("h3", [P, T])
        kvl = sb("kvl", [P, PR * VW + 1])
        sfac = sb("sfac", [P, 1])
        hsum = sb("hsum", [P, 1])
        hsB = sb("hsB", [P, P])
        evs = sb("evs", [P, HD])
        kvb = sb("kvb", [P, PR, P])
        ksb = sb("ksb", [P, PR, 2])
        qsqb = sb("qsqb", [P, 2, T])
        qs = sb("qs", [P, 8])
        qm = sb("qm", [P, 8])
        nb = sb("nb", [P, 8])
        uq = sb("uq", [P, 2, T])
        qT = sb("qT", [P, 2, T])
        rd = sb("rd", [P, 8])
        at = sb("at", [P, 2, T])
        aT = sb("aT", [P, 2, T])
        o1T = sb("o1T", [P, T])
        x2 = sb("x2s", [P, J, D])
        gab = sb("gab", [P, 2, D])
        gg = sb("gg", [P, D])
        gbe = sb("gbe", [P, D])
        vb = sb("vb", [P, 2, T])
        ee = sb("ee", [P, 2, T])
        hE = sb("hE", [P, FC, T])
        t6 = sb("t6", [P, J, D])
        x3 = sb("x3", [P, J, D])
        hT4 = sb("hT4", [P, T])
        m8 = sb("m8b", [P, J, 8])
        idx = sb("idxb", [P, J, 8], U32)
        gd = sb("gd", [P, J])
        gex = sb("gex", [P, J])
        gsum = sb("gsum", [P, J])
        gw1 = sb("gw1", [P, J])
        gw2 = sb("gw2", [P, J])
        oh1 = sb("oh1", [P, J, E1])
        oh2 = sb("oh2", [P, J, E1])
        disp = sb("disp", [P, J, E1])
        dT = sb("dT", [E1, T])
        NX = MC + SC
        th = sb("th", [P, 2, T])
        sl = sb("sl", [P, 2, T])
        hm = sb("hm", [P, NX, T])
        fo = sb("fo", [P, J, D])
        ob = sb("ob", [P, J, D])

        w_in, init, nmx_ok, passed = (sem(n) for n in ("w2_in", "init2", "nmx_ok", "passed2"))
        h3_in, kv_in, x2_in, gab_in, res_out = (sig(n, 16) for n in ("h3_in", "kv_in", "x2_in", "gab_in", "res_out"))
        gab_in.per = 32
        L5, L6, L7 = (Norm(sb, sig, n, e) for n, e in (("n5", EPS_ENC), ("n6", EPS_ENC), ("n7", EPS_MOD)))
        M = 2 * J
        (sf, hsb, vsps, evs_ok, kvb_ok, qps, qd, qsq, qss, qu, qe, qt, qT_ok, num, rd_ok, at_ok, att, aT_ok,
         wo_ok, chainC) = (sig(n, p) for n, p in (
             ("sf", 1), ("hsb", 1), ("vsps", 2), ("evs_ok", 2), ("kvb_ok", 1), ("qps", M), ("qd", M), ("qsq", M),
             ("qss", M), ("qu", M), ("qe", M), ("qt", M), ("qT_ok", M), ("num", M), ("rd_ok", M), ("at_ok", M),
             ("att", M), ("aT_ok", M), ("wo_ok", M), ("chainC", 1 + 2 * M)))
        (w1ps, vb_ok, ee_ok, em_ok, he, w2ps, gg_ok, t6a, t6b, x3_ok, lg_ok, gidx, gd_ok, gex_ok, disp_ok, dtp, dT_ok,
         xps, yps, th_ok, sl_ok, hm_ok, mo, fin, ob_ok, chainD) = (sig(n, p) for n, p in (
             ("w1ps", FC), ("vb_ok", FC), ("ee_ok", FC), ("em_ok", FC), ("he", FC), ("w2ps", 1), ("gg_ok", 1), ("t6a", 1),
             ("t6b", 1), ("x3_ok", 1), ("lg_ok", 1), ("gidx", 1), ("gd_ok", 1), ("gex_ok", 1), ("disp_ok", 1),
             ("dtp", 1), ("dT_ok", 1), ("xps", NX), ("yps", NX), ("th_ok", NX), ("sl_ok", NX), ("hm_ok", NX),
             ("mo", 1), ("fin", 1), ("ob_ok", 1), ("chainD", 8)))

        ringC = []
        for t in range(M + 3):
            if t < M:
                ringC += [(f"q{t}", qsq, t + 1), (f"d{t}", qu, t + 1)]
            if t == 0:
                ringC += [("vs0", evs_ok, 1), ("vs1", evs_ok, 2)]
            if 1 <= t <= M:
                ringC += [(f"t{t - 1}", qT_ok, t)]
            if 2 <= t <= M + 1:
                ringC += [(f"n{t - 2}", at_ok, t - 1)]
            if t >= 3:
                ringC += [(f"a{t - 3}", aT_ok, t - 2)]
        ringD = [("turn5", L5.out, 1)] + [(f"w{f}", vb_ok, f + 1) for f in range(FC)]
        ringD += [("turn7", L7.out, 1), ("lg", gidx, 1)]
        for q in range(NX):
            if q == 1:
                ringD += [("dT", dT_ok, 1)]
            ringD += [(f"x{q}", sl_ok, q + 1), (f"y{q}", hm_ok, q + 1)]

        def make_ring(uses, first, size):
            place = {name: n for n, (name, _, _) in enumerate(uses)}

            def bank(name):
                return banks[first + place[name] % size]

            def free(pe, name, b):
                n = place[name]
                if n >= size:
                    _, done, count = uses[n - size]
                    pe.wait_ge(*done(b, count))
                else:
                    back = max(k for k in range(len(uses)) if k % size == n % size)
                    _, done, _ = uses[back]
                    pe.wait_ge(*done(b, 0))
            return bank, free

        bankC, freeC = make_ring(ringC, 0, 3)
        bankD, freeD = make_ring(ringD, 5, 2)
        SLOTS = M + 4

        def at_slot(slot, lag):
            return slot - lag if 0 <= slot - lag < M else None

        XQ = {6: (0,), 7: (1,), 8: (2, 3), 9: (4, 5), 10: (6, 7), 11: (8, 9)}
        DOWN = {8: (0, 1), 9: (2, 3), 10: (4, 5), 11: (6, 7)}
        WF = {1: (0, 1), 2: (2, 3)}
        WD = {2: (0, 1), 3: (2, 3)}

        def sweep(eng, step):
            step(0, None)
            step(1, 0)
            with eng.Fori(2, NB) as i:
                step(i, i - 1)
            step(None, NB - 1)

        with nc.Block() as block:
            @block.sync
            def _(sp):
                sp.dma_start(two_sb[:, :], two).then_inc(w_in, 16)

                def load_keys(c):
                    sp.wait_ge(*qd(c, 0))
                    sp.dma_start(h3[:, :], h3_dram[c]).then_inc(h3_in.sem, 16)
                    sp.wait_ge(*kvb_ok(c, 0))
                    sp.dma_start(kvl[:, :], kv_dram[c]).then_inc(kv_in.sem, 16)

                def load_feed(d):
                    sp.wait_ge(*x3_ok(d, 0))
                    sp.dma_start(x2[:, :, :].rearrange("p j d -> p (j d)"), x2_dram[d]).then_inc(x2_in.sem, 16)
                    sp.wait_ge(*fin(d, 0))
                    for k in range(2):
                        sp.dma_start(gab[:, k, :], gate_rows[2 + k, d].partition_broadcast(P))\
                          .then_inc(gab_in.sem, 16)

                def store(d):
                    sp.wait_ge(*ob_ok(d, 1))
                    sp.dma_start(out_v[d], ob[:, :, :]).then_inc(res_out.sem, 16)

                load_keys(0)
                load_keys(1)
                load_feed(0)
                load_keys(2)
                store(0)
                with sp.Fori(2, NB - 1) as i:
                    load_feed(i - 1)
                    load_keys(i + 1)
                    store(i - 1)
                for d in (NB - 2, NB - 1):
                    load_feed(d)
                    store(d)
                sp.wait_ge(*res_out(NB, 0))

            @block.scalar
            def _(act):
                act.wait_ge(w_in, 16)
                act.wait_ge(nmx_ok, 1)

                def square(m, c):
                    act.wait_ge(*qps(c, m + 1))
                    act.wait_ge(*qss(c, m - 1 if m >= 2 else 0))
                    act.activation(qsqb[:, m % 2, :], bankC(f"q{m}")[:, :], ACT.Square).then_inc(qsq.sem, 1)

                def feature(m, c):
                    act.wait_ge(*qu(c, m + 1))
                    act.activation(uq[:, m % 2, :], uq[:, m % 2, :], ACT.Exp).then_inc(qe.sem, 1)

                def keys(c):
                    act.wait_ge(*kv_in(c, 16))
                    act.wait_ge(*kvb_ok(c, 0))
                    act.activation(sfac[:, :], kvl[:, PR * VW:], ACT.Exp, bias=nmx[:, 0:1]).then_inc(sf.sem, 1)
                    for s in range(2):
                        act.wait_ge(*vsps(c, s + 1))
                        act.activation(evs[:, s * T:(s + 1) * T], bankC(f"vs{s}")[:, :], ACT.Copy,
                                       scale=EPS_FEAT).then_inc(evs_ok.sem, 1)

                def keep_features(m, c):
                    act.wait_ge(*qt(c, m + 1))
                    act.wait_ge(*num(c, m - 1 if m >= 2 else 0))
                    act.activation(qT[:, m % 2, :], bankC(f"t{m}")[:, :], ACT.Copy, bias=EPS_FEAT)\
                       .then_inc(qT_ok.sem, 1)

                def keep_quotient(m, c):
                    act.wait_ge(*att(c, m + 1))
                    act.wait_ge(*wo_ok(c, m - 1 if m >= 2 else 0))
                    act.activation(aT[:, m % 2, :], bankC(f"a{m}")[:, :], ACT.Copy).then_inc(aT_ok.sem, 1)

                def first_norm(d):
                    act.wait_ge(*L5.turned(d, 1))
                    act.wait_ge(*w2ps(d, 0))
                    act.activation(o1T[:, :], bankD("turn5")[:, :], ACT.Identity, scale=g1, bias=be1)\
                       .then_inc(L5.out.sem, 1)

                def elu(f, d):
                    act.wait_ge(*w1ps(d, f + 1))
                    act.wait_ge(*he(d, f - 1 if f >= 2 else 0))
                    act.activation(vb[:, f % 2, :], bankD(f"w{f}")[:, :], ACT.Identity,
                                   bias=b1c[:, f:f + 1]).then_inc(vb_ok.sem, 1)
                    act.wait_ge(*em_ok(d, f + 1))
                    act.activation(ee[:, f % 2, :], ee[:, f % 2, :], ACT.Exp).then_inc(ee_ok.sem, 1)

                def modulate(d):
                    act.wait_ge(*L7.turned(d, 1))
                    act.wait_ge(*xps(d, 0))
                    act.wait_ge(*yps(d, 0))
                    act.activation(hT4[:, :], bankD("turn7")[:, :], ACT.Identity, scale=modc[:, 1, d, 3:4],
                                   bias=modc[:, 1, d, 2:3]).then_inc(L7.out.sem, 1)

                def gates(d):
                    act.wait_ge(*gd_ok(d, 1))
                    act.activation(gex[:, :], gd[:, :], ACT.Exp).then_inc(gex_ok.sem, 1)

                def keep_dispatch(d):
                    act.wait_ge(*dtp(d, 1))
                    act.activation(dT[:, :], bankD("dT")[0:E1, :], ACT.Copy).then_inc(dT_ok.sem, 1)

                def tanh(q, d):
                    act.wait_ge(*xps(d, q + 1))
                    act.wait_ge(*sl_ok(d, q - 1 if q >= 2 else 0))
                    act.activation(th[:, q % 2, :], bankD(f"x{q}")[:, :], ACT.Tanh, scale=0.5)\
                       .then_inc(th_ok.sem, 1)

                def step(c, d):
                    for slot in range(SLOTS):
                        chunks = XQ.get(slot, ()) if d is not None else ()
                        if c is not None and slot < M:
                            square(slot, c)
                        if d is not None and slot == 0:
                            first_norm(d)
                        if c is not None and slot == 0:
                            keys(c)
                        if d is not None and slot == 6:
                            modulate(d)
                        for q in chunks[:1] if slot > 6 else ():
                            tanh(q, d)
                        if c is not None and slot < M:
                            feature(slot, c)
                        if d is not None and slot in WF:
                            for f in WF[slot]:
                                elu(f, d)
                        if d is not None and slot == 6:
                            gates(d)
                        if d is not None and slot == 7:
                            keep_dispatch(d)
                        for q in chunks[1:] if slot > 6 else chunks:
                            tanh(q, d)
                        if c is not None and at_slot(slot, 1) is not None:
                            keep_features(at_slot(slot, 1), c)
                        if c is not None and at_slot(slot, 3) is not None:
                            keep_quotient(at_slot(slot, 3), c)

                sweep(act, step)

            @block.gpsimd
            def _(pool):
                pool.memset(kvb[:, :, :], 0.0).then_inc(init, 1)
                pool.memset(ksb[:, :, :], 0.0).then_inc(init, 1)
                pool.tensor_scalar(nmx[:, :], mxrun[:, :], -1.0, None, ALU.mult).then_inc(nmx_ok, 1)
                pool.wait_ge(w_in, 16)

                def step(c, d):
                    if d is not None:
                        pool.wait_ge(*gab_in(d, 32))
                        pool.wait_ge(*x3_ok(d, 0))
                        pool.tensor_tensor(gg[:, :], g2, gab[:, 0, :], ALU.mult)
                        pool.tensor_tensor(gbe[:, :], be2, gab[:, 0, :], ALU.mult).then_inc(gg_ok.sem, 1)
                        norm_pool(pool, L6, half, d, passed)
                        pool.wait_ge(*gg_ok(d, 1))
                        pool.wait_ge(*L6.xhat(d, 1))
                        pool.tensor_tensor(t6[:, :, :], L6.xh[:, :, :], mid(gg[:, :], J), ALU.mult).then_inc(t6a.sem, 1)
                        pool.wait_ge(*t6a(d, 1))
                        pool.tensor_tensor(t6[:, :, :], t6[:, :, :], mid(gbe[:, :], J), ALU.add).then_inc(t6b.sem, 1)
                        pool.wait_ge(*t6b(d, 1))
                        pool.wait_ge(*x2_in(d, 16))
                        pool.wait_ge(*ob_ok(d, 0))
                        pool.wait_ge(*L7.xhat(d, 0))
                        pool.tensor_tensor(x3[:, :, :], x2[:, :, :], t6[:, :, :], ALU.add).then_inc(x3_ok.sem, 1)
                        norm_pool(pool, L7, half, d, passed)
                    if c is not None:
                        norm_pool(pool, L5, half, c, passed)
                    if d is not None:
                        pool.wait_ge(*fin(d, 1))
                        pool.wait_ge(*res_out(d, 0))
                        pool.tensor_tensor(ob[:, :, :], x3[:, :, :], fo[:, :, :], ALU.add).then_inc(ob_ok.sem, 1)

                sweep(pool, step)

            @block.tensor
            def _(pe):
                pe.wait_ge(w_in, 16)

                def query(m, c, name):
                    j, s = divmod(m, 2)
                    w, done = (wq, qps) if name == "q" else (pq[:, :], qd)
                    if m == 0:
                        pe.wait_ge(*h3_in(c, 16))
                    freeC(pe, f"{name}{m}", c)
                    pe.matmul(bankC(f"{name}{m}")[:, :], h3[:, j * P:(j + 1) * P], w[:, s * T:(s + 1) * T],
                              start=True, stop=True).then_inc(done.sem, 1)

                def value_sums(c):
                    pe.wait_ge(*hsb(c, 1))
                    for s in range(2):
                        freeC(pe, f"vs{s}", c)
                        pe.matmul(bankC(f"vs{s}")[:, :], hsB[:, :], wv[:, s * T:(s + 1) * T],
                                  start=True, stop=True).then_inc(vsps.sem, 1)

                def residual(c):
                    pe.wait_ge(*L5.xhat(c, 0))
                    for j in range(J):
                        pe.matmul(banks[3][:, j * D:(j + 1) * D], h3[:, j * P:(j + 1) * P], ident,
                                  start=(j == 0), stop=False, skip_group_check=True)

                def turn_features(m, c):
                    freeC(pe, f"t{m}", c)
                    pe.wait_ge(*qe(c, m + 1))
                    for k in range(4):
                        last = pe.transpose(bankC(f"t{m}")[:, k * P:(k + 1) * P],
                                            uq[:, m % 2, k * P:(k + 1) * P], ident)
                    last.then_inc(qt.sem, 1)

                def numerators(m, c):
                    s = m % 2
                    freeC(pe, f"n{m}", c)
                    pe.wait_ge(*qT_ok(c, m + 1))
                    pe.wait_ge(*kvb_ok(c, 1))
                    pe.wait_ge(*rd_ok(c, m))
                    for k in range(4):
                        lhs = qT[:, m % 2, k * P:(k + 1) * P]
                        pe.matmul(bankC(f"n{m}")[:, k * P:(k + 1) * P], lhs, kvb[:, 4 * s + k, :],
                                  start=True, stop=True)
                        last = pe.matmul(banks[4][:, 2 * k:2 * k + 2], lhs, ksb[:, 4 * s + k, :],
                                         start=True, stop=True)
                    last.then_inc(num.sem, 1)

                def turn_quotient(m, c):
                    freeC(pe, f"a{m}", c)
                    pe.wait_ge(*at_ok(c, m + 1))
                    for k in range(4):
                        last = pe.transpose(bankC(f"a{m}")[:, k * P:(k + 1) * P],
                                            at[:, m % 2, k * P:(k + 1) * P], ident)
                    last.then_inc(att.sem, 1)

                def output(m, c):
                    j, s = divmod(m, 2)
                    pe.wait_ge(*aT_ok(c, m + 1))
                    for k in range(4):
                        last = pe.matmul(banks[3][:, j * D:(j + 1) * D], aT[:, m % 2, k * P:(k + 1) * P],
                                         wo[:, 4 * s + k, :], start=False, stop=(s == 1 and k == 3),
                                         skip_group_check=True)
                    last.then_inc(wo_ok.sem, 1)

                def feed_first(f, d):
                    if f == 0:
                        pe.wait_ge(*L5.out(d, 1))
                    freeD(pe, f"w{f}", d)
                    pe.matmul(bankD(f"w{f}")[:, :], w1[:, f * P:(f + 1) * P], o1T[:, :],
                              start=True, stop=True).then_inc(w1ps.sem, 1)

                def feed_second(f, d):
                    if f == 0:
                        pe.wait_ge(*fin(d, 0))
                        pe.matmul(banks[7][:, :], ones[0:1, :], b2r[0:1, :], start=True, stop=False,
                                  skip_group_check=True)
                        for j in range(J):
                            pe.matmul(banks[7][:, j * D:(j + 1) * D], o1T[:, j * P:(j + 1) * P], ident,
                                      start=False, stop=False, skip_group_check=True)
                    pe.wait_ge(*he(d, f + 1))
                    for j in range(J):
                        last = pe.matmul(banks[7][:, j * D:(j + 1) * D], hE[:, f, j * P:(j + 1) * P],
                                         w2[:, f, :], start=False, stop=(f == FC - 1), skip_group_check=True)
                    if f == FC - 1:
                        last.then_inc(w2ps.sem, 1)

                def logits(d):
                    freeD(pe, "lg", d)
                    pe.wait_ge(*L7.out(d, 1))
                    for j in range(J):
                        last = pe.matmul(bankD("lg")[:, j * E1:(j + 1) * E1], hT4[:, j * P:(j + 1) * P], gatew,
                                         start=True, stop=True)
                    last.then_inc(lg_ok.sem, 1)

                def turn_dispatch(d):
                    freeD(pe, "dT", d)
                    pe.wait_ge(*disp_ok(d, 1))
                    for j in range(J):
                        last = pe.transpose(bankD("dT")[0:E1, j * P:(j + 1) * P], disp[:, j, :], ident)
                    last.then_inc(dtp.sem, 1)

                def hidden(q, d):
                    w = s1w[:, q * P:(q + 1) * P] if q < SC else mw1[:, (q - SC) * P:(q - SC + 1) * P]
                    freeD(pe, f"x{q}", d)
                    pe.matmul(bankD(f"x{q}")[:, :], w, hT4[:, :], start=True, stop=True).then_inc(xps.sem, 1)

                def factor(q, d):
                    if q < SC:
                        w, rhs = s2w[:, q * P:(q + 1) * P], hT4[:, :]
                    else:
                        w, rhs = pick[0:E1, q - SC, :], dT[:, :]
                        pe.wait_ge(*dT_ok(d, 1))
                    freeD(pe, f"y{q}", d)
                    pe.matmul(bankD(f"y{q}")[:, :], w, rhs, start=True, stop=True).then_inc(yps.sem, 1)

                def down(q, d):
                    w = s3w[:, q, :] if q < SC else mw2[:, q - SC, :]
                    if q == 0:
                        pe.wait_ge(*L6.xhat(d, 1))
                    pe.wait_ge(*hm_ok(d, q + 1))
                    for j in range(J):
                        last = pe.matmul(banks[7][:, j * D:(j + 1) * D], hm[:, q, j * P:(j + 1) * P], w,
                                         start=(q == 0 and j == 0), stop=(q == NX - 1), skip_group_check=True)
                    if q == NX - 1:
                        last.then_inc(mo.sem, 1)

                def step(c, d):
                    for slot in range(SLOTS):
                        chunks = XQ.get(slot, ()) if d is not None else ()
                        if d is not None and slot == 6:
                            freeD(pe, "turn7", d)
                            norm_pe(pe, L7, bankD("turn7"), ident, d)
                        if c is not None and slot < M:
                            query(slot, c, "q")
                        if d is not None and slot == 0:
                            freeD(pe, "turn5", d)
                            norm_pe(pe, L5, bankD("turn5"), ident, d)
                        if slot > 6:
                            for q in chunks[:1]:
                                hidden(q, d) if slot != 7 else None
                        if c is not None and slot < M:
                            query(slot, c, "d")
                        if c is not None and slot == 0:
                            value_sums(c)
                        if d is not None and slot == 6:
                            logits(d)
                        if d is not None and slot == 7:
                            turn_dispatch(d)
                            hidden(chunks[0], d)
                        for q in chunks[:1]:
                            if slot == 6:
                                hidden(q, d)
                            factor(q, d)
                        if c is not None and slot == 3:
                            residual(c)
                        if c is not None and at_slot(slot, 4) is not None:
                            output(at_slot(slot, 4), c)
                        if d is not None:
                            for f in WF.get(slot, ()):
                                feed_first(f, d)
                            for q in DOWN.get(slot, ()):
                                down(q, d)
                        for q in chunks[1:]:
                            hidden(q, d)
                        if c is not None and at_slot(slot, 1) is not None:
                            turn_features(at_slot(slot, 1), c)
                        for q in chunks[1:]:
                            factor(q, d)
                        if c is not None and at_slot(slot, 2) is not None:
                            numerators(at_slot(slot, 2), c)
                        if d is not None:
                            for f in WD.get(slot, ()):
                                feed_second(f, d)
                        if c is not None and at_slot(slot, 3) is not None:
                            turn_quotient(at_slot(slot, 3), c)
                    if d is not None:
                        down(NX - 2, d)
                        down(NX - 1, d)

                sweep(pe, step)

            @block.vector
            def _(dve):
                dve.wait_ge(w_in, 16)
                dve.wait_ge(init, 2)
                cC, cD = Chain(dve, chainC), Chain(dve, chainD)
                attn = banks[3][:, :].rearrange("p (j d) -> p j d", j=J)
                ffn = banks[7][:, :].rearrange("p (j d) -> p j d", j=J)

                def sum_keys(c):
                    dve.wait_ge(*h3_in(c, 16))
                    cC.step(dve.tensor_reduce(hsum[:, :], h3[:, :], AX.X, ALU.add))
                    dve.wait_ge(*vsps(c, 0))
                    dve.tensor_scalar(hsB[:, :], ones[:, :], hsum[:, 0:1], None, ALU.mult).then_inc(hsb.sem, 1)

                def exponent(m, c):
                    dash = bankC(f"d{m}")[:, :].rearrange("p (h k) -> p h k", h=8)
                    dve.wait_ge(*qsq(c, m + 1))
                    dve.wait_ge(*qu(c, m))
                    dve.tensor_reduce(qs[:, :], qsqb[:, m % 2, :].rearrange("p (h k) -> p h k", h=8),
                                      AX.X, ALU.add).then_inc(qss.sem, 1)
                    dve.wait_ge(*qd(c, m + 1))
                    cC.step(dve.tensor_reduce(qm[:, :], dash, AX.X, ALU.max))
                    cC.step(dve.scalar_tensor_tensor(nb[:, :], qs[:, :], -DIAG, qm[:, :], ALU.mult, ALU.subtract))
                    dve.wait_ge(*qt(c, m - 1 if m >= 2 else 0))
                    dve.tensor_tensor(uq[:, m % 2, :].rearrange("p (h k) -> p h k", h=8), dash,
                                      inner(nb[:, :], DH), ALU.add).then_inc(qu.sem, 1)

                def keys(c):
                    dve.wait_ge(*sf(c, 1))
                    dve.wait_ge(*evs_ok(c, 2))
                    dve.wait_ge(*num(c, 0))
                    kvw = kvl[:, 0:PR * VW].rearrange("p (r v) -> p r v", r=PR)
                    ev = evs[:, :].rearrange("p (r v) -> p r v", r=PR)
                    for k in range(2):
                        r = slice(k * DH, (k + 1) * DH)
                        dve.scalar_tensor_tensor(kvb[r, :, r], kvw[r, :, r], sfac[r, 0:1], ev[r, :, r],
                                                 ALU.mult, ALU.add)
                        last = dve.tensor_scalar(ksb[r, :, k:k + 1], kvw[r, :, P:VW], sfac[r, 0:1],
                                                 T * EPS_FEAT, ALU.mult, ALU.add)
                    last.then_inc(kvb_ok.sem, 1)

                def quotient(m, c):
                    dve.wait_ge(*num(c, m + 1))
                    dve.wait_ge(*at_ok(c, m))
                    dve.reciprocal(rd[:, :], banks[4][:, 0:8]).then_inc(rd_ok.sem, 1)
                    dve.wait_ge(*rd_ok(c, m + 1))
                    dve.wait_ge(*att(c, m - 1 if m >= 2 else 0))
                    dve.tensor_tensor(at[:, m % 2, :].rearrange("p (h k) -> p h k", h=8),
                                      bankC(f"n{m}")[:, :].rearrange("p (h k) -> p h k", h=8),
                                      inner(rd[:, :], DH), ALU.mult).then_inc(at_ok.sem, 1)

                def elu(f, d):
                    if f == 0:
                        dve.wait_ge(*w2ps(d, 0))
                    dve.wait_ge(*vb_ok(d, f + 1))
                    dve.wait_ge(*he(d, f - 1 if f >= 2 else 0))
                    dve.tensor_scalar(ee[:, f % 2, :], vb[:, f % 2, :], 0.0, None, ALU.min).then_inc(em_ok.sem, 1)
                    dve.wait_ge(*ee_ok(d, f + 1))
                    dve.scalar_tensor_tensor(hE[:, f, :], ee[:, f % 2, :], -1.0, vb[:, f % 2, :],
                                             ALU.add, ALU.max).then_inc(he.sem, 1)

                def gates(d):
                    lg = bankD("lg")[:, 0:J * E1].rearrange("p (j e) -> p j e", j=J)
                    dve.wait_ge(*lg_ok(d, 1))
                    hold(dve, passed)
                    for j in range(J):
                        last = dve.max(m8[:, j, :], lg[:, j, :])
                    cD.step(last)
                    hold(dve, passed)
                    for j in range(J):
                        last = dve.max_index(idx[:, j, :], m8[:, j, :], lg[:, j, :])
                    last.then_inc(gidx.sem, 1)
                    dve.wait_ge(*gidx(d, 1))
                    dve.wait_ge(*gex_ok(d, 0))
                    dve.tensor_tensor(gd[:, :], m8[:, :, 1], m8[:, :, 0], ALU.subtract).then_inc(gd_ok.sem, 1)
                    for k, oh in enumerate((oh1, oh2)):
                        cD.step(dve.tensor_tensor(oh[:, :, :], mid(iota[:, 0:E1], J),
                                                  idx[:, :, k:k + 1].to_broadcast([P, J, E1]), ALU.is_equal))
                    dve.wait_ge(*gex_ok(d, 1))
                    cD.step(dve.tensor_scalar(gsum[:, :], gex[:, :], 1.0, None, ALU.add))
                    cD.step(dve.reciprocal(gw1[:, :], gsum[:, :]))
                    cD.step(dve.tensor_tensor(gw2[:, :], gex[:, :], gw1[:, :], ALU.mult))
                    cD.step(dve.tensor_tensor(oh1[:, :, :], oh1[:, :, :], inner(gw1[:, :], E1), ALU.mult))
                    cD.step(dve.tensor_tensor(oh2[:, :, :], oh2[:, :, :], inner(gw2[:, :], E1), ALU.mult))
                    dve.wait_ge(*dtp(d, 0))
                    dve.tensor_tensor(disp[:, :, :], oh1[:, :, :], oh2[:, :, :], ALU.add).then_inc(disp_ok.sem, 1)

                def silu(q, d):
                    dve.wait_ge(*th_ok(d, q + 1))
                    dve.wait_ge(*hm_ok(d, q - 1 if q >= 2 else 0))
                    dve.scalar_tensor_tensor(sl[:, q % 2, :], th[:, q % 2, :], 1.0, bankD(f"x{q}")[:, :],
                                             ALU.add, ALU.mult).then_inc(sl_ok.sem, 1)
                    dve.wait_ge(*sl_ok(d, q + 1))
                    dve.wait_ge(*yps(d, q + 1))
                    if q == 0:
                        dve.wait_ge(*mo(d, 0))
                    dve.scalar_tensor_tensor(hm[:, q, :], sl[:, q % 2, :], 0.5, bankD(f"y{q}")[:, :],
                                             ALU.mult, ALU.mult).then_inc(hm_ok.sem, 1)

                def step(c, d):
                    cC.begin(c)
                    cD.begin(d)
                    for slot in range(SLOTS):
                        chunks = XQ.get(slot, ()) if d is not None else ()
                        if c is not None and slot == 0:
                            sum_keys(c)
                        if c is not None and slot < M:
                            exponent(slot, c)
                        if c is not None and slot == 1:
                            keys(c)
                        if c is not None and slot == SLOTS - 1:
                            dve.wait_ge(*wo_ok(c, M))
                            dve.wait_ge(*L5.turned(c, 0))
                            norm_stats(dve, L5, attn, c, passed)
                        if d is not None:
                            for f in WF.get(slot, ()):
                                elu(f, d)
                            if slot == 4:
                                dve.wait_ge(*w2ps(d, 1))
                                dve.wait_ge(*t6a(d, 0))
                                norm_stats(dve, L6, ffn, d, passed)
                            if slot == 6:
                                gates(d)
                        for q in chunks[:1]:
                            silu(q, d)
                        if c is not None and slot == SLOTS - 1:
                            norm_apply(dve, L5, attn, c)
                        for q in chunks[1:]:
                            silu(q, d)
                        if c is not None and at_slot(slot, 2) is not None:
                            quotient(at_slot(slot, 2), c)
                        if d is not None and slot == 4:
                            norm_apply(dve, L6, ffn, d)
                        if d is not None and slot == 5:
                            dve.wait_ge(*x3_ok(d, 1))
                            dve.wait_ge(*L7.turned(d, 0))
                            norm_dve(dve, L7, x3, d, passed)
                    if d is not None:
                        dve.wait_ge(*mo(d, 1))
                        dve.wait_ge(*ob_ok(d, 0))
                        dve.tensor_tensor(fo[:, :, :], ffn, mid(gab[:, 1, :], J), ALU.mult).then_inc(fin.sem, 1)

                sweep(dve, step)


def kernel(**inputs):
    import ml_dtypes
    import numpy as np
    import concourse.bacc as _bacc
    from concourse.bass_utils import run_bass_kernel_spmd as _run

    A = {k: np.asarray(v) for k, v in inputs.items()}

    def pack(where, width, parts):
        w = np.zeros((P, width), np.float32)
        for name, (first, n) in where.items():
            a = parts[name]
            r, a = a if isinstance(a, tuple) else (0, a)
            a = a.reshape(a.shape[0], -1)
            w[r:r + a.shape[0], first:first + a.shape[1]] = a
        return w

    def chunks(a, n):
        return a.reshape(n, P, -1).transpose(1, 0, 2)

    def blocks(a, n):
        w = np.zeros((n * a.shape[0], n * a.shape[1]), np.float32)
        for k in range(n):
            w[k * a.shape[0]:(k + 1) * a.shape[0], k * a.shape[1]:(k + 1) * a.shape[1]] = a
        return w

    ident = np.eye(P, dtype=np.float32)
    iota = np.tile(np.arange(E1, dtype=np.float32), (P, 1))
    keep = pack(KEEP, KEEP_N, {"ident": ident, "iota": iota, "wv": A["L1_attn_Wv"]})

    once = pack(ONCE, ONCE_N, {
        "wmod0": A["L0_wmod"], "wmod1": A["L1_wmod"], "c0": A["L0_c"].T, "c1": A["L1_c"].T,
        "wkT": chunks(A["L1_attn_Wk"].reshape(D, HD).T, PR), "wqT": chunks(A["L1_attn_Wq"].reshape(D, HD).T, PR),
        "proj": blocks(A["L1_attn_proj"].T, 2)})

    xp = A["L0_attn_x_proj_w"]
    xw = np.zeros((DI, P), np.float32)
    for k in range(3):
        xw[:, 32 * k:32 * k + 32] = xp[:, RK:]
    xw[:, 96:96 + RK] = xp[:, :RK]
    b2 = np.zeros((P, J, D), np.float32)
    for j in range(J):
        b2[32 * j:32 * j + E0, j, :] = A["L0_ffn_b2"]
    one = pack(ONE, ONE_N, {
        "inw": A["L0_attn_in_proj_w"],
        "convw": chunks(A["L0_attn_conv_w"][:, 0, :].T, G), "convb": chunks(A["L0_attn_conv_b"], G),
        "xw": chunks(xw, G), "dtw": (96, A["L0_attn_dt_proj_w"]), "dtb": chunks(A["L0_attn_dt_proj_b"], G),
        "alog": chunks(A["L0_attn_A_log"], G), "dskip": chunks(A["L0_attn_D"], G),
        "outw": chunks(A["L0_attn_out_proj_w"], G), "gate": A["L0_ffn_gate_w"].T,
        "w1": A["L0_ffn_w1"].transpose(1, 0, 2), "b1": A["L0_ffn_b1"].reshape(E0 * FC, P).T,
        "w2": A["L0_ffn_w2"].reshape(E0, FC, P, D).transpose(2, 0, 1, 3), "b2": b2, "wk": A["L1_attn_Wk"]})

    pick = np.zeros((E1, MC, P), np.float32)
    for r in range(MC):
        for k in range(2):
            pick[2 * r + k, r, k * HE:(k + 1) * HE] = 1.0
    mw2 = A["L1_ffn_w2"].transpose(0, 2, 1).reshape(E1 * HE, D)
    two = pack(TWO, TWO_N, {
        "wq": A["L1_attn_Wq"], "wo": chunks(A["L1_attn_Wo"].reshape(HD, D), PR), "w1": A["L1_attn_W1"],
        "b1": A["L1_attn_b1"].reshape(FC, P).T, "w2": chunks(A["L1_attn_W2"], FC),
        "b2": np.tile(A["L1_attn_b2"], J)[None], "g1": A["L1_attn_ln1_g"][:, None],
        "be1": A["L1_attn_ln1_b"][:, None], "g2": np.tile(A["L1_attn_ln2_g"], (P, 1)),
        "be2": np.tile(A["L1_attn_ln2_b"], (P, 1)), "gate": A["L1_ffn_gate_w"].T,
        "mw1": A["L1_ffn_w1"].reshape(E1 * HE, D).T, "mw2": chunks(mw2, MC),
        "s1": A["L1_ffn_sfc1"].T, "s2": A["L1_ffn_sfc2"].T, "s3": chunks(A["L1_ffn_sfc3"].T, SC), "pick": pick})

    pick16 = np.zeros((3 * 2 * NS, 2 * NS, P), ml_dtypes.bfloat16)
    for n in range(2 * NS):
        pick16[n::2 * NS, n, :] = 1.0

    arrays = {"x": np.ascontiguousarray(A["L0_attn_x"]), "keep": keep, "once": once, "one": one, "two": two,
              "pick16": pick16}
    nc = _bacc.Bacc("TRN2", target_bir_lowering=False, num_devices=1)
    args = [nc.dram_tensor(f"in_{n}", a.shape, mybir.dt.from_np(a.dtype), kind="ExternalInput").ap()
            for n, a in arrays.items()]
    out = nc.dram_tensor("out_0", (NB, T, D), F32, kind="ExternalOutput").ap()
    adaln_depth2(nc, *args, out)
    r = _run(nc, [{f"in_{n}": a for n, a in arrays.items()}], core_ids=[0])
    return r.results[0]["out_0"]
```

```python
from contextlib import ExitStack

import concourse.bass as bass
from concourse import mybir

F32 = mybir.dt.float32
F32R = mybir.dt.float32r
BF16 = mybir.dt.bfloat16
U32 = mybir.dt.uint32
ALU = mybir.AluOpType
ACT = mybir.ActivationFunctionType
AX = mybir.AxisListType
RMAX = bass.bass_isa.ReduceOp.max

P = 128
NB, T, D = 16, 512, 128
J = T // P
DI = 256
G = DI // P
NS = 16
RK = DI // 16
TAPS = 4
PAD = TAPS - 1
E0, FF = 8, 512
FC = FF // P
H, DH = 16, 64
HD = H * DH
PR = HD // P
VW = P + 1
E1, HE = 16, 64
MC = E1 * HE // P
SC = 256 // P
EPS_MOD = 1e-5
EPS_ENC = 1e-6
EPS_FEAT = 1e-6
DN = float(DH) ** -0.25
DIAG = DN * DN / 2.0
BIG = 3.0e38


def columns(parts):
    at, where = 0, {}
    for name, n in parts:
        where[name] = (at, n)
        at += n
    return where, at


KEEP, KEEP_N = columns([("ident", P), ("iota", E1), ("wv", HD)])
ONCE, ONCE_N = columns([("wmod0", 6 * D), ("wmod1", 6 * D), ("c0", NB), ("c1", NB),
                        ("wkT", HD), ("wqT", HD), ("proj", P)])
ONE, ONE_N = columns([("inw", 2 * DI), ("convw", G * TAPS), ("convb", G), ("xw", G * P), ("dtw", DI),
                      ("dtb", G), ("alog", G * NS), ("dskip", G), ("outw", G * D), ("gate", E0),
                      ("b1", E0 * FC), ("w2", E0 * FF), ("b2", J * D), ("wk", HD)])
TWO, TWO_N = columns([("wq", HD), ("mw1", E1 * HE), ("s1", SC * P), ("s2", SC * P), ("w1", FF),
                      ("wo", HD), ("b1", FC), ("w2", FF), ("b2", T),
                      ("g1", 1), ("be1", 1), ("g2", D), ("be2", D), ("gate", E1),
                      ("mw2", E1 * HE), ("s3", SC * D)])
SPLIT_N = TWO["wo"][0]


class Signal:

    def __init__(self, sem, per):
        self.sem, self.per = sem, per

    def __call__(self, batch, n):
        return self.sem, batch * self.per + n


class Chain:

    def __init__(self, eng, signal):
        self.eng, self.step_of, self.n, self.batch = eng, signal, 0, None

    def begin(self, batch):
        assert self.n in (0, self.step_of.per), (self.n, self.step_of.per)
        self.n, self.batch = 0, batch

    def step(self, ins):
        self.n += 1
        ins.then_inc(self.step_of.sem, 1)
        self.eng.wait_ge(*self.step_of(self.batch, self.n))


class Norm:

    def __init__(self, sb, sig, name, eps, xh=None):
        self.eps = eps
        self.st = sb(name + "_st", [P, J, 6])
        self.mv = sb(name + "_mv", [P, J, 2])
        self.ve = sb(name + "_ve", [P, J])
        self.rs = sb(name + "_rs", [P, J])
        self.xh = sb(name + "_xh", [P, J, D]) if xh is None else xh
        self.sums, self.stats, self.veps, self.rstd, self.xhat, self.turned, self.out = (
            sig(name + "_" + n, 1) for n in ("sums", "stats", "veps", "rstd", "xhat", "turned", "out"))


def hold(eng, passed):
    eng.sem_inc(passed, 1)


def norm_dve(dve, ln, src, it, passed):
    norm_stats(dve, ln, src, it, passed)
    norm_apply(dve, ln, src, it)


def norm_stats(dve, ln, src, it, passed):
    dve.wait_ge(*ln.xhat(it, 0))
    for j in range(J):
        last = dve.bn_stats(ln.st[:, j, :], src[:, j, :])
    last.then_inc(ln.sums.sem, 1)
    dve.wait_ge(*ln.sums(it, 1))
    hold(dve, passed)
    for j in range(J):
        last = dve.bn_aggr(ln.mv[:, j, :], ln.st[:, j, :])
    last.then_inc(ln.stats.sem, 1)


def norm_apply(dve, ln, src, it):
    dve.wait_ge(*ln.rstd(it, 1))
    for j in range(J):
        last = dve.tensor_scalar(ln.xh[:, j, :], src[:, j, :], ln.mv[:, j, 0:1], ln.rs[:, j:j + 1],
                                 ALU.subtract, ALU.mult)
    last.then_inc(ln.xhat.sem, 1)


def norm_pool(pool, ln, half, it, passed):
    pool.wait_ge(*ln.stats(it, 1))
    hold(pool, passed)
    pool.tensor_scalar(ln.ve[:, :], ln.mv[:, :, 1], ln.eps, None, ALU.add).then_inc(ln.veps.sem, 1)
    pool.wait_ge(*ln.veps(it, 1))
    pool.tensor_tensor(ln.rs[:, :], ln.ve[:, :], half[:, 0:J], ALU.pow).then_inc(ln.rstd.sem, 1)


def norm_pe(pe, ln, ps, ident, it):
    pe.wait_ge(*ln.xhat(it, 1))
    for j in range(J):
        last = pe.transpose(ps[:, j * P:(j + 1) * P], ln.xh[:, j, :], ident)
    last.then_inc(ln.turned.sem, 1)


def split_product(pe, dst, lhs, rhs):
    pe.matmul(dst, lhs[1], rhs[0], start=True, stop=False)
    pe.matmul(dst, lhs[0], rhs[1], start=False, stop=False)
    return pe.matmul(dst, lhs[0], rhs[0], start=False, stop=True)


def mid(ap, n):
    return ap.unsqueeze(1).to_broadcast([ap.shape[0], n, ap.shape[1]])


def inner(ap, m):
    return ap.unsqueeze(2).to_broadcast([ap.shape[0], ap.shape[1], m])


def adaln_depth2(nc, x, keep, once, one, up1, two, pick16, pickd, out):
    ctx = ExitStack()
    with ctx:
        held = []

        def sem(name):
            held.append(nc.alloc_semaphore(name=name))
            return held[-1]

        def end_part():
            nc.clear_and_free_semaphores(held)
            held.clear()
            nc.all_engine_barrier()

        def sig(name, per):
            return Signal(sem(name), per)

        def sbuf(stack):
            def sb(name, shape, dt=F32):
                return stack.enter_context(nc.sbuf_tensor(name, shape, dt))
            return sb

        x_v = x.rearrange("b (j p) d -> b p j d", p=P)
        out_v = out.rearrange("b (j p) d -> b p j d", p=P)
        gate_rows = nc.dram_tensor("gate_rows", (4, NB, D), F32, kind="Internal").ap()
        pq_dram = nc.dram_tensor("pq_dram", (P, HD), F32, kind="Internal").ap()
        x2_dram = nc.dram_tensor("x2_dram", (NB, P, J * D), F32, kind="Internal").ap()
        h3_dram = nc.dram_tensor("h3_dram", (NB, P, T), F32, kind="Internal").ap()
        kv_dram = nc.dram_tensor("kv_dram", (NB, P, PR * VW + 1), F32, kind="Internal").ap()

        kept = sbuf(ctx)
        keep_sb = kept("keep_sb", [P, KEEP_N])
        ident, iota, wv = (keep_sb[:, KEEP[n][0]:KEEP[n][0] + KEEP[n][1]] for n in ("ident", "iota", "wv"))
        modc = kept("modc", [P, 2, NB, 4])
        pk = kept("pk", [P, HD])
        ones = kept("ones", [P, P])
        half = kept("half", [P, 8])
        mxrun = kept("mxrun", [P, 1])
        nmx = kept("nmx", [P, 1])
        banks = [ctx.enter_context(nc.psum_tensor(f"bank{n}", [P, T], F32))[:, :] for n in range(2)]
        pair = ctx.enter_context(nc.psum_tensor("banks23", [P, 2, T], F32))
        banks += [pair[:, n, :] for n in range(2)]
        banks += [ctx.enter_context(nc.psum_tensor(f"bank{n}", [P, T], F32))[:, :] for n in range(4, 8)]

        with ExitStack() as part:
            sb = sbuf(part)
            once_sb = sb("once_sb", [P, ONCE_N])

            def W(name, a=0, b=None):
                at, n = ONCE[name]
                return once_sb[:, at + a:at + (n if b is None else b)]

            pq = sb("pq_folded", [P, HD])
            sc = sb("sc", [P, 2 * NB])
            gr_s = sb("gr_s", [NB, T])
            gr_m = sb("gr_m", [NB, T])
            gr = sb("gr", [NB, T])
            w_in, c_ready, fold, mods, gates, chain_s, gr_ready, gr_out, done_s, setup_dve = (
                sem(n) for n in ("setup_in", "c_ready", "folded", "mods", "gates", "gate_chain", "gate_rows_ready",
                                 "gate_rows_out", "folds_kept", "setup_dve"))
            with nc.Block() as block:
                @block.sync
                def _(sp):
                    sp.dma_start(once_sb[:, :], once).then_inc(w_in, 16)
                    sp.dma_start(keep_sb[:, :], keep).then_inc(w_in, 16)
                    sp.wait_ge(gr_ready, 1)
                    sp.dma_start(gate_rows.rearrange("r b d -> b r d"),
                                 gr[:, :].rearrange("b (r d) -> b r d", r=4)).then_inc(gr_out, 16)
                    sp.wait_ge(done_s, 4)
                    sp.dma_start(pq_dram, pq[:, :]).then_inc(gr_out, 16)
                    sp.wait_ge(gr_out, 32)

                @block.gpsimd
                def _(pool):
                    pool.memset(ones[:, :], 1.0)
                    pool.memset(half[:, :], -0.5)
                    pool.memset(mxrun[:, :], -BIG)

                @block.scalar
                def _(act):
                    act.wait_ge(w_in, 32)
                    act.activation(sc[:, :], W("c0", 0, 2 * NB), ACT.Silu).then_inc(c_ready, 1)
                    for n, dst in enumerate((pk, pk, pq, pq)):
                        act.wait_ge(fold, n + 1)
                        o = (n % 2) * T
                        act.activation(dst[:, o:o + T], banks[n][:, :], ACT.Copy, scale=DN).then_inc(done_s, 1)

                @block.tensor
                def _(pe):
                    pe.wait_ge(w_in, 32)
                    for n, src in enumerate(("wkT", "wkT", "wqT", "wqT")):
                        for k in range(PR // 2):
                            pr = (n % 2) * (PR // 2) + k
                            last = pe.matmul(banks[n][:, k * P:(k + 1) * P], W(src, pr * P, (pr + 1) * P),
                                             W("proj"), start=True, stop=True)
                        last.then_inc(fold, 1)
                    pe.wait_ge(c_ready, 1)
                    for l in range(2):
                        for k, col in enumerate((0, 1, 3, 4)):
                            at = (l * 4 + k) * NB
                            last = pe.matmul(banks[6][:, at:at + NB], W(f"wmod{l}", col * D, (col + 1) * D),
                                             sc[:, l * NB:(l + 1) * NB], start=True, stop=True)
                    last.then_inc(mods, 1)
                    for l in range(2):
                        for k, col in enumerate((2, 5)):
                            at = (l * 2 + k) * D
                            last = pe.matmul(banks[7][0:NB, at:at + D], sc[:, l * NB:(l + 1) * NB],
                                             W(f"wmod{l}", col * D, (col + 1) * D), start=True, stop=True)
                    last.then_inc(gates, 1)

                @block.vector
                def _(dve):
                    dve.wait_ge(mods, 1)
                    ps = banks[6][:, 0:2 * 4 * NB].rearrange("p (l k b) -> p l b k", l=2, k=4)
                    for l in range(2):
                        for k in range(4):
                            dve.tensor_scalar(modc[:, l, :, k], ps[:, l, :, k], float(k % 2), None, ALU.add)\
                               .then_inc(setup_dve, 1)
                    dve.wait_ge(gates, 1)
                    gp = banks[7][0:NB, :]
                    dve.tensor_scalar(gr_s[:, :], gp, 0.0, 2.0, ALU.is_ge, ALU.mult).then_inc(chain_s, 1)
                    dve.tensor_scalar(gr_m[:, :], gp, -1.0, None, ALU.mult).then_inc(chain_s, 1)
                    dve.wait_ge(chain_s, 2)
                    dve.tensor_tensor(gr_m[:, :], gr_m[:, :], gp, ALU.max).then_inc(chain_s, 1)
                    dve.wait_ge(chain_s, 3)
                    dve.tensor_scalar(gr_m[:, :], gr_m[:, :], 0.25, None, ALU.max).then_inc(chain_s, 1)
                    dve.wait_ge(chain_s, 4)
                    dve.scalar_tensor_tensor(gr[:, :], gr_s[:, :], -1.0, gr_m[:, :], ALU.add, ALU.mult)\
                       .then_inc(gr_ready, 1)

            end_part()

        with ExitStack() as part:
            sb = sbuf(part)
            one_sb = sb("one_sb", [P, ONE_N])

            def V1(name):
                at, n = ONE[name]
                return one_sb[:, at:at + n]

            inw, convb, dtb, dskip, alog, gatew, b1c = (V1(n) for n in ("inw", "convb", "dtb", "dskip", "alog",
                                                                       "gate", "b1"))
            convw = V1("convw").rearrange("p (g k) -> p g k", g=G)
            xw = V1("xw").rearrange("p (g m) -> p g m", g=G)
            dtw = V1("dtw")
            outw = V1("outw").rearrange("p (g d) -> p g d", g=G)
            w1_high = sb("w1_high", [P, E0 * FF], F32R)
            w1_low = sb("w1_low", [P, E0 * FF], F32R)
            w2 = V1("w2").rearrange("p (e f d) -> p e f d", e=E0, f=FC)
            b2 = V1("b2")
            wk = V1("wk")
            pick_sb = sb("pick_sb", [3 * 2 * NS, 2 * NS], BF16)
            aneg = sb("aneg", [P, G, NS])
            xs = sb("xs", [P, J, D])
            ga = sb("ga", [P, D])
            hT = sb("hT", [P, T])
            xpad = sb("xpad", [P, G, PAD + T])
            cv = sb("cv", [P, G, T])
            ax = cv
            zs = sb("zs", [P, G, T])
            xc = sb("xc", [P, G, T])
            S = sb("S", [P, T], BF16)
            R = sb("R", [P, T])
            dtr = R
            Rb = sb("Rb", [P, T], BF16)
            dt = sb("dt", [P, G, T])
            dtx = sb("dtx", [P, G, T])
            acc = sb("acc", [P, G, T])
            dec = sb("dec", [P, 2, G, T])
            u = sb("u", [P, G, T])
            yz = u
            h = sb("h", [P, G, T])
            zz = sb("zz", [P, 2, G, T])
            xh = sb("xh", [P, J, D])
            ao = xh
            x1 = sb("x1", [P, J, D])
            gb = sb("gb", [P, D])
            hT2 = sb("hT2", [P, T])
            hT2h = sb("hT2h", [P, T], F32R)
            hT2l = sb("hT2l", [P, T], F32R)
            m8 = sb("m8", [P, J, 8])
            idx = sb("idx", [P, J, 8], U32)
            oh = sb("oh", [P, J, E0])
            lm = sb("lm", [P, J, E0])
            ex = sb("ex", [P, J, E0])
            esum = sb("esum", [P, J])
            erec = sb("erec", [P, J])
            gp = sb("gp", [P, J, 32])
            gT = sb("gT", [P, P])
            hid = sb("hid", [P, 2, FC, T])
            prod = sb("prod", [P, 2, J, D])
            facc = sb("facc", [P, J, D])
            x2 = sb("x2", [P, J, D])
            hT3 = sb("hT3", [P, T])
            kvs = sb("kvs", [P, PR * VW + 1])
            sq = kvs[:, 0:2 * T].rearrange("p (n t) -> p n t", n=2)
            ssq = sb("ssq", [P, 2 * J, 8])
            mxs = sb("mxs", [P, 2 * J])
            bmx = sb("bmx", [P, 1])
            cb = sb("cb", [P, 1])
            ncb = sb("ncb", [P, 1])
            Ek = sb("Ek", [P, J, HD])
            V = sb("V", [P, J, PR, VW])

            w_in, a_exp, a_neg, init, passed, w_high, w_low = (
                sem(n) for n in ("w1_in", "a_exp", "a_neg", "init1", "passed1", "w1_high_ok", "w1_low_ok"))
            h2_high, h2_low = sig("h2_high", 1), sig("h2_low", 1)
            x_in, r_in, ga_in, gb_in, x2_out, h3_out, kv_out = (
                sig(n, 16) for n in ("x_in", "r_in", "ga_in", "gb_in", "x2_out", "h3_out", "kv_out"))
            L1, L2, L3 = (Norm(sb, sig, n, EPS_MOD, xh) for n in ("n1", "n2", "n3"))
            (in_done, xraw, zsilu, conv, xc_ok, xdbl, dtr_ok, s_hi, s_mid, s_rem, s_remb, s_lo, dtps, dtabs, dtexp,
             dtln, dtmax, dt_ok, dtx_ok, acc0, bb, cbc, dec_ok, u_ok, scan, z_ok, accum, yz_ok, oproj, ao_ok,
             x1_ok, chainA) = (sig(n, p) for n, p in (
                 ("in_done", 4), ("xraw", 2), ("zsilu", 2), ("conv", 2), ("xc_ok", 1), ("xdbl", 1), ("dtr_ok", 1),
                 ("s_hi", 1), ("s_mid", 1), ("s_rem", 1), ("s_remb", 1), ("s_lo", 1), ("dtps", 2), ("dtabs", 2),
                 ("dtexp", 1), ("dtln", 1), ("dtmax", 2), ("dt_ok", 1), ("dtx_ok", 1), ("acc0", 1), ("bb", NS),
                 ("cbc", NS), ("dec_ok", 2 * NS), ("u_ok", NS), ("scan", 2 * NS), ("z_ok", NS), ("accum", NS),
                 ("yz_ok", 1), ("oproj", 1), ("ao_ok", 1), ("x1_ok", 1), ("chainA", G * (TAPS - 1))))
            (logits, lshift, lexp, gw, gturn, gT_ok, b2ps, facc0, up, hid_ok, down, prod_ok, fadd, x2m, x2_ok,
             kps, dps, vps, sq_ok, ssum, ush, vc, bmx_ok, call, ncb_ok, mxr, kvc, kf, kv, kvs_ok, chainB) = (
                sig(n, p) for n, p in (
                    ("logits", 1), ("lshift", 1), ("lexp", 1), ("gw", 1), ("gturn", 1), ("gT_ok", 1), ("b2ps", 1),
                    ("facc0", 1), ("up", E0 * FC), ("hid_ok", E0 * FC), ("down", E0), ("prod_ok", E0), ("fadd", E0),
                    ("x2m", 1), ("x2_ok", 1), ("kps", 2 * J), ("dps", 2 * J), ("vps", 2 * J), ("sq_ok", 2 * J),
                    ("ssum", 2 * J), ("ush", 2 * J), ("vc", 2 * J), ("bmx_ok", 1), ("call", 1), ("ncb_ok", 1),
                    ("mxr", 1), ("kvc", 1), ("kf", J), ("kv", 1), ("kvs_ok", 3), ("chainB", 5 + 2 * J)))

            SLOTS = NS + 2
            END = SLOTS - 1
            UPS = {0: (0,), 1: (1, 2), 2: (3,), 3: (4,), 4: (5, 6), 5: (7,), 6: (8, 9), 7: (10, 11), 8: (12, 13),
                   9: (14, 15)}
            DOWNS = {2: 0, 3: 1, 5: 2, 6: 3, 7: 4, 8: 5, 9: 6, 10: 7}
            PRODS = {slot + 1: e for slot, e in DOWNS.items()}
            GATES = 2
            before_gates = 2 * sum(len(qs) for slot, qs in UPS.items() if slot <= GATES)
            NORM3 = 12
            KEYS_FROM = 13
            KEYS = {13: (0, 1), 14: (2, 3), 15: (4, 5), 16: (6, 7)}
            GATE = {4: 0, 5: 1}
            NORM1, TURN, SILU = 5, 6, 11
            XIN = {7: 0, 8: 1}
            CONV = {8: 0, 9: 1}

            uses = {n: [] for n in range(2, 7)}
            ring = [("oproj", ao_ok, 1), ("turn2", L2.out, 1)]
            ring += [(f"up{n}", hid_ok, n + 1) for n in range(before_gates)] + [("gates", gT_ok, 1)]
            ring += [(f"up{n}", hid_ok, n + 1) for n in range(before_gates, E0 * FC)] + [("turn3", L3.out, 1)]
            for n, entry in enumerate(ring):
                uses[2 + n % 3].append(entry)
            for e in range(E0):
                uses[5 + e % 2].append((f"down{e}", prod_ok, e + 1))
            keys = [(f"{name}{m}", done, m + 1) for m in range(2 * J)
                    for name, done in (("k", sq_ok), ("d", ush), ("v", vc))]
            for n, entry in enumerate(keys):
                uses[2 + (n + 3) % 5].append(entry)
            for n in range(2):
                uses[5 + n].append((f"kv{n}", kvs_ok, n + 1))
            bank_of = {entry[0]: n for n, entries in uses.items() for entry in entries}

            def bank1(name):
                return banks[bank_of[name]][:, :]

            def free1(pe, name, b):
                entries = uses[bank_of[name]]
                n = [entry[0] for entry in entries].index(name)
                if n > 0:
                    _, done, count = entries[n - 1]
                    pe.wait_ge(*done(b, count))
                elif not isinstance(b, int) or b > 0:
                    _, done, count = entries[-1]
                    pe.wait_ge(*done(b - 1, count))

            def sweep(eng, step):
                step(None, None, 0)
                step(0, None, 1)
                step(1, 0, 2)
                with eng.Fori(2, NB - 1) as i:
                    step(i, i - 1, i + 1)
                step(NB - 1, NB - 2, None)
                step(None, NB - 1, None)

            with nc.Block() as block:
                @block.sync
                def _(sp):
                    sp.dma_start(one_sb[:, :], one).then_inc(w_in, 16)
                    sp.dma_start(pick_sb[:, :], pick16).then_inc(w_in, 16)
                    sp.dma_start(Ek[:, :, :].rearrange("p j n -> p (j n)"), up1).then_inc(w_in, 16)

                    def step(a, b, n):
                        if n is not None:
                            sp.wait_ge(*L1.xhat(n, 0))
                            sp.dma_start(xs[:, :, :], x_v[n]).then_inc(x_in.sem, 16)
                        if a is not None:
                            sp.wait_ge(*ao_ok(a, 0))
                            sp.dma_start(ga[:, :], gate_rows[0, a].partition_broadcast(P)).then_inc(ga_in.sem, 16)
                        if b is not None:
                            sp.wait_ge(*x2_ok(b, 0))
                            sp.dma_start(gb[:, :], gate_rows[1, b].partition_broadcast(P)).then_inc(gb_in.sem, 16)
                            sp.wait_ge(*x2_ok(b, 1))
                            sp.dma_start(x2_dram[b], x2[:, :, :].rearrange("p j d -> p (j d)"))\
                              .then_inc(x2_out.sem, 16)
                        if a is not None:
                            sp.dma_start(x1[:, :, :], x_v[a]).then_inc(r_in.sem, 16)
                        if b is not None:
                            sp.wait_ge(*L3.out(b, 1))
                            sp.dma_start(h3_dram[b], hT3[:, :]).then_inc(h3_out.sem, 16)

                    sweep(sp, step)
                    sp.wait_ge(*x2_out(NB, 0))
                    sp.wait_ge(*h3_out(NB, 0))
                    sp.wait_ge(*kv_out(NB, 0))

                staged = Ek[:, :, :].rearrange("p j n -> p (j n)")

                @block.scalar
                def _(act):
                    act.wait_ge(w_in, 48)
                    act.activation(aneg[:, :, :].rearrange("p g n -> p (g n)"), alog, ACT.Exp).then_inc(a_exp, 1)
                    act.wait_ge(a_neg, 1)
                    for n in range(E0):
                        act.activation(w1_high[:, n * FF:(n + 1) * FF], staged[:, n * FF:(n + 1) * FF], ACT.Copy)\
                            .then_inc(w_high, 1)
                    act.wait_ge(init, 3)

                    def modulate1(n):
                        act.wait_ge(*L1.turned(n, 1))
                        act.wait_ge(*in_done(n, 0))
                        act.activation(hT[:, :], banks[7][:, :], ACT.Identity, scale=modc[:, 0, n, 1:2],
                                       bias=modc[:, 0, n, 0:1]).then_inc(L1.out.sem, 1)

                    def keep_x(g, n):
                        act.wait_ge(*in_done(n, g + 1))
                        act.wait_ge(*conv(n, 0))
                        act.activation(xpad[:, g, PAD:], banks[7][:, :], ACT.Copy).then_inc(xraw.sem, 1)

                    def silu_x(n):
                        act.wait_ge(*conv(n, G))
                        act.wait_ge(*acc0(n, 0))
                        act.wait_ge(*dtx_ok(n, 0))
                        act.activation(xc[:, :, :], cv[:, :, :], ACT.Silu).then_inc(xc_ok.sem, 1)

                    def silu_z(g, a):
                        act.wait_ge(*in_done(a, G + g + 1))
                        act.wait_ge(*yz_ok(a, 0))
                        act.activation(zs[:, g, :], banks[7][:, :], ACT.Silu).then_inc(zsilu.sem, 1)

                    def split_x(n):
                        act.wait_ge(*xdbl(n, 1))
                        act.wait_ge(*dtps(n, 0))
                        act.activation(dtr[96:96 + RK, :], banks[0][96:96 + RK, :], ACT.Copy).then_inc(dtr_ok.sem, 1)
                        act.wait_ge(*cbc(n, 0))
                        act.activation(S[0:96, :], banks[0][0:96, :], ACT.Copy).then_inc(s_hi.sem, 1)

                    def round_rest(n):
                        act.wait_ge(*s_rem(n, 1))
                        act.activation(Rb[64:96, :], R[64:96, :], ACT.Copy).then_inc(s_remb.sem, 1)

                    def magnitude(g, n):
                        act.wait_ge(*dtps(n, g + 1))
                        act.wait_ge(*xc_ok(n, 1))
                        act.activation(ax[:, g, :], banks[1 - g][:, :], ACT.Abs, bias=dtb[:, g:g + 1])\
                            .then_inc(dtabs.sem, 1)

                    def softplus(n):
                        act.wait_ge(*dtabs(n, G))
                        act.activation(ax[:, :, :], ax[:, :, :], ACT.Exp, scale=-1.0).then_inc(dtexp.sem, 1)
                        act.wait_ge(*dtexp(n, 1))
                        act.activation(ax[:, :, :], ax[:, :, :], ACT.Ln, bias=1.0).then_inc(dtln.sem, 1)

                    def skip(a):
                        act.wait_ge(*yz_ok(a, 0))
                        for g in range(G):
                            last = act.activation(acc[:, g, :], xc[:, g, :], ACT.Copy, scale=dskip[:, g:g + 1])
                        last.then_inc(acc0.sem, 1)

                    def decay(k, a):
                        if k == 0:
                            act.wait_ge(*dt_ok(a, 1))
                        act.wait_ge(*scan(a, G * (k - 1) if k >= 2 else 0))
                        for g in range(G):
                            act.activation(dec[:, k % 2, g, :], dt[:, g, :], ACT.Exp,
                                           scale=aneg[:, g, k:k + 1]).then_inc(dec_ok.sem, 1)

                    def modulate2(b):
                        act.wait_ge(*L2.turned(b, 1))
                        act.wait_ge(*up(b, 0))
                        act.activation(hT2[:, :], bank1("turn2"), ACT.Identity, scale=modc[:, 0, b, 3:4],
                                       bias=modc[:, 0, b, 2:3]).then_inc(L2.out.sem, 1)
                        act.wait_ge(*L2.out(b, 1))
                        act.activation(hT2h[:, :], hT2[:, :], ACT.Copy).then_inc(h2_high.sem, 1)

                    def gate_exp(b):
                        act.wait_ge(*lshift(b, 1))
                        act.activation(ex[:, :, :], lm[:, :, :], ACT.Exp).then_inc(lexp.sem, 1)

                    def keep_gates(b):
                        act.wait_ge(*gturn(b, 1))
                        act.wait_ge(*b2ps(b, 0))
                        act.activation(gT[:, :], bank1("gates")[:, 0:P], ACT.Copy).then_inc(gT_ok.sem, 1)

                    def relu(n, b):
                        e, f = divmod(n, FC)
                        act.wait_ge(*up(b, n + 1))
                        act.wait_ge(*down(b, e - 1 if e >= 2 else 0))
                        act.activation(hid[:, e % 2, f, :], bank1(f"up{n}"), ACT.Relu,
                                       bias=b1c[:, n:n + 1]).then_inc(hid_ok.sem, 1)

                    def modulate3(b):
                        act.wait_ge(*L3.turned(b, 1))
                        act.wait_ge(*vps(b, 0))
                        act.wait_ge(*h3_out(b, 0))
                        act.activation(hT3[:, :], bank1("turn3"), ACT.Identity, scale=modc[:, 1, b, 1:2],
                                       bias=modc[:, 1, b, 0:1]).then_inc(L3.out.sem, 1)

                    def key_tile(m, b):
                        j, s = divmod(m, 2)
                        act.wait_ge(*kps(b, m + 1))
                        act.wait_ge(*ssum(b, m - 1 if m >= 2 else 0))
                        if m < 2:
                            act.wait_ge(*kv_out(b, 0))
                        act.activation(sq[:, m % 2, :], bank1(f"k{m}"), ACT.Square).then_inc(sq_ok.sem, 1)
                        act.wait_ge(*vps(b, m + 1))
                        act.wait_ge(*kv(b, 0))
                        act.activation(V[:, j, 4 * s:4 * s + 4, 0:P],
                                       bank1(f"v{m}").rearrange("p (r d) -> p r d", r=4),
                                       ACT.Copy).then_inc(vc.sem, 1)

                    def key_exp(j, b):
                        act.wait_ge(*ncb_ok(b, 1))
                        act.wait_ge(*ush(b, 2 * J))
                        act.activation(Ek[:, j, :], Ek[:, j, :], ACT.Exp, bias=ncb[:, 0:1]).then_inc(kf.sem, 1)

                    def keep_sums(b):
                        act.wait_ge(*kv(b, 1))
                        act.wait_ge(*ssum(b, 2 * J))
                        act.wait_ge(*kv_out(b, 0))
                        for n, (first, count) in enumerate(((0, 3), (3, 3), (6, 2))):
                            act.activation(kvs[:, first * VW:(first + count) * VW],
                                           banks[5 + n][:, 0:count * VW], ACT.Copy).then_inc(kvs_ok.sem, 1)
                        act.wait_ge(*kvs_ok(b, 3))
                        act.wait_ge(*kvc(b, 1))
                        act.dma_start(kv_dram[b], kvs[:, :]).then_inc(kv_out.sem, 16)

                    def step(a, b, n):
                        for slot in range(END):
                            if b is not None:
                                if slot == 1:
                                    gate_exp(b)
                                if slot == GATES:
                                    keep_gates(b)
                                for q in UPS.get(slot, ()):
                                    relu(2 * q, b)
                                    relu(2 * q + 1, b)
                                for m in KEYS.get(slot, ())[:1]:
                                    key_tile(m, b)
                            if a is not None and slot + 1 <= NS - 1:
                                decay(slot + 1, a)
                            if b is not None and slot == NORM3:
                                modulate3(b)
                            if n is not None and slot == NS:
                                split_x(n)
                            if b is not None:
                                for m in KEYS.get(slot, ())[1:]:
                                    key_tile(m, b)
                            if a is not None and slot in GATE:
                                silu_z(GATE[slot], a)
                            if n is not None:
                                if slot == TURN:
                                    modulate1(n)
                                if slot in XIN:
                                    keep_x(XIN[slot], n)
                                if slot == SILU:
                                    silu_x(n)
                        if n is not None:
                            round_rest(n)
                            magnitude(0, n)
                            magnitude(1, n)
                            softplus(n)
                        if b is not None:
                            for j in range(J):
                                key_exp(j, b)
                        if n is not None:
                            decay(0, n)
                        if a is not None:
                            modulate2(a)
                        if n is not None:
                            skip(n)
                        if b is not None:
                            keep_sums(b)

                    sweep(act, step)

                @block.gpsimd
                def _(pool):
                    pool.memset(xpad[:, :, 0:PAD], 0.0).then_inc(init, 1)
                    pool.memset(V[:, :, :, P:VW], 1.0).then_inc(init, 1)
                    pool.memset(gp[:, :, :], 0.0).then_inc(init, 1)

                    def add_state(k, a):
                        if k == 0:
                            pool.wait_ge(*acc0(a, 1))
                        pool.wait_ge(*z_ok(a, k + 1))
                        pool.wait_ge(*accum(a, k))
                        pool.tensor_tensor(acc[:, :, :], acc[:, :, :], zz[:, k % 2, :, :], ALU.add)\
                            .then_inc(accum.sem, 1)

                    def add_expert(e, b):
                        pool.wait_ge(*prod_ok(b, e + 1))
                        if e == 0:
                            pool.wait_ge(*facc0(b, 1))
                        pool.wait_ge(*fadd(b, e))
                        pool.tensor_tensor(facc[:, :, :], facc[:, :, :], prod[:, e % 2, :, :], ALU.add)\
                            .then_inc(fadd.sem, 1)

                    def second_residual(b):
                        pool.wait_ge(*fadd(b, E0))
                        pool.wait_ge(*gb_in(b, 16))
                        pool.tensor_tensor(facc[:, :, :], facc[:, :, :], mid(gb[:, :], J), ALU.mult)\
                            .then_inc(x2m.sem, 1)
                        pool.wait_ge(*x2m(b, 1))
                        pool.wait_ge(*x2_out(b, 0))
                        pool.wait_ge(*L3.xhat(b, 0))
                        pool.tensor_tensor(x2[:, :, :], x1[:, :, :], facc[:, :, :], ALU.add).then_inc(x2_ok.sem, 1)

                    def largest_key(b):
                        pool.wait_ge(*bmx_ok(b, 1))
                        pool.wait_ge(*kf(b, 0))
                        pool.wait_ge(*kvc(b, 0))
                        hold(pool, passed)
                        pool.partition_all_reduce(cb[:, :], bmx[:, :], P, RMAX).then_inc(call.sem, 1)
                        pool.wait_ge(*call(b, 1))
                        hold(pool, passed)
                        pool.tensor_scalar(ncb[:, :], cb[:, :], -1.0, None, ALU.mult).then_inc(ncb_ok.sem, 1)
                        pool.wait_ge(*mxr(b, 0))
                        hold(pool, passed)
                        pool.tensor_scalar(mxrun[:, :], mxrun[:, :], cb[:, 0:1], None, ALU.max).then_inc(mxr.sem, 1)
                        pool.wait_ge(*kv_out(b, 0))
                        hold(pool, passed)
                        pool.tensor_copy(kvs[:, PR * VW:], cb[:, :]).then_inc(kvc.sem, 1)

                    def step(a, b, n):
                        for slot in range(END):
                            if b is not None:
                                if slot in PRODS:
                                    add_expert(PRODS[slot], b)
                                if slot == max(PRODS):
                                    second_residual(b)
                                if slot == NORM3:
                                    norm_pool(pool, L3, half, b, passed)
                            if n is not None and slot == NORM1:
                                norm_pool(pool, L1, half, n, passed)
                            if a is not None and slot > 0:
                                add_state(slot - 1, a)
                        if b is not None:
                            largest_key(b)
                        if a is not None:
                            norm_pool(pool, L2, half, a, passed)

                    sweep(pool, step)

                @block.tensor
                def _(pe):
                    pe.wait_ge(w_in, 48)
                    pe.wait_ge(w_low, E0)

                    def turn1(a, n):
                        if a is not None:
                            pe.wait_ge(*zsilu(a, G))
                        norm_pe(pe, L1, banks[7], ident, n)

                    def in_proj(c, n):
                        pe.matmul(banks[7][:, :], inw[:, c * P:(c + 1) * P], hT[:, :],
                                  start=True, stop=True).then_inc(in_done.sem, 1)

                    def x_proj(a, n):
                        pe.wait_ge(*xc_ok(n, 1))
                        if a is not None:
                            pe.wait_ge(*u_ok(a, NS))
                        for g in range(G):
                            last = pe.matmul(banks[0][:, :], xw[:, g, :], xc[:, g, :],
                                             start=(g == 0), stop=(g == G - 1))
                        last.then_inc(xdbl.sem, 1)

                    def dt_proj(g, a, n):
                        pe.wait_ge(*dtr_ok(n, 1))
                        if g == 0:
                            if a is not None:
                                pe.wait_ge(*z_ok(a, NS))
                        else:
                            pe.wait_ge(*s_hi(n, 1))
                            pe.wait_ge(*s_rem(n, 1))
                        pe.matmul(banks[1 - g][:, :], dtw[96:96 + RK, g * P:(g + 1) * P],
                                  dtr[96:96 + RK, :], start=True, stop=True).then_inc(dtps.sem, 1)

                    def spread(k, which, a):
                        if k == 0:
                            pe.wait_ge(*s_mid(a, 1))
                            pe.wait_ge(*s_lo(a, 1))
                            pe.wait_ge(*dtmax(a, 2 - which))
                        else:
                            pe.wait_ge(*(z_ok if which else u_ok)(a, k))
                        at = which * NS + k
                        pe.matmul(banks[which][:, :], pick_sb[:, at:at + 1].to_broadcast([96, P]), S[0:96, :],
                                  start=True, stop=True).then_inc((cbc if which else bb).sem, 1)

                    def out_proj(a):
                        free1(pe, "oproj", a)
                        pe.wait_ge(*yz_ok(a, 1))
                        for j in range(J):
                            for g in range(G):
                                last = pe.matmul(bank1("oproj")[:, j * D:(j + 1) * D], yz[:, g, j * P:(j + 1) * P],
                                                 outw[:, g, :], start=(g == 0), stop=(g == G - 1))
                        last.then_inc(oproj.sem, 1)

                    def turn2(a):
                        free1(pe, "turn2", a)
                        norm_pe(pe, L2, banks[bank_of["turn2"]], ident, a)

                    def gate_logits(a, b):
                        pe.wait_ge(*kvs_ok(b, 0))
                        if a is not None:
                            pe.wait_ge(*xraw(a, G))
                        pe.wait_ge(*L2.out(b, 1))
                        for j in range(J):
                            last = pe.matmul(banks[7][:, j * E0:(j + 1) * E0], hT2[:, j * P:(j + 1) * P],
                                             gatew, start=True, stop=True)
                        last.then_inc(logits.sem, 1)

                    def turn_gates(b):
                        pe.wait_ge(*gw(b, 1))
                        free1(pe, "gates", b)
                        pe.transpose(bank1("gates")[:, 0:P], gp[:, :, :].rearrange("p j e -> p (j e)"),
                                     ident).then_inc(gturn.sem, 1)

                    def biases(b):
                        pe.wait_ge(*gT_ok(b, 1))
                        pe.wait_ge(*lshift(b, 1))
                        pe.matmul(banks[7][:, :], gT[:, :], b2, start=True, stop=True).then_inc(b2ps.sem, 1)

                    def ups(q, b):
                        for n in range(2 * q, 2 * q + 2):
                            e, f = divmod(n, FC)
                            free1(pe, f"up{n}", b)
                            first = e * FF + f * P
                            split_product(pe, bank1(f"up{n}"), (w1_high[:, first:first + P],
                                                                w1_low[:, first:first + P]),
                                          (hT2h[:, :], hT2l[:, :])).then_inc(up.sem, 1)

                    def downs(e, b):
                        pe.wait_ge(*hid_ok(b, FC * (e + 1)))
                        free1(pe, f"down{e}", b)
                        for j in range(J):
                            for f in range(FC):
                                last = pe.matmul(bank1(f"down{e}")[:, j * D:(j + 1) * D],
                                                 hid[:, e % 2, f, j * P:(j + 1) * P], w2[:, e, f, :],
                                                 start=(f == 0), stop=(f == FC - 1))
                        last.then_inc(down.sem, 1)

                    def turn3(b):
                        free1(pe, "turn3", b)
                        norm_pe(pe, L3, banks[bank_of["turn3"]], ident, b)

                    def key_tile(m, b):
                        j, s = divmod(m, 2)
                        if m == 0:
                            pe.wait_ge(*L3.out(b, 1))
                        for name, w, done in (("k", wk, kps), ("d", pk[:, :], dps), ("v", wv, vps)):
                            free1(pe, f"{name}{m}", b)
                            pe.matmul(bank1(f"{name}{m}"), hT3[:, j * P:(j + 1) * P],
                                      w[:, s * T:(s + 1) * T], start=True, stop=True).then_inc(done.sem, 1)

                    def key_sums(j, a, b, n):
                        if j == 0:
                            free1(pe, "kv0", b)
                            free1(pe, "kv1", b)
                            pe.wait_ge(*facc0(b, 1))
                            if a is not None:
                                pe.wait_ge(*zsilu(a, G))
                            if n is not None:
                                pe.wait_ge(*xraw(n, G))
                            pe.wait_ge(*vc(b, 2 * J))
                        pe.wait_ge(*kf(b, j + 1))
                        for pr in range(PR):
                            at = (pr % 3) * VW
                            last = pe.matmul(banks[5 + pr // 3][:, at:at + VW],
                                             Ek[:, j, pr * P:(pr + 1) * P], V[:, j, pr, :],
                                             start=(j == 0 and pr % 3 == 0), stop=(j == J - 1),
                                             skip_group_check=True)
                        if j == J - 1:
                            last.then_inc(kv.sem, 1)

                    def step(a, b, n):
                        for slot in range(END):
                            k = slot - 1
                            if a is not None and k > 0:
                                spread(k, 1, a)
                            tiles = KEYS.get(slot, ()) if b is not None else ()
                            if b is not None:
                                if slot == 0:
                                    pe.wait_ge(*h2_low(b, 1))
                                for q in UPS.get(slot, ()):
                                    ups(q, b)
                                if slot == 0:
                                    gate_logits(a, b)
                                if slot == GATES:
                                    turn_gates(b)
                            for m in tiles[:1]:
                                key_tile(m, b)
                            if a is not None and 0 < k + 1 < NS:
                                spread(k + 1, 0, a)
                            if n is not None and slot == NS:
                                x_proj(a, n)
                            for m in tiles[1:]:
                                key_tile(m, b)
                            if b is not None:
                                if slot in DOWNS:
                                    downs(DOWNS[slot], b)
                                if slot == GATES:
                                    biases(b)
                                if slot == NORM3:
                                    turn3(b)
                            if a is not None and slot in GATE:
                                if GATE[slot] > 0:
                                    pe.wait_ge(*zsilu(a, GATE[slot]))
                                elif b is not None:
                                    pe.wait_ge(*facc0(b, 1))
                                else:
                                    pe.wait_ge(*xraw(a, G))
                                in_proj(G + GATE[slot], a)
                            if n is not None:
                                if slot == TURN:
                                    turn1(a, n)
                                if slot in XIN:
                                    if XIN[slot] == 0:
                                        pe.wait_ge(*L1.out(n, 1))
                                    else:
                                        pe.wait_ge(*xraw(n, XIN[slot]))
                                    in_proj(XIN[slot], n)
                        if n is not None:
                            dt_proj(0, a, n)
                            dt_proj(1, a, n)
                        if a is not None:
                            out_proj(a)
                        if b is not None:
                            key_sums(0, a, b, n)
                            key_sums(1, a, b, n)
                        if n is not None:
                            spread(0, 0, n)
                            spread(0, 1, n)
                        if b is not None:
                            key_sums(2, a, b, n)
                        if a is not None:
                            turn2(a)
                        if b is not None:
                            key_sums(3, a, b, n)

                    sweep(pe, step)

                @block.vector
                def _(dve):
                    dve.wait_ge(a_exp, 1)
                    dve.tensor_scalar(aneg[:, :, :], aneg[:, :, :], -1.0, None, ALU.mult).then_inc(a_neg, 1)
                    dve.wait_ge(init, 3)
                    for n in range(E0):
                        dve.wait_ge(w_high, n + 1)
                        part_n = slice(n * FF, (n + 1) * FF)
                        dve.tensor_tensor(w1_low[:, part_n], staged[:, part_n], w1_high[:, part_n].bitcast(F32),
                                          ALU.subtract).then_inc(w_low, 1)
                    cA, cB = Chain(dve, chainA), Chain(dve, chainB)

                    def convolve(g, n):
                        if g == 0:
                            dve.wait_ge(*xc_ok(n, 0))
                            dve.wait_ge(*dt_ok(n, 0))
                        dve.wait_ge(*xraw(n, g + 1))
                        cA.step(dve.tensor_scalar(cv[:, g, :], xpad[:, g, PAD:], convw[:, g, PAD:],
                                                  convb[:, g:g + 1], ALU.mult, ALU.add))
                        for k in range(PAD):
                            ins = dve.scalar_tensor_tensor(cv[:, g, :], xpad[:, g, k:k + T],
                                                           convw[:, g, k:k + 1], cv[:, g, :],
                                                           ALU.mult, ALU.add)
                            if k < PAD - 1:
                                cA.step(ins)
                            else:
                                ins.then_inc(conv.sem, 1)

                    def split_mid(n):
                        dve.wait_ge(*s_hi(n, 1))
                        dve.tensor_tensor(S[32:64, :], banks[0][32:64, :], S[32:64, :], ALU.subtract)\
                           .then_inc(s_mid.sem, 1)
                        dve.wait_ge(*s_lo(n, 0))
                        dve.tensor_tensor(R[64:96, :], banks[0][64:96, :], S[64:96, :], ALU.subtract)\
                           .then_inc(s_rem.sem, 1)

                    def split_low(n):
                        dve.wait_ge(*s_remb(n, 1))
                        dve.tensor_tensor(S[64:96, :], R[64:96, :], Rb[64:96, :], ALU.subtract)\
                           .then_inc(s_lo.sem, 1)

                    def positive(g, n):
                        dve.wait_ge(*dec_ok(n, 0))
                        dve.wait_ge(*dtx_ok(n, 0))
                        dve.wait_ge(*dtabs(n, g + 1))
                        dve.tensor_scalar(dt[:, g, :], banks[1 - g][:, :], dtb[:, g:g + 1], 0.0,
                                          ALU.add, ALU.max).then_inc(dtmax.sem, 1)

                    def softplus(a):
                        dve.wait_ge(*dtln(a, 1))
                        dve.wait_ge(*dtmax(a, G))
                        dve.tensor_tensor(dt[:, :, :], dt[:, :, :], ax[:, :, :], ALU.add).then_inc(dt_ok.sem, 1)
                        dve.wait_ge(*dt_ok(a, 1))
                        dve.tensor_tensor(dtx[:, :, :], dt[:, :, :], xc[:, :, :], ALU.mult).then_inc(dtx_ok.sem, 1)
                        dve.wait_ge(*dtx_ok(a, 1))
                        dve.wait_ge(*oproj(a, 0))

                    def state_input(k, a):
                        dve.wait_ge(*bb(a, k + 1))
                        dve.wait_ge(*scan(a, G * k))
                        dve.tensor_tensor(u[:, :, :], dtx[:, :, :], mid(banks[0][:, :], G), ALU.mult)\
                           .then_inc(u_ok.sem, 1)

                    def scans(k, a):
                        dve.wait_ge(*u_ok(a, k + 1))
                        dve.wait_ge(*z_ok(a, k))
                        for g in range(G):
                            dve.wait_ge(*dec_ok(a, G * k + g + 1))
                            dve.tensor_tensor_scan(h[:, g, :], dec[:, k % 2, g, :], u[:, g, :], 0.0,
                                                   ALU.mult, ALU.add).then_inc(scan.sem, 1)

                    def weigh(k, a):
                        dve.wait_ge(*scan(a, G * (k + 1)))
                        dve.wait_ge(*cbc(a, k + 1))
                        dve.wait_ge(*accum(a, k - 1 if k >= 2 else 0))
                        dve.tensor_tensor(zz[:, k % 2, :, :], h[:, :, :], mid(banks[1][:, :], G), ALU.mult)\
                           .then_inc(z_ok.sem, 1)

                    def gated(a):
                        dve.wait_ge(*accum(a, NS))
                        dve.wait_ge(*zsilu(a, G))
                        dve.tensor_tensor(yz[:, :, :], acc[:, :, :], zs[:, :, :], ALU.mult).then_inc(yz_ok.sem, 1)

                    def first_residual(a, b, n):
                        dve.wait_ge(*oproj(a, 1))
                        dve.wait_ge(*ga_in(a, 16))
                        dve.wait_ge(*x1_ok(a, 0))
                        if b is not None:
                            dve.wait_ge(*L3.turned(b, 1))
                        if n is not None:
                            dve.wait_ge(*L1.turned(n, 1))
                        dve.tensor_tensor(ao[:, :, :], bank1("oproj").rearrange("p (j d) -> p j d", j=J),
                                          mid(ga[:, :], J), ALU.mult).then_inc(ao_ok.sem, 1)
                        dve.wait_ge(*ao_ok(a, 1))
                        dve.wait_ge(*r_in(a, 16))
                        dve.tensor_tensor(x1[:, :, :], x1[:, :, :], ao[:, :, :], ALU.add).then_inc(x1_ok.sem, 1)

                    def gates(b):
                        dve.wait_ge(*logits(b, 1))
                        lg = banks[7][:, 0:J * E0].rearrange("p (j e) -> p j e", j=J)
                        hold(dve, passed)
                        for j in range(J):
                            last = dve.max(m8[:, j, :], lg[:, j, :])
                        cB.step(last)
                        hold(dve, passed)
                        for j in range(J):
                            last = dve.max_index(idx[:, j, :], m8[:, j, :], lg[:, j, :])
                        cB.step(last)
                        dve.wait_ge(*gw(b, 0))
                        cB.step(dve.tensor_tensor(oh[:, :, :], mid(iota[:, 0:E0], J),
                                                  idx[:, :, 0:1].to_broadcast([P, J, E0]), ALU.is_equal))
                        dve.wait_ge(*lexp(b, 0))
                        dve.tensor_tensor(lm[:, :, :], lg, m8[:, :, 0:1].to_broadcast([P, J, E0]),
                                          ALU.subtract).then_inc(lshift.sem, 1)
                        dve.wait_ge(*lexp(b, 1))
                        cB.step(dve.tensor_reduce(esum[:, :], ex[:, :, :], AX.X, ALU.add))
                        cB.step(dve.reciprocal(erec[:, :], esum[:, :]))
                        dve.wait_ge(*gturn(b, 0))
                        dve.wait_ge(*prod_ok(b, 0))
                        dve.tensor_tensor(gp[:, :, 0:E0], oh[:, :, :], inner(erec[:, :], E0),
                                          ALU.mult).then_inc(gw.sem, 1)
                        dve.wait_ge(*gw(b, 1))

                    def keep_biases(b):
                        dve.wait_ge(*b2ps(b, 1))
                        dve.wait_ge(*x2_ok(b, 0))
                        dve.tensor_copy(facc[:, :, :].rearrange("p j d -> p (j d)"), banks[7][:, :])\
                           .then_inc(facc0.sem, 1)

                    def weighted(e, b):
                        dve.wait_ge(*down(b, e + 1))
                        dve.wait_ge(*fadd(b, e - 1 if e >= 2 else 0))
                        dve.tensor_tensor(prod[:, e % 2, :, :],
                                          bank1(f"down{e}").rearrange("p (j d) -> p j d", j=J),
                                          gp[:, :, e:e + 1].to_broadcast([P, J, D]), ALU.mult)\
                           .then_inc(prod_ok.sem, 1)

                    def key_tile(m, b):
                        j, s = divmod(m, 2)
                        dash = bank1(f"d{m}").rearrange("p (h k) -> p h k", h=8)
                        dve.wait_ge(*sq_ok(b, m + 1))
                        dve.tensor_reduce(ssq[:, m, :], sq[:, m % 2, :].rearrange("p (h k) -> p h k", h=8),
                                          AX.X, ALU.add).then_inc(ssum.sem, 1)
                        dve.wait_ge(*dps(b, m + 1))
                        cB.step(dve.tensor_reduce(mxs[:, m:m + 1], dash, AX.XY, ALU.max))
                        dve.wait_ge(*ssum(b, m + 1))
                        dve.wait_ge(*kv(b, 0))
                        dve.scalar_tensor_tensor(
                            Ek[:, j, s * T:(s + 1) * T].rearrange("p (h k) -> p h k", h=8),
                            inner(ssq[:, m, :], DH), -DIAG, dash, ALU.mult, ALU.add).then_inc(ush.sem, 1)

                    def step(a, b, n):
                        cA.begin(n)
                        cB.begin(b)
                        for slot in range(END):
                            k = slot - 1
                            if b is not None and slot == 0:
                                dve.wait_ge(*h2_high(b, 1))
                                dve.wait_ge(*up(b, 0))
                                dve.tensor_tensor(hT2l[:, :], hT2[:, :], hT2h[:, :].bitcast(F32), ALU.subtract)\
                                   .then_inc(h2_low.sem, 1)
                            if a is not None and k >= 0:
                                state_input(k, a)
                            if b is not None:
                                if slot in PRODS:
                                    weighted(PRODS[slot], b)
                                if slot == NORM3:
                                    dve.wait_ge(*x2_ok(b, 1))
                                    norm_stats(dve, L3, x2, b, passed)
                                    if n is not None:
                                        dve.wait_ge(*L1.turned(n, 1))
                                for m in KEYS.get(slot, ())[:0 if slot == KEYS_FROM else 1]:
                                    key_tile(m, b)
                            if n is not None and slot == NORM1:
                                dve.wait_ge(*x_in(n, 16))
                                norm_stats(dve, L1, xs, n, passed)
                                if b is not None:
                                    dve.wait_ge(*L2.turned(b, 1))
                            if a is not None and k >= 0:
                                scans(k, a)
                            if b is not None and slot == NORM3:
                                norm_apply(dve, L3, x2, b)
                            if a is not None and k >= 0:
                                weigh(k, a)
                            if n is not None and slot == NS:
                                split_mid(n)
                            if b is not None:
                                if slot == 1:
                                    gates(b)
                                if slot == min(PRODS):
                                    keep_biases(b)
                                for m in KEYS.get(slot, ())[0 if slot == KEYS_FROM else 1:]:
                                    key_tile(m, b)
                            if n is not None:
                                if slot == NORM1:
                                    norm_apply(dve, L1, xs, n)
                                if slot in CONV:
                                    convolve(CONV[slot], n)
                        if b is not None:
                            dve.wait_ge(*call(b, 0))
                            dve.tensor_reduce(bmx[:, :], mxs[:, :], AX.X, ALU.max).then_inc(bmx_ok.sem, 1)
                        if n is not None:
                            split_low(n)
                        if a is not None:
                            gated(a)
                        if n is not None:
                            positive(0, n)
                            positive(1, n)
                        if a is not None:
                            first_residual(a, b, n)
                            dve.wait_ge(*x1_ok(a, 1))
                            norm_stats(dve, L2, x1, a, passed)
                        if n is not None:
                            softplus(n)
                        if a is not None:
                            norm_apply(dve, L2, x1, a)

                    sweep(dve, step)

            end_part()

        sweep_two(nc, ctx, sem, sig, sbuf, banks, pair, ident, iota, wv, pq_dram, modc, ones, half, mxrun, nmx, two, pickd,
                  gate_rows, x2_dram, h3_dram, kv_dram, out_v)


def sweep_two(nc, ctx, sem, sig, sbuf, banks, pair, ident, iota, wv, pq_dram, modc, ones, half, mxrun, nmx, two, pickd,
              gate_rows, x2_dram, h3_dram, kv_dram, out_v):
    with ExitStack() as part:
        sb = sbuf(part)
        two_sb = sb("two_sb", [P, TWO_N])

        def V2(name):
            at, n = TWO[name]
            return two_sb[:, at:at + n]

        b1c, b2r, g1, be1, g2, be2, gatew = (V2(n) for n in ("b1", "b2", "g1", "be1", "g2", "be2", "gate"))
        wo = V2("wo").rearrange("p (r d) -> p r d", r=PR)
        w2 = V2("w2").rearrange("p (f d) -> p f d", f=FC)
        mw2 = V2("mw2").rearrange("p (r d) -> p r d", r=MC)
        high = sb("high", [P, SPLIT_N], F32R)
        low = sb("low", [P, SPLIT_N], F32R)
        pq = sb("pq_in", [P, HD])
        pq_high = sb("pq_high", [P, HD], F32R)
        pq_low = sb("pq_low", [P, HD], F32R)

        def halves(name, first, n):
            a = TWO[name][0] + first
            return high[:, a:a + n], low[:, a:a + n]

        s3w = V2("s3").rearrange("p (r d) -> p r d", r=SC)
        pick = sb("pick", [3 * 32, MC, P], BF16)
        h3 = sb("h3", [P, T])
        h3h = sb("h3h", [P, T], F32R)
        h3l = sb("h3l", [P, T], F32R)
        kvl = sb("kvl", [P, PR * VW + 1])
        sfac = sb("sfac", [P, 1])
        hsum = sb("hsum", [P, 1])
        hsB = sb("hsB", [P, P])
        evs = sb("evs", [P, HD])
        HW = DH + 1
        kvb = sb("kvb", [P, PR, 2 * HW])
        qsqb = sb("qsqb", [P, 2, T])
        qs = sb("qs", [P, 8])
        qm = sb("qm", [P, 8])
        nb = sb("nb", [P, 8])
        uq = sb("uq", [P, 2, T])
        qT = sb("qT", [P, 2, T])
        rd = sb("rd", [P, 8])
        at = sb("at", [P, 2, T])
        aT = sb("aT", [P, 2, T])
        o1T = sb("o1T", [P, T])
        o1h = sb("o1h", [P, T], F32R)
        o1l = sb("o1l", [P, T], F32R)
        x2 = sb("x2s", [P, J, D])
        gab = sb("gab", [P, 2, D])
        gg = sb("gg", [P, D])
        gbe = sb("gbe", [P, D])
        vb = sb("vb", [P, 2, T])
        ee = sb("ee", [P, 2, T])
        hE = sb("hE", [P, FC, T])
        t6 = sb("t6", [P, J, D])
        x3 = sb("x3", [P, J, D])
        hT4 = sb("hT4", [P, T])
        h4h = sb("h4h", [P, T], F32R)
        h4l = sb("h4l", [P, T], F32R)
        m8 = sb("m8b", [P, J, 8])
        idx = sb("idxb", [P, J, 8], U32)
        gd = sb("gd", [P, J])
        gex = sb("gex", [P, J])
        gsum = sb("gsum", [P, J])
        gw1 = sb("gw1", [P, J])
        gw2 = sb("gw2", [P, J])
        oh1 = sb("oh1", [P, J, E1])
        oh2 = sb("oh2", [P, J, E1])
        disp = sb("disp", [P, J, 3, 32])
        dT = sb("dT", [3 * 32, T], BF16)
        dR = sb("dR", [3 * 32, T])
        dRb = sb("dRb", [3 * 32, T], BF16)
        NX = MC + SC
        th = sb("th", [P, 2, T])
        sl = sb("sl", [P, 2, T])
        hm = sb("hm", [P, NX, T])
        fo = sb("fo", [P, J, D])
        ob = sb("ob", [P, J, D])

        w_in, init, nmx_ok, passed, w_high, w_low = (
            sem(n) for n in ("w2_in", "init2", "nmx_ok", "passed2", "w_high", "w_low"))
        h3_in, kv_in, x2_in, gab_in, res_out = (sig(n, 16) for n in ("h3_in", "kv_in", "x2_in", "gab_in", "res_out"))
        gab_in.per = 32
        L5, L6, L7 = (Norm(sb, sig, n, e) for n, e in (("n5", EPS_ENC), ("n6", EPS_ENC), ("n7", EPS_MOD)))
        M = 2 * J
        (sf, hsb, vsps, evs_ok, kvb_ok, qps, qd, qsq, qss, qu, qe, qt, qT_ok, num, rd_ok, at_ok, att, aT_ok,
         wo_ok, chainC) = (sig(n, p) for n, p in (
             ("sf", 1), ("hsb", 1), ("vsps", 2), ("evs_ok", 2), ("kvb_ok", 1), ("qps", M), ("qd", M), ("qsq", M),
             ("qss", M), ("qu", M), ("qe", M), ("qt", M), ("qT_ok", M), ("num", M), ("rd_ok", M), ("at_ok", M),
             ("att", M), ("aT_ok", M), ("wo_ok", M), ("chainC", 2 * M)))
        hsum_ok, h3_high, h3_low, o1_high, o1_low, h4_high, h4_low, d_mid, d_rem, d_remb, d_low = (
            sig(n, 1) for n in ("hsum_ok", "h3_high", "h3_low", "o1_high", "o1_low", "h4_high", "h4_low", "d_mid", "d_rem",
                                "d_remb", "d_low"))
        (w1ps, vb_ok, ee_ok, em_ok, he, w2ps, gg_ok, t6a, t6b, x3_ok, lg_ok, gidx, gd_ok, gex_ok, disp_ok, dtp, dT_ok,
         xps, yps, th_ok, sl_ok, hm_ok, mo, fin, ob_ok, chainD) = (sig(n, p) for n, p in (
             ("w1ps", FC), ("vb_ok", FC), ("ee_ok", FC), ("em_ok", FC), ("he", FC), ("w2ps", 1), ("gg_ok", 1), ("t6a", 1),
             ("t6b", 1), ("x3_ok", 1), ("lg_ok", 1), ("gidx", 1), ("gd_ok", 1), ("gex_ok", 1), ("disp_ok", 1),
             ("dtp", 1), ("dT_ok", 1), ("xps", NX), ("yps", NX), ("th_ok", NX), ("sl_ok", NX), ("hm_ok", NX),
             ("mo", 1), ("fin", 1), ("ob_ok", 1), ("chainD", 8)))

        ringC = [("vs0", evs_ok, 1), ("vs1", evs_ok, 2)]
        for t in range(M + 3):
            if t < M:
                ringC += [(f"q{t}", qsq, t + 1), (f"d{t}", qu, t + 1)]
            if 1 <= t <= M:
                ringC += [(f"t{t - 1}", qT_ok, t)]
            if t >= 3:
                ringC += [(f"a{t - 3}", aT_ok, t - 2)]
        ringD = [("turn5", L5.out, 1)] + [(f"w{f}", vb_ok, f + 1) for f in range(FC)]
        ringD += [("turn7", L7.out, 1), ("lg", gidx, 1)]
        for q in range(NX):
            if q == SC:
                ringD += [("dT", d_rem, 1)]
            ringD += [(f"x{q}", sl_ok, q + 1), (f"y{q}", hm_ok, q + 1)]

        def make_ring(uses, first, size):
            place = {name: n for n, (name, _, _) in enumerate(uses)}

            def bank(name):
                return banks[first + place[name] % size]

            def free(pe, name, b):
                n = place[name]
                if n >= size:
                    _, done, count = uses[n - size]
                    pe.wait_ge(*done(b, count))
                else:
                    back = max(k for k in range(len(uses)) if k % size == n % size)
                    _, done, _ = uses[back]
                    pe.wait_ge(*done(b, 0))
            return bank, free

        bankC, freeC = make_ring(ringC, 0, 2)
        bankD, freeD = make_ring(ringD, 5, 2)
        SLOTS = M + 4

        def at_slot(slot, lag):
            return slot - lag if 0 <= slot - lag < M else None

        XQ = {7: (0, 1), 8: (2, 3), 9: (4, 5), 10: (6, 7), 11: (8, 9)}
        DOWN = {8: (0, 1), 9: (2, 3), 10: (4, 5), 11: (6, 7)}
        NORM7, GATES, DISPATCH, HALVES = 6, 7, 8, 9
        WF = {1: (0, 1), 2: (2, 3)}
        WD = {2: (0, 1), 3: (2, 3)}

        def sweep(eng, step):
            step(None, None, 0)
            step(0, None, 1)
            step(1, 0, 2)
            with eng.Fori(2, NB - 1) as i:
                step(i, i - 1, i + 1)
            step(NB - 1, NB - 2, None)
            step(None, NB - 1, None)

        with nc.Block() as block:
            @block.sync
            def _(sp):
                sp.dma_start(two_sb[:, :], two).then_inc(w_in, 16)
                sp.dma_start(pick[:, :, :], pickd).then_inc(w_in, 16)
                sp.dma_start(pq[:, :], pq_dram).then_inc(w_in, 16)

                def load_keys(c):
                    sp.wait_ge(*qd(c, 0))
                    sp.dma_start(h3[:, :], h3_dram[c]).then_inc(h3_in.sem, 16)
                    sp.wait_ge(*kvb_ok(c, 0))
                    sp.dma_start(kvl[:, :], kv_dram[c]).then_inc(kv_in.sem, 16)

                def load_feed(d):
                    sp.wait_ge(*x3_ok(d, 0))
                    sp.dma_start(x2[:, :, :].rearrange("p j d -> p (j d)"), x2_dram[d]).then_inc(x2_in.sem, 16)
                    sp.wait_ge(*fin(d, 0))
                    for k in range(2):
                        sp.dma_start(gab[:, k, :], gate_rows[2 + k, d].partition_broadcast(P))\
                          .then_inc(gab_in.sem, 16)

                def store(d):
                    sp.wait_ge(*ob_ok(d, 1))
                    sp.dma_start(out_v[d], ob[:, :, :]).then_inc(res_out.sem, 16)

                load_keys(0)
                load_keys(1)
                load_feed(0)
                load_keys(2)
                store(0)
                with sp.Fori(2, NB - 1) as i:
                    load_feed(i - 1)
                    load_keys(i + 1)
                    store(i - 1)
                for d in (NB - 2, NB - 1):
                    load_feed(d)
                    store(d)
                sp.wait_ge(*res_out(NB, 0))

            @block.scalar
            def _(act):
                act.wait_ge(w_in, 48)
                for first in range(0, SPLIT_N, T):
                    act.activation(high[:, first:first + T], two_sb[:, first:first + T], ACT.Copy).then_inc(w_high, 1)
                for first in range(0, HD, T):
                    act.activation(pq_high[:, first:first + T], pq[:, first:first + T], ACT.Copy).then_inc(w_high, 1)
                act.wait_ge(nmx_ok, 1)

                def key_halves(c):
                    act.wait_ge(*h3_in(c, 16))
                    act.wait_ge(*qd(c, 0))
                    act.activation(h3h[:, :], h3[:, :], ACT.Copy).then_inc(h3_high.sem, 1)

                def square(m, c):
                    act.wait_ge(*qps(c, m + 1))
                    act.wait_ge(*qss(c, m - 1 if m >= 2 else 0))
                    act.activation(qsqb[:, m % 2, :], bankC(f"q{m}")[:, :], ACT.Square).then_inc(qsq.sem, 1)

                def feature(m, c):
                    act.wait_ge(*qu(c, m + 1))
                    act.activation(uq[:, m % 2, :], uq[:, m % 2, :], ACT.Exp).then_inc(qe.sem, 1)

                def keys(c):
                    act.wait_ge(*kv_in(c, 16))
                    act.wait_ge(*kvb_ok(c, 0))
                    act.activation(sfac[:, :], kvl[:, PR * VW:], ACT.Exp, bias=nmx[:, 0:1]).then_inc(sf.sem, 1)
                    for s in range(2):
                        act.wait_ge(*vsps(c, s + 1))
                        act.activation(evs[:, s * T:(s + 1) * T], bankC(f"vs{s}")[:, :], ACT.Copy,
                                       scale=EPS_FEAT).then_inc(evs_ok.sem, 1)

                def keep_features(m, c):
                    act.wait_ge(*qt(c, m + 1))
                    act.wait_ge(*num(c, m - 1 if m >= 2 else 0))
                    act.activation(qT[:, m % 2, :], bankC(f"t{m}")[:, :], ACT.Copy, bias=EPS_FEAT)\
                       .then_inc(qT_ok.sem, 1)

                def keep_quotient(m, c):
                    act.wait_ge(*att(c, m + 1))
                    act.wait_ge(*wo_ok(c, m - 1 if m >= 2 else 0))
                    act.activation(aT[:, m % 2, :], bankC(f"a{m}")[:, :], ACT.Copy).then_inc(aT_ok.sem, 1)

                def first_norm(d):
                    act.wait_ge(*L5.turned(d, 1))
                    act.wait_ge(*w2ps(d, 0))
                    act.activation(o1T[:, :], bankD("turn5")[:, :], ACT.Identity, scale=g1, bias=be1)\
                       .then_inc(L5.out.sem, 1)
                    act.wait_ge(*L5.out(d, 1))
                    act.activation(o1h[:, :], o1T[:, :], ACT.Copy).then_inc(o1_high.sem, 1)

                def elu(f, d):
                    act.wait_ge(*w1ps(d, f + 1))
                    act.wait_ge(*he(d, f - 1 if f >= 2 else 0))
                    act.activation(vb[:, f % 2, :], bankD(f"w{f}")[:, :], ACT.Identity,
                                   bias=b1c[:, f:f + 1]).then_inc(vb_ok.sem, 1)
                    act.wait_ge(*em_ok(d, f + 1))
                    act.activation(ee[:, f % 2, :], ee[:, f % 2, :], ACT.Exp).then_inc(ee_ok.sem, 1)

                def modulate(d):
                    act.wait_ge(*L7.turned(d, 1))
                    act.wait_ge(*xps(d, 0))
                    act.wait_ge(*yps(d, 0))
                    act.activation(hT4[:, :], bankD("turn7")[:, :], ACT.Identity, scale=modc[:, 1, d, 3:4],
                                   bias=modc[:, 1, d, 2:3]).then_inc(L7.out.sem, 1)
                    act.wait_ge(*L7.out(d, 1))
                    act.activation(h4h[:, :], hT4[:, :], ACT.Copy).then_inc(h4_high.sem, 1)

                def gates(d):
                    act.wait_ge(*gd_ok(d, 1))
                    act.activation(gex[:, :], gd[:, :], ACT.Exp).then_inc(gex_ok.sem, 1)

                def keep_dispatch(d):
                    act.wait_ge(*dtp(d, 1))
                    act.wait_ge(*yps(d, 0))
                    act.activation(dT[:, :], bankD("dT")[0:96, :], ACT.Copy).then_inc(dT_ok.sem, 1)
                    act.wait_ge(*d_rem(d, 1))
                    act.activation(dRb[64:96, :], dR[64:96, :], ACT.Copy).then_inc(d_remb.sem, 1)

                def tanh(q, d):
                    act.wait_ge(*xps(d, q + 1))
                    act.wait_ge(*sl_ok(d, q - 1 if q >= 2 else 0))
                    act.activation(th[:, q % 2, :], bankD(f"x{q}")[:, :], ACT.Tanh, scale=0.5)\
                       .then_inc(th_ok.sem, 1)

                def step(c, d, n):
                    for slot in range(SLOTS):
                        chunks = XQ.get(slot, ()) if d is not None else ()
                        if c is not None and slot < M:
                            square(slot, c)
                        if d is not None and slot == 0:
                            first_norm(d)
                        for q in chunks[:1]:
                            tanh(q, d)
                        if c is not None and slot < M:
                            feature(slot, c)
                        if d is not None and slot == GATES:
                            gates(d)
                        if d is not None and slot == DISPATCH:
                            keep_dispatch(d)
                        if c is not None and at_slot(slot, 1) is not None:
                            keep_features(at_slot(slot, 1), c)
                        if d is not None:
                            for f in WF.get(slot, ()):
                                elu(f, d)
                            if slot == NORM7:
                                modulate(d)
                        for q in chunks[1:]:
                            tanh(q, d)
                        if c is not None and at_slot(slot, 3) is not None:
                            keep_quotient(at_slot(slot, 3), c)
                        if n is not None and slot == HALVES:
                            key_halves(n)
                    if n is not None:
                        keys(n)

                sweep(act, step)

            @block.gpsimd
            def _(pool):
                pool.memset(kvb[:, :, :], 0.0).then_inc(init, 1)
                pool.memset(disp[:, :, :, :], 0.0).then_inc(init, 1)
                pool.tensor_scalar(nmx[:, :], mxrun[:, :], -1.0, None, ALU.mult).then_inc(nmx_ok, 1)
                pool.wait_ge(w_in, 48)

                def step(c, d, n):
                    if d is not None:
                        pool.wait_ge(*gab_in(d, 32))
                        pool.wait_ge(*x3_ok(d, 0))
                        pool.tensor_tensor(gg[:, :], g2, gab[:, 0, :], ALU.mult)
                        pool.tensor_tensor(gbe[:, :], be2, gab[:, 0, :], ALU.mult).then_inc(gg_ok.sem, 1)
                        pool.wait_ge(*gg_ok(d, 1))
                        pool.wait_ge(*x2_in(d, 16))
                        pool.tensor_tensor(x2[:, :, :], x2[:, :, :], mid(gbe[:, :], J), ALU.add).then_inc(t6b.sem, 1)
                        norm_pool(pool, L6, half, d, passed)
                        pool.wait_ge(*L6.xhat(d, 1))
                        pool.tensor_tensor(t6[:, :, :], L6.xh[:, :, :], mid(gg[:, :], J), ALU.mult).then_inc(t6a.sem, 1)
                        pool.wait_ge(*t6a(d, 1))
                        pool.wait_ge(*t6b(d, 1))
                        pool.wait_ge(*ob_ok(d, 0))
                        pool.wait_ge(*L7.xhat(d, 0))
                        pool.tensor_tensor(x3[:, :, :], x2[:, :, :], t6[:, :, :], ALU.add).then_inc(x3_ok.sem, 1)
                        norm_pool(pool, L7, half, d, passed)
                    if c is not None:
                        norm_pool(pool, L5, half, c, passed)
                    if d is not None:
                        pool.wait_ge(*fin(d, 1))
                        pool.wait_ge(*res_out(d, 0))
                        pool.tensor_tensor(ob[:, :, :], x3[:, :, :], fo[:, :, :], ALU.add).then_inc(ob_ok.sem, 1)

                sweep(pool, step)

            @block.tensor
            def _(pe):
                pe.wait_ge(w_in, 48)
                pe.wait_ge(w_low, (SPLIT_N + HD) // T)

                def query(m, c, name):
                    j, s = divmod(m, 2)
                    done = qps if name == "q" else qd
                    if name == "q":
                        w = halves("wq", s * T, T)
                    else:
                        w = pq_high[:, s * T:(s + 1) * T], pq_low[:, s * T:(s + 1) * T]
                    if m == 0:
                        pe.wait_ge(*h3_low(c, 1))
                    freeC(pe, f"{name}{m}", c)
                    split_product(pe, bankC(f"{name}{m}"), (h3h[:, j * P:(j + 1) * P], h3l[:, j * P:(j + 1) * P]),
                                  w).then_inc(done.sem, 1)

                def value_sums(c):
                    pe.wait_ge(*hsb(c, 1))
                    for s in range(2):
                        freeC(pe, f"vs{s}", c)
                        pe.matmul(bankC(f"vs{s}")[:, :], hsB[:, :], wv[:, s * T:(s + 1) * T],
                                  start=True, stop=True).then_inc(vsps.sem, 1)

                def residual(c):
                    pe.wait_ge(*L5.xhat(c, 0))
                    for j in range(J):
                        pe.matmul(banks[4][:, j * D:(j + 1) * D], h3[:, j * P:(j + 1) * P], ident,
                                  start=(j == 0), stop=False, skip_group_check=True)

                def turn_features(m, c):
                    freeC(pe, f"t{m}", c)
                    pe.wait_ge(*qe(c, m + 1))
                    for k in range(4):
                        last = pe.transpose(bankC(f"t{m}")[:, k * P:(k + 1) * P],
                                            uq[:, m % 2, k * P:(k + 1) * P], ident)
                    last.then_inc(qt.sem, 1)

                def numerators(m, c):
                    s = m % 2
                    pe.wait_ge(*qT_ok(c, m + 1))
                    pe.wait_ge(*kvb_ok(c, 1))
                    pe.wait_ge(*at_ok(c, m))
                    for k in range(4):
                        at_k = (k % 2) * 2 * HW
                        last = pe.matmul(pair[:, k // 2, at_k:at_k + 2 * HW], qT[:, m % 2, k * P:(k + 1) * P],
                                         kvb[:, 4 * s + k, :], start=True, stop=True)
                    last.then_inc(num.sem, 1)

                def turn_quotient(m, c):
                    freeC(pe, f"a{m}", c)
                    pe.wait_ge(*at_ok(c, m + 1))
                    for k in range(4):
                        last = pe.transpose(bankC(f"a{m}")[:, k * P:(k + 1) * P],
                                            at[:, m % 2, k * P:(k + 1) * P], ident)
                    last.then_inc(att.sem, 1)

                def output(m, c):
                    j, s = divmod(m, 2)
                    pe.wait_ge(*aT_ok(c, m + 1))
                    for k in range(4):
                        last = pe.matmul(banks[4][:, j * D:(j + 1) * D], aT[:, m % 2, k * P:(k + 1) * P],
                                         wo[:, 4 * s + k, :], start=False, stop=(s == 1 and k == 3),
                                         skip_group_check=True)
                    last.then_inc(wo_ok.sem, 1)

                def feed_first(f, d):
                    if f == 0:
                        pe.wait_ge(*o1_low(d, 1))
                    freeD(pe, f"w{f}", d)
                    split_product(pe, bankD(f"w{f}"), halves("w1", f * P, P), (o1h[:, :], o1l[:, :]))\
                        .then_inc(w1ps.sem, 1)

                def feed_second(f, d):
                    if f == 0:
                        pe.wait_ge(*fin(d, 0))
                        pe.matmul(banks[7][:, :], ones[0:1, :], b2r[0:1, :], start=True, stop=False,
                                  skip_group_check=True)
                        for j in range(J):
                            pe.matmul(banks[7][:, j * D:(j + 1) * D], o1T[:, j * P:(j + 1) * P], ident,
                                      start=False, stop=False, skip_group_check=True)
                    pe.wait_ge(*he(d, f + 1))
                    for j in range(J):
                        last = pe.matmul(banks[7][:, j * D:(j + 1) * D], hE[:, f, j * P:(j + 1) * P],
                                         w2[:, f, :], start=False, stop=(f == FC - 1), skip_group_check=True)
                    if f == FC - 1:
                        last.then_inc(w2ps.sem, 1)

                def logits(d):
                    freeD(pe, "lg", d)
                    pe.wait_ge(*L7.out(d, 1))
                    for j in range(J):
                        last = pe.matmul(bankD("lg")[:, j * E1:(j + 1) * E1], hT4[:, j * P:(j + 1) * P], gatew,
                                         start=True, stop=True)
                    last.then_inc(lg_ok.sem, 1)

                def turn_dispatch(d):
                    freeD(pe, "dT", d)
                    pe.wait_ge(*disp_ok(d, 1))
                    for j in range(J):
                        last = pe.transpose(bankD("dT")[0:96, j * P:(j + 1) * P],
                                            disp[:, j, :, :].rearrange("p k e -> p (k e)"), ident)
                    last.then_inc(dtp.sem, 1)

                def hidden(q, d):
                    w = halves("s1", q * P, P) if q < SC else halves("mw1", (q - SC) * P, P)
                    if q == 0:
                        pe.wait_ge(*h4_low(d, 1))
                    freeD(pe, f"x{q}", d)
                    split_product(pe, bankD(f"x{q}"), w, (h4h[:, :], h4l[:, :])).then_inc(xps.sem, 1)

                def factor(q, d):
                    freeD(pe, f"y{q}", d)
                    if q < SC:
                        last = split_product(pe, bankD(f"y{q}"), halves("s2", q * P, P), (h4h[:, :], h4l[:, :]))
                    else:
                        pe.wait_ge(*d_mid(d, 1))
                        pe.wait_ge(*d_low(d, 1))
                        last = pe.matmul(bankD(f"y{q}"), pick[:, q - SC, :], dT[:, :], start=True, stop=True)
                    last.then_inc(yps.sem, 1)

                def down(q, d):
                    w = s3w[:, q, :] if q < SC else mw2[:, q - SC, :]
                    if q == 0:
                        pe.wait_ge(*L6.xhat(d, 1))
                    pe.wait_ge(*hm_ok(d, q + 1))
                    for j in range(J):
                        last = pe.matmul(banks[7][:, j * D:(j + 1) * D], hm[:, q, j * P:(j + 1) * P], w,
                                         start=(q == 0 and j == 0), stop=(q == NX - 1), skip_group_check=True)
                    if q == NX - 1:
                        last.then_inc(mo.sem, 1)

                def step(c, d, n):
                    for slot in range(SLOTS):
                        chunks = XQ.get(slot, ()) if d is not None else ()
                        if c is not None and slot < M:
                            query(slot, c, "q")
                        if d is not None and slot == 0:
                            freeD(pe, "turn5", d)
                            norm_pe(pe, L5, bankD("turn5"), ident, d)
                        for q in chunks[:1]:
                            hidden(q, d)
                        if c is not None and slot >= M:
                            output(at_slot(slot, 4), c)
                        if c is not None and slot < M:
                            query(slot, c, "d")
                        if c is not None and slot == 3:
                            residual(c)
                        if c is not None and 4 <= slot < M:
                            output(at_slot(slot, 4), c)
                        if d is not None:
                            for f in WF.get(slot, ()):
                                feed_first(f, d)
                            for q in DOWN.get(slot, ()):
                                down(q, d)
                        if c is not None and at_slot(slot, 1) is not None:
                            turn_features(at_slot(slot, 1), c)
                        if d is not None and slot == NORM7:
                            freeD(pe, "turn7", d)
                            norm_pe(pe, L7, bankD("turn7"), ident, d)
                        for q in chunks[:1]:
                            factor(q, d)
                        for q in chunks[1:]:
                            hidden(q, d)
                        if c is not None and at_slot(slot, 2) is not None:
                            numerators(at_slot(slot, 2), c)
                        for q in chunks[1:]:
                            factor(q, d)
                        if d is not None:
                            for f in WD.get(slot, ()):
                                feed_second(f, d)
                        if c is not None and at_slot(slot, 3) is not None:
                            turn_quotient(at_slot(slot, 3), c)
                        if d is not None:
                            if slot == NORM7:
                                logits(d)
                            if slot == DISPATCH - 1:
                                turn_dispatch(d)
                    if n is not None:
                        value_sums(n)
                    if d is not None:
                        down(NX - 2, d)
                        down(NX - 1, d)

                sweep(pe, step)

            @block.vector
            def _(dve):
                dve.wait_ge(w_in, 48)
                for n, first in enumerate(range(0, SPLIT_N, T)):
                    dve.wait_ge(w_high, n + 1)
                    dve.tensor_tensor(low[:, first:first + T], two_sb[:, first:first + T], high[:, first:first + T].bitcast(F32), ALU.subtract)\
                       .then_inc(w_low, 1)
                for n, first in enumerate(range(0, HD, T)):
                    dve.wait_ge(w_high, SPLIT_N // T + n + 1)
                    dve.tensor_tensor(pq_low[:, first:first + T], pq[:, first:first + T], pq_high[:, first:first + T].bitcast(F32), ALU.subtract)\
                       .then_inc(w_low, 1)
                dve.wait_ge(init, 2)
                cC, cD = Chain(dve, chainC), Chain(dve, chainD)
                attn = banks[4][:, :].rearrange("p (j d) -> p j d", j=J)
                ffn = banks[7][:, :].rearrange("p (j d) -> p j d", j=J)

                def low_half(low_part, x, high_half, high_ok, low_ok, it):
                    dve.wait_ge(*high_ok(it, 1))
                    dve.tensor_tensor(low_part[:, :], x[:, :], high_half[:, :].bitcast(F32), ALU.subtract)\
                       .then_inc(low_ok.sem, 1)

                def sum_keys(c):
                    dve.wait_ge(*h3_in(c, 16))
                    dve.wait_ge(*hsb(c, 0))
                    dve.tensor_reduce(hsum[:, :], h3[:, :], AX.X, ALU.add).then_inc(hsum_ok.sem, 1)
                    dve.wait_ge(*hsum_ok(c, 1))
                    dve.wait_ge(*vsps(c, 0))
                    dve.tensor_scalar(hsB[:, :], ones[:, :], hsum[:, 0:1], None, ALU.mult).then_inc(hsb.sem, 1)

                def exponent(m, c):
                    dash = bankC(f"d{m}")[:, :].rearrange("p (h k) -> p h k", h=8)
                    dve.wait_ge(*qsq(c, m + 1))
                    dve.wait_ge(*qu(c, m))
                    dve.tensor_reduce(qs[:, :], qsqb[:, m % 2, :].rearrange("p (h k) -> p h k", h=8),
                                      AX.X, ALU.add).then_inc(qss.sem, 1)
                    dve.wait_ge(*qd(c, m + 1))
                    cC.step(dve.tensor_reduce(qm[:, :], dash, AX.X, ALU.max))
                    cC.step(dve.scalar_tensor_tensor(nb[:, :], qs[:, :], -DIAG, qm[:, :], ALU.mult, ALU.subtract))
                    dve.wait_ge(*qt(c, m - 1 if m >= 2 else 0))
                    dve.tensor_tensor(uq[:, m % 2, :].rearrange("p (h k) -> p h k", h=8), dash,
                                      inner(nb[:, :], DH), ALU.add).then_inc(qu.sem, 1)

                def keys(c):
                    dve.wait_ge(*sf(c, 1))
                    dve.wait_ge(*evs_ok(c, 2))
                    dve.wait_ge(*num(c, 0))
                    kvw = kvl[:, 0:PR * VW].rearrange("p (r v) -> p r v", r=PR)
                    ev = evs[:, :].rearrange("p (r v) -> p r v", r=PR)
                    for k in range(2):
                        r = slice(k * DH, (k + 1) * DH)
                        dve.scalar_tensor_tensor(kvb[r, :, k * HW:k * HW + DH], kvw[r, :, r], sfac[r, 0:1], ev[r, :, r],
                                                 ALU.mult, ALU.add)
                        last = dve.tensor_scalar(kvb[r, :, k * HW + DH:(k + 1) * HW], kvw[r, :, P:VW], sfac[r, 0:1],
                                                 T * EPS_FEAT, ALU.mult, ALU.add)
                    last.then_inc(kvb_ok.sem, 1)

                def quotient(m, c):
                    dve.wait_ge(*num(c, m + 1))
                    dve.wait_ge(*at_ok(c, m))
                    heads = pair[:, :, 0:4 * HW].rearrange("p b (h k) -> p b h k", h=4)
                    rds = rd[:, :].rearrange("p (b h) -> p b h", b=2)
                    dve.reciprocal(rds, heads[:, :, :, DH]).then_inc(rd_ok.sem, 1)
                    dve.wait_ge(*rd_ok(c, m + 1))
                    dve.wait_ge(*att(c, m - 1 if m >= 2 else 0))
                    dve.tensor_tensor(at[:, m % 2, :].rearrange("p (b h k) -> p b h k", b=2, h=4),
                                      heads[:, :, :, 0:DH], rds.unsqueeze(3).to_broadcast([P, 2, 4, DH]),
                                      ALU.mult).then_inc(at_ok.sem, 1)

                def elu(f, d):
                    if f == 0:
                        dve.wait_ge(*w2ps(d, 0))
                    dve.wait_ge(*vb_ok(d, f + 1))
                    dve.wait_ge(*he(d, f - 1 if f >= 2 else 0))
                    dve.tensor_scalar(ee[:, f % 2, :], vb[:, f % 2, :], 0.0, None, ALU.min).then_inc(em_ok.sem, 1)
                    dve.wait_ge(*ee_ok(d, f + 1))
                    dve.scalar_tensor_tensor(hE[:, f, :], ee[:, f % 2, :], -1.0, vb[:, f % 2, :],
                                             ALU.add, ALU.max).then_inc(he.sem, 1)

                def gates(d):
                    lg = bankD("lg")[:, 0:J * E1].rearrange("p (j e) -> p j e", j=J)
                    dve.wait_ge(*lg_ok(d, 1))
                    hold(dve, passed)
                    for j in range(J):
                        last = dve.max(m8[:, j, :], lg[:, j, :])
                    cD.step(last)
                    hold(dve, passed)
                    for j in range(J):
                        last = dve.max_index(idx[:, j, :], m8[:, j, :], lg[:, j, :])
                    last.then_inc(gidx.sem, 1)
                    dve.wait_ge(*gidx(d, 1))
                    dve.wait_ge(*gex_ok(d, 0))
                    dve.tensor_tensor(gd[:, :], m8[:, :, 1], m8[:, :, 0], ALU.subtract).then_inc(gd_ok.sem, 1)
                    for k, oh in enumerate((oh1, oh2)):
                        cD.step(dve.tensor_tensor(oh[:, :, :], mid(iota[:, 0:E1], J),
                                                  idx[:, :, k:k + 1].to_broadcast([P, J, E1]), ALU.is_equal))
                    dve.wait_ge(*gex_ok(d, 1))
                    cD.step(dve.tensor_scalar(gsum[:, :], gex[:, :], 1.0, None, ALU.add))
                    cD.step(dve.reciprocal(gw1[:, :], gsum[:, :]))
                    cD.step(dve.tensor_tensor(gw2[:, :], gex[:, :], gw1[:, :], ALU.mult))
                    cD.step(dve.tensor_tensor(oh1[:, :, :], oh1[:, :, :], inner(gw1[:, :], E1), ALU.mult))
                    cD.step(dve.tensor_tensor(oh2[:, :, :], oh2[:, :, :], inner(gw2[:, :], E1), ALU.mult))
                    dve.wait_ge(*dtp(d, 0))
                    dve.tensor_tensor(disp[:, :, :, 0:E1], oh1[:, :, :].unsqueeze(2).to_broadcast([P, J, 3, E1]),
                                      oh2[:, :, :].unsqueeze(2).to_broadcast([P, J, 3, E1]), ALU.add)\
                       .then_inc(disp_ok.sem, 1)

                def split_dispatch(d):
                    w = bankD("dT")
                    dve.wait_ge(*dT_ok(d, 1))
                    dve.tensor_tensor(dT[32:64, :], w[32:64, :], dT[32:64, :], ALU.subtract).then_inc(d_mid.sem, 1)
                    dve.wait_ge(*d_low(d, 0))
                    dve.tensor_tensor(dR[64:96, :], w[64:96, :], dT[64:96, :], ALU.subtract).then_inc(d_rem.sem, 1)
                    dve.wait_ge(*d_remb(d, 1))
                    dve.tensor_tensor(dT[64:96, :], dR[64:96, :], dRb[64:96, :], ALU.subtract).then_inc(d_low.sem, 1)

                def silu(q, d):
                    dve.wait_ge(*th_ok(d, q + 1))
                    dve.wait_ge(*hm_ok(d, q - 1 if q >= 2 else 0))
                    dve.scalar_tensor_tensor(sl[:, q % 2, :], th[:, q % 2, :], 1.0, bankD(f"x{q}")[:, :],
                                             ALU.add, ALU.mult).then_inc(sl_ok.sem, 1)
                    dve.wait_ge(*sl_ok(d, q + 1))
                    dve.wait_ge(*yps(d, q + 1))
                    if q == 0:
                        dve.wait_ge(*mo(d, 0))
                    dve.scalar_tensor_tensor(hm[:, q, :], sl[:, q % 2, :], 0.5, bankD(f"y{q}")[:, :],
                                             ALU.mult, ALU.mult).then_inc(hm_ok.sem, 1)

                def step(c, d, n):
                    cC.begin(c)
                    cD.begin(d)
                    for slot in range(SLOTS):
                        chunks = XQ.get(slot, ()) if d is not None else ()
                        if c is not None and slot < M:
                            exponent(slot, c)
                        if d is not None and slot == 0:
                            dve.wait_ge(*w1ps(d, 0))
                            low_half(o1l, o1T, o1h, o1_high, o1_low, d)
                        if c is not None and slot == SLOTS - 1:
                            dve.wait_ge(*wo_ok(c, M))
                            dve.wait_ge(*L5.turned(c, 0))
                            norm_stats(dve, L5, attn, c, passed)
                        if d is not None and slot == GATES:
                            gates(d)
                        if d is not None and slot == DISPATCH:
                            split_dispatch(d)
                        for q in chunks[:1]:
                            silu(q, d)
                        if c is not None and slot == SLOTS - 1:
                            norm_apply(dve, L5, attn, c)
                        if d is not None:
                            for f in WF.get(slot, ()):
                                elu(f, d)
                            if slot == 4:
                                dve.wait_ge(*w2ps(d, 1))
                                dve.wait_ge(*t6a(d, 0))
                                norm_stats(dve, L6, ffn, d, passed)
                        if c is not None and at_slot(slot, 2) is not None:
                            quotient(at_slot(slot, 2), c)
                        for q in chunks[1:]:
                            silu(q, d)
                        if d is not None:
                            if slot == 4:
                                norm_apply(dve, L6, ffn, d)
                            if slot == 5:
                                dve.wait_ge(*x3_ok(d, 1))
                                dve.wait_ge(*L7.turned(d, 0))
                                norm_dve(dve, L7, x3, d, passed)
                            if slot == NORM7:
                                dve.wait_ge(*yps(d, 0))
                                low_half(h4l, hT4, h4h, h4_high, h4_low, d)
                        if n is not None and slot == HALVES:
                            dve.wait_ge(*qd(n, 0))
                            low_half(h3l, h3, h3h, h3_high, h3_low, n)
                            sum_keys(n)
                    if d is not None:
                        dve.wait_ge(*mo(d, 1))
                        dve.wait_ge(*ob_ok(d, 0))
                        dve.tensor_tensor(fo[:, :, :], ffn, mid(gab[:, 1, :], J), ALU.mult).then_inc(fin.sem, 1)
                    if n is not None:
                        keys(n)

                sweep(dve, step)


def kernel(**inputs):
    import ml_dtypes
    import numpy as np
    import concourse.bacc as _bacc
    from concourse.bass_utils import run_bass_kernel_spmd as _run

    A = {k: np.asarray(v) for k, v in inputs.items()}

    def pack(where, width, parts):
        w = np.zeros((P, width), np.float32)
        for name, (first, n) in where.items():
            a = parts[name]
            r, a = a if isinstance(a, tuple) else (0, a)
            a = a.reshape(a.shape[0], -1)
            w[r:r + a.shape[0], first:first + a.shape[1]] = a
        return w

    def chunks(a, n):
        return a.reshape(n, P, -1).transpose(1, 0, 2)

    def blocks(a, n):
        w = np.zeros((n * a.shape[0], n * a.shape[1]), np.float32)
        for k in range(n):
            w[k * a.shape[0]:(k + 1) * a.shape[0], k * a.shape[1]:(k + 1) * a.shape[1]] = a
        return w

    ident = np.eye(P, dtype=np.float32)
    iota = np.tile(np.arange(E1, dtype=np.float32), (P, 1))
    keep = pack(KEEP, KEEP_N, {"ident": ident, "iota": iota, "wv": A["L1_attn_Wv"]})

    once = pack(ONCE, ONCE_N, {
        "wmod0": A["L0_wmod"], "wmod1": A["L1_wmod"], "c0": A["L0_c"].T, "c1": A["L1_c"].T,
        "wkT": chunks(A["L1_attn_Wk"].reshape(D, HD).T, PR), "wqT": chunks(A["L1_attn_Wq"].reshape(D, HD).T, PR),
        "proj": blocks(A["L1_attn_proj"].T, 2)})

    xp = A["L0_attn_x_proj_w"]
    xw = np.zeros((DI, P), np.float32)
    for k in range(3):
        xw[:, 32 * k:32 * k + 32] = xp[:, RK:]
    xw[:, 96:96 + RK] = xp[:, :RK]
    b2 = np.zeros((P, J, D), np.float32)
    for j in range(J):
        b2[32 * j:32 * j + E0, j, :] = A["L0_ffn_b2"]
    one = pack(ONE, ONE_N, {
        "inw": A["L0_attn_in_proj_w"],
        "convw": chunks(A["L0_attn_conv_w"][:, 0, :].T, G), "convb": chunks(A["L0_attn_conv_b"], G),
        "xw": chunks(xw, G), "dtw": (96, A["L0_attn_dt_proj_w"]), "dtb": chunks(A["L0_attn_dt_proj_b"], G),
        "alog": chunks(A["L0_attn_A_log"], G), "dskip": chunks(A["L0_attn_D"], G),
        "outw": chunks(A["L0_attn_out_proj_w"], G), "gate": A["L0_ffn_gate_w"].T,
        "b1": A["L0_ffn_b1"].reshape(E0 * FC, P).T,
        "w2": A["L0_ffn_w2"].reshape(E0, FC, P, D).transpose(2, 0, 1, 3), "b2": b2, "wk": A["L1_attn_Wk"]})

    pickd = np.zeros((3, 32, MC, P), ml_dtypes.bfloat16)
    for r in range(MC):
        for k in range(2):
            pickd[:, 2 * r + k, r, k * HE:(k + 1) * HE] = 1.0
    mw2 = A["L1_ffn_w2"].transpose(0, 2, 1).reshape(E1 * HE, D)
    two = pack(TWO, TWO_N, {
        "wq": A["L1_attn_Wq"], "wo": chunks(A["L1_attn_Wo"].reshape(HD, D), PR), "w1": A["L1_attn_W1"],
        "b1": A["L1_attn_b1"].reshape(FC, P).T, "w2": chunks(A["L1_attn_W2"], FC),
        "b2": np.tile(A["L1_attn_b2"], J)[None], "g1": A["L1_attn_ln1_g"][:, None],
        "be1": A["L1_attn_ln1_b"][:, None], "g2": np.tile(A["L1_attn_ln2_g"], (P, 1)),
        "be2": np.tile(A["L1_attn_ln2_b"], (P, 1)), "gate": A["L1_ffn_gate_w"].T,
        "mw1": A["L1_ffn_w1"].reshape(E1 * HE, D).T, "mw2": chunks(mw2, MC),
        "s1": A["L1_ffn_sfc1"].T, "s2": A["L1_ffn_sfc2"].T, "s3": chunks(A["L1_ffn_sfc3"].T, SC)})

    pick16 = np.zeros((3 * 2 * NS, 2 * NS), ml_dtypes.bfloat16)
    for n in range(2 * NS):
        pick16[n::2 * NS, n] = 1.0

    arrays = {"x": np.ascontiguousarray(A["L0_attn_x"]), "keep": keep, "once": once, "one": one,
              "up1": np.ascontiguousarray(A["L0_ffn_w1"].transpose(1, 0, 2)).reshape(D, E0 * FF), "two": two,
              "pick16": pick16, "pickd": pickd.reshape(3 * 32, MC, P)}
    nc = _bacc.Bacc("TRN2", target_bir_lowering=False, num_devices=1)
    args = [nc.dram_tensor(f"in_{n}", a.shape, mybir.dt.from_np(a.dtype), kind="ExternalInput").ap()
            for n, a in arrays.items()]
    out = nc.dram_tensor("out_0", (NB, T, D), F32, kind="ExternalOutput").ap()
    adaln_depth2(nc, *args, out)
    r = _run(nc, [{f"in_{n}": a for n, a in arrays.items()}], core_ids=[0])
    return r.results[0]["out_0"]
```
